# Optimizing a Trainium2 kernel written in Bass

```python
import numpy as np
import jax
import jax.numpy as jnp

def _softmax(x, axis=-1):
    return jax.nn.softmax(x, axis=axis)

def _gelu(x):
    return jax.nn.gelu(x, approximate=True)

def _silu(x):
    return jax.nn.silu(x)

def _sigmoid(x):
    return jax.nn.sigmoid(x)

def _layernorm(x, axis=-1, eps=1e-05):
    m = jnp.mean(x, axis=axis, keepdims=True)
    v = jnp.var(x, axis=axis, keepdims=True)
    return (x - m) / jnp.sqrt(v + eps)

def _scatter_add(tgt, idx, src, axis=0):
    return tgt.at[idx].add(src)

def _segment_sum(src, seg, n):
    return jax.ops.segment_sum(src, seg, n)
kernel_name = 'mk_flamingo_gated_d4_seqx_r8_9c7b60'

def setup_inputs(seed: int=0):
    np.random.seed(seed)
    _w = jnp.asarray

    def _rec_inputs():
        import jax
        import jax.numpy as jnp
        _rk = jax.random.key(seed)
        x = -0.0002928 + 1 * jax.random.normal(jax.random.fold_in(_rk, 1), (4, 512, 128), jnp.float32)
        _lenS = 512 - jax.random.randint(jax.random.fold_in(_rk, 7), (4,), 0, max(1, 512 // 4) + 1, jnp.int32)
        _lenS2 = 77 - jax.random.randint(jax.random.fold_in(_rk, 8), (4,), 0, max(1, 77 // 4) + 1, jnp.int32)
        _ctx_1024P = jax.random.normal(jax.random.fold_in(_rk, 11), (4, 16, 128), jnp.float32)
        _ctx_1024c = jax.random.dirichlet(jax.random.fold_in(_rk, 511), 0.3 * jnp.ones((16,), jnp.float32), (4, 77))
        _ctx_1024t = jnp.einsum('bsk,bkd->bsd', _ctx_1024c, _ctx_1024P)
        _ctx_1024t = _ctx_1024t * jax.lax.rsqrt(jnp.mean(jnp.square(_ctx_1024t)) + 1e-12) * 0.953939
        ctx_1024 = -1.39393e-06 + 0.999914 * (_ctx_1024t + 0.3 * jax.random.normal(jax.random.fold_in(_rk, 611), (4, 77, 128), jnp.float32))
        _validS = jnp.arange(512)[None, :] < _lenS[:, None]
        _validS2 = jnp.arange(77)[None, :] < _lenS2[:, None]
        _causal = jnp.tril(jnp.ones((512, 512), dtype=bool))
        mask_BxS2_ik0 = jnp.where(jnp.broadcast_to(_validS2[:, :], (4, 77)), 0, 1).astype(jnp.int32)
        _g = jax.random.normal(jax.random.fold_in(_rk, 9001), (2, 4), jnp.float32)
        _g = jnp.sign(_g) * jnp.maximum(jnp.abs(_g), 1.0) + (_g == 0) * 1.0
        g_xattn = _g[0]
        g_ffn = _g[1]
        return (x, ctx_1024, mask_BxS2_ik0, g_xattn, g_ffn)
    x, ctx_1024, mask_BxS2_ik0, g_xattn, g_ffn = _rec_inputs()

    def _L0_xattn_setup():
        import jax, jax.numpy as jnp
        import numpy as np
        EPS = 1e-05

        def layer_norm(x, gamma):
            mu = jnp.mean(x, axis=-1, keepdims=True)
            var = jnp.mean(jnp.square(x - mu), axis=-1, keepdims=True)
            return (x - mu) / jnp.sqrt(var + EPS) * gamma
        key = jax.random.key(seed)
        ks = jax.random.split(key, 10)
        b, n, j = (2, 256, 256)
        dim, ctx_dim, heads, dim_head, ff_mult = (128, 128, 16, 64, 4)
        inner = heads * dim_head
        ff_inner = ff_mult * dim
        s = 0.02
        return {'x': jax.random.normal(ks[0], (b, n, dim), jnp.float32), 'context': jax.random.normal(ks[1], (b, j, ctx_dim), jnp.float32), 'mask': jax.random.randint(ks[2], (b, j), 0, 2, jnp.int32), 'gamma': jnp.ones((dim,), jnp.float32), 'ctx_gamma': jnp.ones((ctx_dim,), jnp.float32), 'Wq': jax.random.normal(ks[3], (dim, inner), jnp.float32) * s, 'Wkv': jax.random.normal(ks[4], (ctx_dim, 2 * dim_head), jnp.float32) * s, 'Wout': jax.random.normal(ks[5], (inner, dim), jnp.float32) * s, 'Wff1': jax.random.normal(ks[6], (dim, 2 * ff_inner), jnp.float32) * s, 'Wff2': jax.random.normal(ks[7], (ff_inner, dim), jnp.float32) * s}
    _L0_xattn_all = _L0_xattn_setup()
    _L0_xattn_in = {k: v for k, v in _L0_xattn_all.items() if k in ('gamma', 'ctx_gamma', 'Wq', 'Wkv', 'Wout', 'Wff1', 'Wff2')}
    del _L0_xattn_all

    def _L0_ffn_setup():
        import jax, jax.numpy as jnp
        import numpy as np
        B, S, D, H, E = (4, 256, 128, 256, 8)
        key = jax.random.key(seed)
        ks = jax.random.split(key, 8)
        scale = 0.02
        return {'x': jax.random.normal(ks[0], (B, S, D), dtype=jnp.float32), 'Wr': jax.random.normal(ks[1], (D, E), dtype=jnp.float32) * scale, 'br': jnp.zeros((E,), dtype=jnp.float32), 'W1': jax.random.normal(ks[2], (E, D, H), dtype=jnp.float32) * scale, 'b1': jnp.zeros((E, H), dtype=jnp.float32), 'W2': jax.random.normal(ks[3], (E, H, D), dtype=jnp.float32) * scale, 'b2': jnp.zeros((E, D), dtype=jnp.float32)}
    _L0_ffn_all = _L0_ffn_setup()
    _L0_ffn_in = {k: v for k, v in _L0_ffn_all.items() if k in ('Wr', 'br', 'W1', 'b1', 'W2', 'b2')}
    del _L0_ffn_all

    def _L1_xattn_setup():
        import jax, jax.numpy as jnp
        import numpy as np
        key = jax.random.key(seed)
        k1, k2 = jax.random.split(key)
        B, L, V, D = (8, 256, 128, 128)
        hidden_states = jax.random.normal(k1, (B, L, D), dtype=jnp.float32)
        visual_hidden_state = jax.random.normal(k2, (B, V, D), dtype=jnp.float32)
        return {'hidden_states': hidden_states, 'visual_hidden_state': visual_hidden_state}
    _L1_xattn_all = _L1_xattn_setup()
    _L1_xattn_in = {k: v for k, v in _L1_xattn_all.items() if k in ()}
    del _L1_xattn_all

    def _L1_ffn_setup():
        import jax, jax.numpy as jnp
        import numpy as np
        HIDDEN = 128
        INNER = 512

        def _weight_quant(w):
            scale = 1.0 / jnp.clip(jnp.mean(jnp.abs(w)), 1e-05)
            wq = jnp.clip(jnp.round(w * scale), -1.0, 1.0) / scale
            return w + jax.lax.stop_gradient(wq - w)

        def _act_quant(x):
            scale = 127.0 / jnp.clip(jnp.max(jnp.abs(x), axis=-1, keepdims=True), 1e-05)
            xq = jnp.clip(jnp.round(x * scale), -128.0, 127.0) / scale
            return x + jax.lax.stop_gradient(xq - x)

        def _bitlinear(x, w):
            return jnp.einsum('bsi,oi->bso', _act_quant(x), _weight_quant(w))
        key = jax.random.key(seed)
        k0, k1, k2, k3 = jax.random.split(key, 4)
        x = jax.random.normal(k0, (4, 256, HIDDEN), dtype=jnp.float32)
        w_gate = jax.random.normal(k1, (INNER, HIDDEN), dtype=jnp.float32) / np.sqrt(HIDDEN)
        w_up = jax.random.normal(k2, (INNER, HIDDEN), dtype=jnp.float32) / np.sqrt(HIDDEN)
        w_down = jax.random.normal(k3, (HIDDEN, INNER), dtype=jnp.float32) / np.sqrt(INNER)
        return {'x': x, 'w_gate': w_gate, 'w_up': w_up, 'w_down': w_down}
    _L1_ffn_all = _L1_ffn_setup()
    _L1_ffn_in = {k: v for k, v in _L1_ffn_all.items() if k in ('w_gate', 'w_up', 'w_down')}
    del _L1_ffn_all

    def _L2_xattn_setup():
        import jax, jax.numpy as jnp
        import numpy as np
        D_MODEL = 128
        N_HEADS = 16
        HEAD_SIZE = D_MODEL // N_HEADS
        key = jax.random.key(seed)
        ks = jax.random.split(key, 10)
        B, Lx, Ly = (2, 256, 256)
        s = 0.02
        x = jax.random.normal(ks[0], (B, Lx, D_MODEL), dtype=jnp.float32)
        y = jax.random.normal(ks[1], (B, Ly, D_MODEL), dtype=jnp.float32)
        Wq = jax.random.normal(ks[2], (N_HEADS, D_MODEL, HEAD_SIZE), dtype=jnp.float32) * s
        bq = jax.random.normal(ks[3], (N_HEADS, HEAD_SIZE), dtype=jnp.float32) * s
        Wk = jax.random.normal(ks[4], (N_HEADS, D_MODEL, HEAD_SIZE), dtype=jnp.float32) * s
        bk = jax.random.normal(ks[5], (N_HEADS, HEAD_SIZE), dtype=jnp.float32) * s
        Wv = jax.random.normal(ks[6], (N_HEADS, D_MODEL, HEAD_SIZE), dtype=jnp.float32) * s
        bv = jax.random.normal(ks[7], (N_HEADS, HEAD_SIZE), dtype=jnp.float32) * s
        Wo = jax.random.normal(ks[8], (D_MODEL, D_MODEL), dtype=jnp.float32) * s
        bo = jax.random.normal(ks[9], (D_MODEL,), dtype=jnp.float32) * s
        return {'x': x, 'y': y, 'Wq': Wq, 'bq': bq, 'Wk': Wk, 'bk': bk, 'Wv': Wv, 'bv': bv, 'Wo': Wo, 'bo': bo}
    _L2_xattn_all = _L2_xattn_setup()
    _L2_xattn_in = {k: v for k, v in _L2_xattn_all.items() if k in ('Wq', 'bq', 'Wk', 'bk', 'Wv', 'bv', 'Wo', 'bo')}
    del _L2_xattn_all

    def _L2_ffn_setup():
        import jax, jax.numpy as jnp
        import numpy as np
        B, S, H = (2, 128, 128)
        E, F = (16, 64)
        G, TOPK_G, TOPK = (4, 2, 4)
        N_SHARED = 2
        ROUTE_SCALE = 1.0
        FS = N_SHARED * F

        def _gate(x, w_gate):
            T = x.shape[0]
            scores = jax.nn.sigmoid(x @ w_gate.T)
            sv = scores.reshape(T, G, E // G)
            group_scores = jax.lax.top_k(sv, 2)[0].sum(-1)
            top_groups = jax.lax.top_k(group_scores, TOPK_G)[1]
            allowed = jnp.zeros((T, G), dtype=bool).at[jnp.arange(T)[:, None], top_groups].set(True)
            masked = jnp.where(allowed[:, :, None], sv, -jnp.inf).reshape(T, E)
            _, idx = jax.lax.top_k(masked, TOPK)
            w = jnp.take_along_axis(scores, idx, axis=1)
            w = w / (w.sum(-1, keepdims=True) + 1e-06) * ROUTE_SCALE
            return (w, idx)

        def _swiglu(x, w1, w3, w2):
            return jax.nn.silu(x @ w1.T) * (x @ w3.T) @ w2.T
        key = jax.random.key(seed)
        ks = jax.random.split(key, 8)
        scale = 0.02
        return {'hidden_states': jax.random.normal(ks[0], (B, S, H), dtype=jnp.float32), 'w_gate': jax.random.normal(ks[1], (E, H), dtype=jnp.float32) * scale, 'w1_e': jax.random.normal(ks[2], (E, F, H), dtype=jnp.float32) * scale, 'w3_e': jax.random.normal(ks[3], (E, F, H), dtype=jnp.float32) * scale, 'w2_e': jax.random.normal(ks[4], (E, H, F), dtype=jnp.float32) * scale, 'w1_s': jax.random.normal(ks[5], (FS, H), dtype=jnp.float32) * scale, 'w3_s': jax.random.normal(ks[6], (FS, H), dtype=jnp.float32) * scale, 'w2_s': jax.random.normal(ks[7], (H, FS), dtype=jnp.float32) * scale}
    _L2_ffn_all = _L2_ffn_setup()
    _L2_ffn_in = {k: v for k, v in _L2_ffn_all.items() if k in ('w_gate', 'w1_e', 'w3_e', 'w2_e', 'w1_s', 'w3_s', 'w2_s')}
    del _L2_ffn_all

    def _L3_xattn_setup():
        import jax, jax.numpy as jnp
        import numpy as np
        DIM = 128
        N_HEADS = 16
        HEAD_DIM = DIM // N_HEADS
        B, L, M = (2, 256, 256)
        key = jax.random.key(seed)
        ks = jax.random.split(key, 7)
        s = 1.0 / np.sqrt(DIM)
        return {'q': jax.random.normal(ks[0], (B, L, DIM), dtype=jnp.float32), 'k': jax.random.normal(ks[1], (B, M, DIM), dtype=jnp.float32), 'v': jax.random.normal(ks[2], (B, M, DIM), dtype=jnp.float32), 'Wq': jax.random.normal(ks[3], (DIM, DIM), dtype=jnp.float32) * s, 'Wk': jax.random.normal(ks[4], (DIM, DIM), dtype=jnp.float32) * s, 'Wv': jax.random.normal(ks[5], (DIM, DIM), dtype=jnp.float32) * s, 'Wo': jax.random.normal(ks[6], (DIM, DIM), dtype=jnp.float32) * s}
    _L3_xattn_all = _L3_xattn_setup()
    _L3_xattn_in = {k: v for k, v in _L3_xattn_all.items() if k in ('Wq', 'Wk', 'Wv', 'Wo')}
    del _L3_xattn_all

    def _L3_ffn_setup():
        import jax, jax.numpy as jnp
        import numpy as np
        B, C, D, O = (4, 512, 128, 128)
        PROJ = 32
        RANKS = [1, 2, 4, 8]
        E = len(RANKS)
        CLAMP_MAX = float(np.log(1.0 / 0.01))

        def _l2norm(v, axis):
            return v / jnp.maximum(jnp.linalg.norm(v, axis=axis, keepdims=True), 1e-12)
        key = jax.random.key(seed)
        ks = jax.random.split(key, 16)
        inp = {'x': jax.random.normal(ks[0], (B, C, D), dtype=jnp.float32), 'W': jax.random.normal(ks[1], (O, D), dtype=jnp.float32) / np.sqrt(D), 'Wp': jax.random.normal(ks[2], (PROJ, D), dtype=jnp.float32) / np.sqrt(D), 'bp': jnp.zeros((PROJ,), dtype=jnp.float32), 'sim': jax.random.normal(ks[3], (PROJ, E), dtype=jnp.float32) * 0.01, 'temp': jnp.full((1,), np.log(1.0 / 0.5), dtype=jnp.float32)}
        for i, r in enumerate(RANKS):
            inp[f'Wd{i}'] = jax.random.normal(ks[4 + 2 * i], (r, D), dtype=jnp.float32) / r
            inp[f'Wu{i}'] = jax.random.normal(ks[5 + 2 * i], (O, r), dtype=jnp.float32) * 0.01
        return inp
    _L3_ffn_all = _L3_ffn_setup()
    _L3_ffn_in = {k: v for k, v in _L3_ffn_all.items() if k in ('W', 'Wp', 'bp', 'sim', 'temp', 'Wd0', 'Wu0', 'Wd1', 'Wu1', 'Wd2', 'Wu2', 'Wd3', 'Wu3')}
    del _L3_ffn_all
    return {'x': x, 'ctx_1024': ctx_1024, 'mask_BxS2_ik0': mask_BxS2_ik0, 'g_xattn': g_xattn, 'g_ffn': g_ffn, 'L0_xattn_gamma': _L0_xattn_in['gamma'], 'L0_xattn_ctx_gamma': _L0_xattn_in['ctx_gamma'], 'L0_xattn_Wq': _L0_xattn_in['Wq'], 'L0_xattn_Wkv': _L0_xattn_in['Wkv'], 'L0_xattn_Wout': _L0_xattn_in['Wout'], 'L0_xattn_Wff1': _L0_xattn_in['Wff1'], 'L0_xattn_Wff2': _L0_xattn_in['Wff2'], 'L0_ffn_Wr': _L0_ffn_in['Wr'], 'L0_ffn_br': _L0_ffn_in['br'], 'L0_ffn_W1': _L0_ffn_in['W1'], 'L0_ffn_b1': _L0_ffn_in['b1'], 'L0_ffn_W2': _L0_ffn_in['W2'], 'L0_ffn_b2': _L0_ffn_in['b2'], 'L1_ffn_w_gate': _L1_ffn_in['w_gate'], 'L1_ffn_w_up': _L1_ffn_in['w_up'], 'L1_ffn_w_down': _L1_ffn_in['w_down'], 'L2_xattn_Wq': _L2_xattn_in['Wq'], 'L2_xattn_bq': _L2_xattn_in['bq'], 'L2_xattn_Wk': _L2_xattn_in['Wk'], 'L2_xattn_bk': _L2_xattn_in['bk'], 'L2_xattn_Wv': _L2_xattn_in['Wv'], 'L2_xattn_bv': _L2_xattn_in['bv'], 'L2_xattn_Wo': _L2_xattn_in['Wo'], 'L2_xattn_bo': _L2_xattn_in['bo'], 'L2_ffn_w_gate': _L2_ffn_in['w_gate'], 'L2_ffn_w1_e': _L2_ffn_in['w1_e'], 'L2_ffn_w3_e': _L2_ffn_in['w3_e'], 'L2_ffn_w2_e': _L2_ffn_in['w2_e'], 'L2_ffn_w1_s': _L2_ffn_in['w1_s'], 'L2_ffn_w3_s': _L2_ffn_in['w3_s'], 'L2_ffn_w2_s': _L2_ffn_in['w2_s'], 'L3_xattn_Wq': _L3_xattn_in['Wq'], 'L3_xattn_Wk': _L3_xattn_in['Wk'], 'L3_xattn_Wv': _L3_xattn_in['Wv'], 'L3_xattn_Wo': _L3_xattn_in['Wo'], 'L3_ffn_W': _L3_ffn_in['W'], 'L3_ffn_Wp': _L3_ffn_in['Wp'], 'L3_ffn_bp': _L3_ffn_in['bp'], 'L3_ffn_sim': _L3_ffn_in['sim'], 'L3_ffn_temp': _L3_ffn_in['temp'], 'L3_ffn_Wd0': _L3_ffn_in['Wd0'], 'L3_ffn_Wu0': _L3_ffn_in['Wu0'], 'L3_ffn_Wd1': _L3_ffn_in['Wd1'], 'L3_ffn_Wu1': _L3_ffn_in['Wu1'], 'L3_ffn_Wd2': _L3_ffn_in['Wd2'], 'L3_ffn_Wu2': _L3_ffn_in['Wu2'], 'L3_ffn_Wd3': _L3_ffn_in['Wd3'], 'L3_ffn_Wu3': _L3_ffn_in['Wu3']}

def reference(x, ctx_1024, mask_BxS2_ik0, g_xattn, g_ffn, L0_xattn_gamma, L0_xattn_ctx_gamma, L0_xattn_Wq, L0_xattn_Wkv, L0_xattn_Wout, L0_xattn_Wff1, L0_xattn_Wff2, L0_ffn_Wr, L0_ffn_br, L0_ffn_W1, L0_ffn_b1, L0_ffn_W2, L0_ffn_b2, L1_ffn_w_gate, L1_ffn_w_up, L1_ffn_w_down, L2_xattn_Wq, L2_xattn_bq, L2_xattn_Wk, L2_xattn_bk, L2_xattn_Wv, L2_xattn_bv, L2_xattn_Wo, L2_xattn_bo, L2_ffn_w_gate, L2_ffn_w1_e, L2_ffn_w3_e, L2_ffn_w2_e, L2_ffn_w1_s, L2_ffn_w3_s, L2_ffn_w2_s, L3_xattn_Wq, L3_xattn_Wk, L3_xattn_Wv, L3_xattn_Wo, L3_ffn_W, L3_ffn_Wp, L3_ffn_bp, L3_ffn_sim, L3_ffn_temp, L3_ffn_Wd0, L3_ffn_Wu0, L3_ffn_Wd1, L3_ffn_Wu1, L3_ffn_Wd2, L3_ffn_Wu2, L3_ffn_Wd3, L3_ffn_Wu3):
    import jax
    import jax.numpy as jnp

    def _L0_xattn_ref(x, context, mask, gamma, ctx_gamma, Wq, Wkv, Wout, Wff1, Wff2):
        import jax, jax.numpy as jnp
        import numpy as np
        EPS = 1e-05

        def layer_norm(x, gamma):
            mu = jnp.mean(x, axis=-1, keepdims=True)
            var = jnp.mean(jnp.square(x - mu), axis=-1, keepdims=True)
            return (x - mu) / jnp.sqrt(var + EPS) * gamma
        heads, dim_head = (16, 64)
        b, n, dim = x.shape
        scale = dim_head ** (-0.5)
        xn = layer_norm(x, gamma)
        ctx = layer_norm(context, ctx_gamma)
        q = (xn @ Wq).reshape(b, n, heads, dim_head).transpose(0, 2, 1, 3) * scale
        kv = ctx @ Wkv
        k, v = (kv[..., :dim_head], kv[..., dim_head:])
        sim = jnp.einsum('bhid,bjd->bhij', q, k)
        sim = jnp.where((mask == 0)[:, None, None, :], -jnp.inf, sim)
        attn = jax.nn.softmax(sim, axis=-1)
        out = jnp.einsum('bhij,bjd->bhid', attn, v)
        out = out.transpose(0, 2, 1, 3).reshape(b, n, heads * dim_head)
        out = out @ Wout
        h = xn @ Wff1
        ff_inner = Wff2.shape[0]
        a, gate = (h[..., :ff_inner], h[..., ff_inner:])
        out = out + jax.nn.silu(gate) * a @ Wff2
        return out

    def _L0_ffn_ref(x, Wr, br, W1, b1, W2, b2):
        import jax, jax.numpy as jnp
        import numpy as np
        B, S, D, H, E = (4, 256, 128, 256, 8)
        d = x.shape[-1]
        tokens = x.reshape(-1, d)
        logits = tokens @ Wr + br
        probs = jax.nn.softmax(logits, axis=-1)
        expert = jnp.argmax(probs, axis=-1)
        max_prob = jnp.take_along_axis(probs, expert[:, None], axis=-1)
        h = jax.nn.relu(jnp.einsum('td,edh->teh', tokens, W1) + b1[None])
        y = jnp.einsum('teh,ehd->ted', h, W2) + b2[None]
        out = jnp.take_along_axis(y, expert[:, None, None], axis=1)[:, 0, :]
        return (out * max_prob).reshape(x.shape)

    def _L1_xattn_ref(hidden_states, visual_hidden_state):
        import jax, jax.numpy as jnp
        import numpy as np
        scores = jnp.einsum('bld,bvd->blv', hidden_states, visual_hidden_state)
        probs = jax.nn.softmax(scores, axis=-1)
        return jnp.einsum('blv,bvd->bld', probs, visual_hidden_state)

    def _L1_ffn_ref(x, w_gate, w_up, w_down):
        import jax, jax.numpy as jnp
        import numpy as np
        HIDDEN = 128
        INNER = 512

        def _weight_quant(w):
            scale = 1.0 / jnp.clip(jnp.mean(jnp.abs(w)), 1e-05)
            wq = jnp.clip(jnp.round(w * scale), -1.0, 1.0) / scale
            return w + jax.lax.stop_gradient(wq - w)

        def _act_quant(x):
            scale = 127.0 / jnp.clip(jnp.max(jnp.abs(x), axis=-1, keepdims=True), 1e-05)
            xq = jnp.clip(jnp.round(x * scale), -128.0, 127.0) / scale
            return x + jax.lax.stop_gradient(xq - x)

        def _bitlinear(x, w):
            return jnp.einsum('bsi,oi->bso', _act_quant(x), _weight_quant(w))
        gate = jax.nn.silu(_bitlinear(x, w_gate))
        up = _bitlinear(x, w_up)
        return _bitlinear(gate * up, w_down)

    def _L2_xattn_ref(x, y, Wq, bq, Wk, bk, Wv, bv, Wo, bo):
        import jax, jax.numpy as jnp
        import numpy as np
        D_MODEL = 128
        N_HEADS = 16
        HEAD_SIZE = D_MODEL // N_HEADS
        Q = jnp.einsum('bxd,hde->bhxe', x, Wq) + bq[None, :, None, :]
        K = jnp.einsum('byd,hde->bhye', y, Wk) + bk[None, :, None, :]
        V = jnp.einsum('byd,hde->bhye', y, Wv) + bv[None, :, None, :]
        scale = 1.0 / jnp.sqrt(jnp.float32(HEAD_SIZE))
        scores = jnp.einsum('bhxe,bhye->bhxy', Q, K) * scale
        attn = jax.nn.softmax(scores, axis=-1)
        ctx = jnp.einsum('bhxy,bhye->bhxe', attn, V)
        B, H, Lx, hs = ctx.shape
        ctx = jnp.transpose(ctx, (0, 2, 1, 3)).reshape(B, Lx, H * hs)
        return ctx @ Wo + bo

    def _L2_ffn_ref(hidden_states, w_gate, w1_e, w3_e, w2_e, w1_s, w3_s, w2_s):
        import jax, jax.numpy as jnp
        import numpy as np
        B, S, H = (2, 128, 128)
        E, F = (16, 64)
        G, TOPK_G, TOPK = (4, 2, 4)
        N_SHARED = 2
        ROUTE_SCALE = 1.0
        FS = N_SHARED * F

        def _gate(x, w_gate):
            T = x.shape[0]
            scores = jax.nn.sigmoid(x @ w_gate.T)
            sv = scores.reshape(T, G, E // G)
            group_scores = jax.lax.top_k(sv, 2)[0].sum(-1)
            top_groups = jax.lax.top_k(group_scores, TOPK_G)[1]
            allowed = jnp.zeros((T, G), dtype=bool).at[jnp.arange(T)[:, None], top_groups].set(True)
            masked = jnp.where(allowed[:, :, None], sv, -jnp.inf).reshape(T, E)
            _, idx = jax.lax.top_k(masked, TOPK)
            w = jnp.take_along_axis(scores, idx, axis=1)
            w = w / (w.sum(-1, keepdims=True) + 1e-06) * ROUTE_SCALE
            return (w, idx)

        def _swiglu(x, w1, w3, w2):
            return jax.nn.silu(x @ w1.T) * (x @ w3.T) @ w2.T
        shape = hidden_states.shape
        x = hidden_states.reshape(-1, H)
        weights, idx = _gate(x, w_gate)
        combine = (jax.nn.one_hot(idx, E, dtype=x.dtype) * weights[..., None]).sum(1)
        g = jax.nn.silu(jnp.einsum('th,efh->tef', x, w1_e))
        u = jnp.einsum('th,efh->tef', x, w3_e)
        routed = jnp.einsum('tef,ehf,te->th', g * u, w2_e, combine)
        shared = _swiglu(x, w1_s, w3_s, w2_s)
        return (routed + shared).reshape(shape)

    def _L3_xattn_ref(q, k, v, Wq, Wk, Wv, Wo):
        import jax, jax.numpy as jnp
        import numpy as np
        DIM = 128
        N_HEADS = 16
        HEAD_DIM = DIM // N_HEADS
        B, L, M = (2, 256, 256)
        b, l, _ = q.shape
        m = k.shape[1]
        qp = q @ Wq.T
        kp = k @ Wk.T
        vp = v @ Wv.T
        qh = qp.reshape(b, l, HEAD_DIM, N_HEADS)
        kh = kp.reshape(b, m, HEAD_DIM, N_HEADS)
        score = jnp.einsum('bldn,bmdn->blmn', qh, kh) / jnp.sqrt(jnp.float32(HEAD_DIM))
        attn = jax.nn.softmax(score, axis=2)
        x = jnp.einsum('blmn,bmdn->bldn', attn, kh)
        x = x.reshape(b, l, DIM)
        return x @ Wo.T

    def _L3_ffn_ref(x, W, Wp, bp, sim, temp, Wd0, Wu0, Wd1, Wu1, Wd2, Wu2, Wd3, Wu3):
        import jax, jax.numpy as jnp
        import numpy as np
        B, C, D, O = (4, 512, 128, 128)
        PROJ = 32
        RANKS = [1, 2, 4, 8]
        E = len(RANKS)
        CLAMP_MAX = float(np.log(1.0 / 0.01))

        def _l2norm(v, axis):
            return v / jnp.maximum(jnp.linalg.norm(v, axis=axis, keepdims=True), 1e-12)
        base = jnp.einsum('bcd,od->bco', x, W)
        xf = x.reshape(-1, x.shape[-1])
        proj = _l2norm(xf @ Wp.T + bp, axis=1)
        simn = _l2norm(sim, axis=0)
        scale = jnp.exp(jnp.minimum(temp, CLAMP_MAX))
        logits = proj @ simn * scale
        lw = jax.nn.softmax(logits, axis=1)
        top1 = jnp.argmax(lw, axis=1)
        ret = jnp.where(jnp.arange(E)[None, :] == top1[:, None], lw, 0.0)
        ret = ret.reshape(x.shape[0], x.shape[1], E)
        downs = (Wd0, Wd1, Wd2, Wd3)
        ups = (Wu0, Wu1, Wu2, Wu3)
        l = jnp.stack([jnp.einsum('bcr,or->bco', jnp.einsum('bcd,rd->bcr', x, d), u) for d, u in zip(downs, ups)], axis=2)
        res = jnp.sum(ret[..., None] * l, axis=2)
        return base + res
    x = x + jnp.tanh(g_xattn[0]) * _L0_xattn_ref(_layernorm(x, axis=-1), ctx_1024, mask_BxS2_ik0, L0_xattn_gamma, L0_xattn_ctx_gamma, L0_xattn_Wq, L0_xattn_Wkv, L0_xattn_Wout, L0_xattn_Wff1, L0_xattn_Wff2)
    x = x + jnp.tanh(g_ffn[0]) * _L0_ffn_ref(_layernorm(x, axis=-1), L0_ffn_Wr, L0_ffn_br, L0_ffn_W1, L0_ffn_b1, L0_ffn_W2, L0_ffn_b2)
    x = x + jnp.tanh(g_xattn[1]) * _L1_xattn_ref(_layernorm(x, axis=-1), ctx_1024)
    x = x + jnp.tanh(g_ffn[1]) * _L1_ffn_ref(_layernorm(x, axis=-1), L1_ffn_w_gate, L1_ffn_w_up, L1_ffn_w_down)
    x = x + jnp.tanh(g_xattn[2]) * _L2_xattn_ref(_layernorm(x, axis=-1), ctx_1024, L2_xattn_Wq, L2_xattn_bq, L2_xattn_Wk, L2_xattn_bk, L2_xattn_Wv, L2_xattn_bv, L2_xattn_Wo, L2_xattn_bo)
    x = x + jnp.tanh(g_ffn[2]) * _L2_ffn_ref(_layernorm(x, axis=-1), L2_ffn_w_gate, L2_ffn_w1_e, L2_ffn_w3_e, L2_ffn_w2_e, L2_ffn_w1_s, L2_ffn_w3_s, L2_ffn_w2_s)
    x = x + jnp.tanh(g_xattn[3]) * _L3_xattn_ref(_layernorm(x, axis=-1), ctx_1024, ctx_1024, L3_xattn_Wq, L3_xattn_Wk, L3_xattn_Wv, L3_xattn_Wo)
    x = x + jnp.tanh(g_ffn[3]) * _L3_ffn_ref(_layernorm(x, axis=-1), L3_ffn_W, L3_ffn_Wp, L3_ffn_bp, L3_ffn_sim, L3_ffn_temp, L3_ffn_Wd0, L3_ffn_Wu0, L3_ffn_Wd1, L3_ffn_Wu1, L3_ffn_Wd2, L3_ffn_Wu2, L3_ffn_Wd3, L3_ffn_Wu3)
    return x

_drawn_inputs = setup_inputs


def setup_inputs(seed=0):
    import zlib

    import numpy as np

    out = dict(_drawn_inputs(seed))
    spreads = {'L0_xattn_gamma': (1.0, 0.6),
     'L0_xattn_ctx_gamma': (1.0, 0.586),
     'L0_ffn_br': (0.0, 0.332),
     'L0_ffn_b1': (0.0, 0.8),
     'L0_ffn_b2': (0.0, 0.336),
     'L3_ffn_bp': (0.0, 0.8)}
    factors = {'L0_xattn_Wq': 8.0,
     'L0_xattn_Wff1': 3.217,
     'L0_xattn_Wff2': 3.058,
     'L0_ffn_W1': 4.8,
     'L0_ffn_W2': 3.881,
     'L2_xattn_Wq': 8.0,
     'L2_xattn_bq': 8.0,
     'L2_xattn_Wk': 8.0,
     'L2_xattn_bk': 8.0,
     'L2_xattn_Wv': 4.308,
     'L2_xattn_bv': 8.0,
     'L2_xattn_Wo': 4.036,
     'L2_xattn_bo': 4.605,
     'L2_ffn_w_gate': 8.0,
     'L2_ffn_w1_e': 8.0,
     'L2_ffn_w3_e': 8.0,
     'L2_ffn_w2_e': 8.0,
     'L2_ffn_w1_s': 8.0,
     'L2_ffn_w3_s': 8.0,
     'L2_ffn_w2_s': 8.0,
     'L3_ffn_Wp': 4.398,
     'L3_ffn_sim': 4.151,
     'L3_ffn_Wd0': 7.436,
     'L3_ffn_Wu0': 6.06,
     'L3_ffn_Wd1': 8.0,
     'L3_ffn_Wu1': 8.0,
     'L3_ffn_Wd2': 8.0,
     'L3_ffn_Wu2': 8.0,
     'L3_ffn_Wd3': 8.0,
     'L3_ffn_Wu3': 8.0}
    for name, (base, spread) in spreads.items():
        noise = np.random.default_rng([zlib.crc32(name.encode()), seed]).standard_normal(out[name].shape)
        drawn = base * np.exp(spread * noise) if base else spread * noise
        out[name] = jnp.asarray(drawn.astype(out[name].dtype))
    for name, factor in factors.items():
        out[name] = (out[name] * factor).astype(out[name].dtype)
    return out
```

```python
from contextlib import ExitStack

import numpy as np
import concourse.bass as bass
from concourse import mybir

F32, BF16, I32 = mybir.dt.float32, mybir.dt.bfloat16, mybir.dt.int32
ALU, ACT, AX = mybir.AluOpType, mybir.ActivationFunctionType, mybir.AxisListType

P = 128
D = 128
B, SEQ, CTX = 4, 512, 77
TILES = SEQ // P
H = 16
HC = H * CTX
HB = H // 4
SB = HB * CTX
NCH = -(-HC // P)
LASTROWS = HC - (NCH - 1) * P
DH0 = 64
DH = D // H
VW = DH + 1
FF0 = 512
E0, H0 = 8, 256
FB = 512
E2, F2W, FS2 = 16, 64, 128
GW = 384
RANKS = (1, 2, 4, 8)
R = sum(RANKS)
PROJ = 32
LN_EPS = 1e-5
MASKED = -1e30
MAGIC = 1.5 * 2.0 ** 23
CLAMP = float(np.log(1.0 / 0.01))

DVE_STEPS = 293
BLOCKS = ("A0", "F0", "A1", "F1", "A2", "F2", "A3", "F3")
NB = len(BLOCKS)
GATE = {k: (int(k[1]) if k[0] == "A" else 4 + int(k[1])) for k in BLOCKS}
UNITS = [(BLOCKS[u // TILES], u % TILES) for u in range(NB * TILES)]

PE_PARTS = (("first", 1), ("late_transpose", 3), ("xT", 0), ("middle", 2), ("extra", 1),
            ("project", 0), ("output", 3), ("values", 2), ("spread", 1))
FILLS = {
    "A0": {"xT": ("X xT",), "first": ("S scores",), "middle": ("T0 gate", "T1 up"),
           "late_transpose": ("T0 hT", "T1 pa", "T0 pb", "T1 pc"), "output": ("O out",)},
    "F0": {"xT": ("X xT",), "project": ("X logits",), "extra": ("X pickT",), "spread": ("S masks",),
           "middle": ("O hidden",), "late_transpose": ("O bias", "T0 ya", "T1 yb")},
    "A1": {"xT": ("X xT",), "first": ("S scores",), "middle": ("T0 pT",), "values": ("O out",)},
    "F1": {"xT": ("X xT",), "extra": ("T0 gate", "T1 up"), "middle": ("T0 hT",), "values": ("O out",)},
    "A2": {"xT": ("X xT",), "project": ("X q",), "first": ("S scores",),
           "middle": ("T0 pa", "T1 pb", "T0 pc"), "values": ("O values",),
           "late_transpose": ("X vT",), "output": ("O out",)},
    "F2": {"xT": ("X xT",), "project": ("X gate",), "first": ("S gu",), "middle": ("T0 gate", "T1 up"),
           "late_transpose": ("T0 ha", "T1 hb", "T0 hc"), "output": ("O out",)},
    "F3": {"xT": ("X xT",), "first": ("S all",), "extra": ("X projT",), "middle": ("X logits",),
           "late_transpose": ("X downT",), "output": ("O out",)},
}
FILLS["A3"] = FILLS["A2"]
PRELUDE = ("X wmean", "X simnorm")
PREP = ("X cT", "X kv", "X kv0", "S a", "S b", "T0 ba", "T1 bb", "T0 bc",
        "T0 va", "T1 vb", "T0 vc", "T0 ka", "T1 kb", "T0 kc")


def steps():
    n = len(UNITS)
    for s in range(n + 3):
        for part, phase in PE_PARTS:
            if 0 <= s - phase < n:
                yield part, s - phase


class Bank:

    def __init__(self, name, tile, full, drained):
        self.name, self.tile, self.full, self.drained = name, tile, full, drained
        self.before = sum(f.split()[0] == name for f in PRELUDE)
        self.order = {}
        for f in PREP:
            self.add(f, None)
        for part, u in steps():
            for f in FILLS[UNITS[u][0]].get(part, ()):
                self.add(f, u)
        self.per_batch = len(self.order)

    def add(self, filling, u):
        bank, what = filling.split()
        if bank == self.name:
            self.order[what, u] = len(self.order)


PACKS = {
    "base": [("ident", P, P), ("delta", P, H), ("ones_col", P, NCH * H), ("desc0", P, E0),
             ("desc3", P, 4 + R), ("gates", P, 8), ("tri4", P, 16), ("tri16", P, 256), ("ln_gamma", P, 2)],
    "att0": [("wk0", P, 2 * DH0), ("wv0", P, 2 * DH0), ("wq0", P, 8 * D), ("wo0", P, 8 * D)],
    "att23": [("wq2", P, D), ("wk2", P, D), ("wv2", P, D), ("b2qkv", P, 3), ("wo2", P, D),
              ("bo2", 1, D), ("wq3", P, D), ("wk3", P, D), ("wo3", P, D)],
    "ff0": [("wff1", P, 2 * FF0), ("wff2", P, 4 * D)],
    "top1": [("wr", P, E0), ("br", P, E0), ("w1", P, E0 * H0), ("b1", E0, H0), ("w2", P, 2 * E0 * D),
             ("b2", E0, D)],
    "tern": [("wt", P, 3 * FB)],
    "low": [("w3", P, PROJ + R + D), ("bp", P, PROJ), ("sim", PROJ, 4 + R), ("temp", PROJ, 1),
            ("wu", R, D)],
    "top4": [("wg", P, E2), ("w13", P, 6 * GW), ("w2s", P, 9 * D)],
}
WIDTH = {k: sum(c for _, _, c in v) for k, v in PACKS.items()}


def gated_flamingo(nc, x_in, ctx_in, ctxT_in, mask_in, packs, out):
    with ExitStack() as stack:
        def sb(name, shape, dt=F32):
            return stack.enter_context(nc.sbuf_tensor(name, shape, dt))

        def psum(name, shape):
            return stack.enter_context(nc.psum_tensor(name, shape, F32))

        def sem(name):
            return stack.enter_context(nc.semaphore(name))

        hh = sb("hh", [P, 3, 3 * GW])
        W, loaded = {}, {}
        for pack, parts in PACKS.items():
            tile = hh[:, :, :].rearrange("p b n -> p (b n)") if pack == "tern" else sb("pack_" + pack, [P, WIDTH[pack]])
            loaded[pack] = sem("loaded_" + pack)
            at = 0
            for name, rows, cols in parts:
                W[name] = tile[0:rows, at:at + cols]
                at += cols
            W["pack_" + pack] = tile[:, 0:WIDTH[pack]]
        ident = W["ident"]
        ident_b = sb("ident_b", [P, P], BF16)
        ones = sb("ones", [P, P])
        ones_b = sb("ones_b", [1, P], BF16)
        pick_row = sb("pick_row", [E0, E0, P], BF16)
        half = sb("half", [P, 4])
        tg = sb("tg", [P, 8])
        tgh = sb("tgh", [P, 1])
        sq2 = sb("sq2", [P, 1])
        wt_q = sb("wt_q", [P, 3 * FB], BF16)
        wt_sum = sb("wt_sum", [P, 3])
        wt_mean = sb("wt_mean", [P, 3])
        wt_inv = sb("wt_inv", [P, 3])
        wt_c = sb("wt_c", [P, 3])
        sim_sq = sb("sim_sq", [PROJ, 4 + R])
        sim_n = sb("sim_n", [PROJ, 4 + R])
        sim_s = sb("sim_s", [PROJ, 1])

        ctx_st = sb("ctx_st", [CTX, D])
        ctxT_st = sb("ctxT_st", [D, CTX])
        mask_st = sb("mask_st", [P, CTX], I32)
        x_st = sb("x_st", [P, TILES, D])
        ctx = sb("ctx", [CTX, D])
        ctxT = sb("ctxT", [D, CTX])
        mask_row = sb("mask_row", [1, HB, CTX], BF16)
        seen = sb("seen", [P, CTX])
        anyseen = sb("anyseen", [P, 3])
        cstat = sb("cstat", [CTX, 6])
        cmv = sb("cmv", [CTX, 2])
        cve = sb("cve", [CTX, 1])
        crs = sb("crs", [CTX, 1])
        ctxn = sb("ctxn", [CTX, D])
        ctxnT = sb("ctxnT", [D, CTX])
        k0 = sb("k0", [P, 2, CTX])
        v0 = sb("v0", [P, 2, CTX])
        A0 = sb("A0", [D, HC])
        B0 = sb("B0", [P, NCH, D])
        k2 = sb("k2", [P, CTX])
        v2 = sb("v2", [P, CTX])
        k3 = sb("k3", [P, CTX])
        K2 = sb("K2", [P, H, CTX])
        K3 = sb("K3", [P, H, CTX])
        V2 = sb("V2", [P, NCH, H, VW])
        V3 = sb("V3", [P, NCH, H, VW])

        x = sb("x", [P, TILES, D])
        y = sb("y", [P, TILES, D])
        stat = sb("stat", [P, 6])
        mv = sb("mv", [P, TILES, 2])
        ve = sb("ve", [P, TILES])
        rstd = sb("rstd", [P, TILES])
        xh = sb("xh", [P, TILES, D])
        xhq = sb("xhq", [P, 2, D])
        xq = sb("xq", [P, TILES, D], BF16)
        xT = sb("xT", [D, TILES, P])
        qT = sb("qT", [D, 2, P])
        xTq = sb("xTq", [D, TILES, P], BF16)
        mx = sb("mx", [P, TILES, H])
        pr = sb("pr", [P, 3, HC])
        wt_r = pr[:, :, :].rearrange("p b n -> p (b n)")[:, 0:3 * FB]
        B0T = pr[:, 1, :]
        V2x = pr[:, 2, :].rearrange("p (h c) -> p h c", c=CTX)
        pT = sb("pT", [P, 2, NCH, P])
        rs = sb("rs", [P, TILES, H])
        ri = sb("ri", [P, TILES, H])
        cv = sb("cv", [P, 2, D])
        cvT = sb("cvT", [D, 2, P])
        th = sb("th", [P, 2, 3 * GW])
        g1 = sb("g1", [P, 2, 3 * GW])
        hT = sb("hT", [P, 2, 9, P])
        hq = sb("hq", [P, 2, FB], BF16)
        hqT = sb("hqT", [P, 2, 4, P], BF16)
        sc = sb("sc", [P, TILES, 16])
        lg = sb("lg", [P, TILES, 4 + R])
        tt = sb("tt", [P, TILES, 4 + R])
        oh = sb("oh", [P, TILES, 4 + R])
        ex = sb("ex", [P, TILES, E0])
        ohT = sb("ohT", [E0, TILES, P])
        ohTb = sb("ohTb", [E0, 2, P], BF16)
        xm = sb("xm", [D, 2, E0, P])
        hid = sb("hid", [P, 2, 2, P])
        sg = sb("sg", [P, TILES, E2])
        sig = sb("sig", [P, TILES, E2])
        pairs = sb("pairs", [P, 4, 6])
        gs = sb("gs", [P, 4])
        cmp4 = sb("cmp4", [P, 4, 2, 4])
        rank4 = sb("rank4", [P, 4])
        cmp16 = sb("cmp16", [P, E2, 2, E2])
        rank16 = sb("rank16", [P, E2])
        picked = sb("picked", [P, E2])
        allow1 = sb("allow1", [P, 4])
        psc = sb("psc", [P, 4])
        allow = sb("allow", [P, 4])
        msk = sb("msk", [P, E2])
        comb = sb("comb", [P, TILES, E2])
        pj = sb("pj", [P, TILES, PROJ])
        pj2 = sb("pj2", [P, PROJ])
        pjT = sb("pjT", [PROJ, 2, P])
        dn = sb("dn", [P, TILES, R])
        dm = sb("dm", [P, TILES, R])
        dmT = sb("dmT", [R, 2, P])

        S, T0, T1, O, X = (Bank(n, psum("psum_" + n, s), sem(n + "_full"), sem(n + "_drained")) for n, s in
                           (("S", [P, 4, 512]), ("T0", [P, 512]), ("T1", [P, 512]), ("O", [P, 512]), ("X", [P, 512])))
        banks = (S, T0, T1, O, X)

        U = len(UNITS)
        events = {}

        def event(name, per_batch, before=0):
            events[name] = (sem(name), per_batch, before)

        event("var_ready", U + 1)
        event("rstd_ready", U + 1)
        event("xh_ready", U + 1)
        event("x_copied", 2)
        event("ctx_used", 1)
        event("mask_ready", 1)
        event("expanded", 3)
        event("inv0", TILES)
        event("probs0", TILES)
        event("y_ready", TILES)
        for name in ("probs_A0", "probs_A2", "probs_A3",
                     "tanh_A0", "tanh_F1", "tanh_F2a", "tanh_F2b",
                     "nmax_A1",
                     "centred_F0", "centred_F3",
                     "expsum_F0", "expsum_F3",
                     "pick_ready",
                     "hq_ready",
                     "comb_ready",
                     "weighted_F2a", "weighted_F2b",
                     "pj_ready", "ss_ready",
                     "rn_ready",
                     "dm_ready"):
            event(name, TILES)
        s_x_loaded, s_c_loaded, s_stored = sem("x_loaded"), sem("c_loaded"), sem("stored")
        s_const, s_tg, s_prel = sem("const_ready"), sem("tanh_gates"), sem("prelude")
        s_dve, s_simpow, s_temp, s_quant = sem("dve_step"), sem("sim_pow"), sem("temp_exp"), sem("ternary_ready")
        s_carry = sem("wait_carrier")
        block = stack.enter_context(nc.Block())

        def helpers(eng, it):
            def full(bank, what, u=None):
                eng.wait_ge(bank.full, it * bank.per_batch + (bank.before + bank.order[what, u] + 1))

            def free(bank, what, u=None):
                eng.wait_ge(bank.drained, it * bank.per_batch + (bank.before + bank.order[what, u] + 1))

            def drained(bank, what, u=None):
                eng.wait_ge(bank.drained, it * bank.per_batch + (bank.before + bank.order[what, u] + 2))

            def wait(name, n):
                s, per, before = events[name]
                eng.wait_ge(s, it * per + (before + n + 1))
            return full, free, drained, wait

        def inc(ins, name):
            return ins.then_inc(events[name][0], 1)

        @block.sync
        def _(sp):
            def load_ctx(b):
                sp.dma_start(ctx_st[:, :], ctx_in[b]).then_inc(s_c_loaded, 16)
                sp.dma_start(ctxT_st[:, :], ctxT_in[b]).then_inc(s_c_loaded, 16)
                sp.dma_start(mask_st[:, :], mask_in[b]).then_inc(s_c_loaded, 16)

            def load_x(b):
                sp.dma_start(x_st[:, :, :], x_in[b].rearrange("(t p) d -> p t d", p=P)).then_inc(s_x_loaded, 16)

            sp.sem_inc(s_stored, 16 * TILES)
            for pack in PACKS:
                sp.dma_start(W["pack_" + pack], packs[pack]).then_inc(loaded[pack], 16)
                if pack == "base":
                    load_ctx(0)
                    load_x(0)
            for b in range(B):
                if b + 1 < B:
                    sp.wait_ge(events["x_copied"][0], 2 * (b + 1))
                    sp.wait_ge(events["ctx_used"][0], b + 1)
                    load_ctx(b + 1)
                    load_x(b + 1)
                for t in range(TILES):
                    sp.wait_ge(events["y_ready"][0], TILES * b + t + 1)
                    sp.dma_start(out[b, t * P:(t + 1) * P, :], y[:, t, :]).then_inc(s_stored, 16)
            sp.wait_ge(s_stored, 16 * B * TILES + 16 * TILES)

        @block.tensor
        def _(pe):
            def transposes(dst, src, chunks):
                for n, (lo, hi) in enumerate(chunks):
                    last = pe.transpose(dst[0:hi - lo, n * P:(n + 1) * P], src[:, lo:hi], ident)
                return last

            pe.wait_ge(s_const, 9)
            pe.wait_ge(s_prel, 1)
            pe.wait_ge(X.drained, 1)
            pe.matmul(X.tile[:, 0:3], ones[:, :], wt_sum[:, :], start=True, stop=True).then_inc(X.full, 1)
            pe.wait_ge(X.drained, 2)
            pe.wait_ge(s_prel, 2)
            pe.matmul(X.tile[0:PROJ, 0:4 + R], ones[0:PROJ, 0:PROJ], sim_sq[:, :], start=True, stop=True)\
              .then_inc(X.full, 1)
            for pack in ("att0", "att23"):
                pe.wait_ge(loaded[pack], 16)

            with pe.Fori(0, B) as it:
                full, free, drained, wait = helpers(pe, it)

                wait("xh_ready", 0)
                free(X, "cT")
                pe.transpose(X.tile[:, 0:CTX], ctxn[:, :], ident[0:CTX, 0:CTX]).then_inc(X.full, 1)
                wait("x_copied", 0)
                free(X, "kv")
                pe.matmul(X.tile[:, 0:CTX], W["wk2"], ctxT[:, :], start=True, stop=True)
                pe.matmul(X.tile[:, P:P + CTX], W["wv2"], ctxT[:, :], start=True, stop=True)
                pe.matmul(X.tile[:, 2 * P:2 * P + CTX], W["wk3"], ctxT[:, :], start=True, stop=True)\
                  .then_inc(X.full, 1)
                free(X, "kv0")
                pe.matmul(X.tile[:, 0:CTX], W["wk0"], ctxnT[:, :], start=True, stop=True)
                pe.matmul(X.tile[:, P:P + CTX], W["wv0"], ctxnT[:, :], start=True, stop=True).then_inc(X.full, 1)
                drained(X, "kv0")
                for what, w, kv in (("a", "wq0", k0), ("b", "wo0", v0)):
                    free(S, what)
                    for g in range(H // 2):
                        last = pe.matmul(S.tile[:, g // 2, g % 2 * 2 * CTX:(g % 2 + 1) * 2 * CTX],
                                         W[w][:, g * D:(g + 1) * D], kv[:, :, :], start=True, stop=True)
                    last.then_inc(S.full, 1)
                cuts = [(n * P, min((n + 1) * P, HC)) for n in range(NCH)]
                trio = (cuts[0:4], cuts[4:8], cuts[8:NCH])

                def turn(src, names):
                    for bank, what, cs in zip((T0, T1, T0), names, trio):
                        free(bank, what)
                        transposes(bank.tile, src, cs).then_inc(bank.full, 1)

                drained(S, "b")
                turn(B0T, ("ba", "bb", "bc"))
                wait("expanded", 1)
                turn(V2x.rearrange("p h c -> p (h c)"), ("va", "vb", "vc"))
                wait("expanded", 2)
                turn(K3[:, :, :].rearrange("p h c -> p (h c)"), ("ka", "kb", "kc"))
                drained(T0, "kc")

                def xT_(k, u, t):
                    wait("xh_ready", u + 1)
                    free(X, "xT", u)
                    if k == "F1":
                        pe.transpose(X.tile[:, 0:P // 2].bitcast(BF16), xq[:, t, :], ident_b[:, :])\
                          .then_inc(X.full, 1)
                    else:
                        pe.transpose(X.tile[:, 0:P], xh[:, t, :], ident).then_inc(X.full, 1)

                def first(k, u, t):
                    n = 4 * int(k[1]) + t
                    if k == "A0":
                        wait("mask_ready", 0)
                        drained(X, "xT", u)
                        drained(T0, "bc")
                        free(S, "scores", u)
                        for q in range(4):
                            pe.matmul(S.tile[:, q, 0:SB], xT[:, t, :], A0[:, q * SB:(q + 1) * SB],
                                      start=True, stop=False)
                            last = pe.matmul(S.tile[:, q, 0:SB], ones_b[:, :],
                                             mask_row[:, :, :].rearrange("o h c -> o (h c)"),
                                             start=False, stop=True)
                        last.then_inc(S.full, 1)
                    elif k in ("A2", "A3"):
                        K = (K2 if k == "A2" else K3)[:, :, :].rearrange("p h c -> p (h c)")
                        drained(X, "q", u)
                        free(S, "scores", u)
                        for q in range(4):
                            last = pe.matmul(S.tile[:, q, 0:SB], qT[:, u % 2, :], K[:, q * SB:(q + 1) * SB],
                                             start=True, stop=True)
                        last.then_inc(S.full, 1)
                    elif k == "A1":
                        drained(X, "xT", u)
                        free(S, "scores", u)
                        pe.matmul(S.tile[:, 0, 0:CTX], xT[:, t, :], ctxT[:, :], start=True, stop=True)\
                          .then_inc(S.full, 1)
                    elif k == "F2":
                        pe.wait_ge(loaded["top4"], 16)
                        drained(X, "xT", u)
                        free(S, "gu", u)
                        for q, c in enumerate((0, 1, 3, 4)):
                            last = pe.matmul(S.tile[:, q, 0:GW], xT[:, t, :], W["w13"][:, c * GW:(c + 1) * GW],
                                             start=True, stop=True)
                        last.then_inc(S.full, 1)
                    elif k == "F3":
                        pe.wait_ge(loaded["low"], 16)
                        drained(X, "xT", u)
                        free(S, "all", u)
                        pe.matmul(S.tile[:, 0, 0:PROJ + R + D], xT[:, t, :], W["w3"], start=True, stop=True)\
                          .then_inc(S.full, 1)

                def late_transpose(k, u, t):
                    if k == "A0":
                        drained(T1, "up", u)
                        free(T0, "hT", u)
                        transposes(T0.tile, hh[:, u % 3, :], cuts[0:4]).then_inc(T0.full, 1)
                        wait("probs0", t)
                        for bank, what, cs in zip((T1, T0, T1), ("pa", "pb", "pc"), trio):
                            free(bank, what, u)
                            transposes(bank.tile, pr[:, u % 3, :], cs).then_inc(bank.full, 1)
                    elif k == "F0":
                        free(O, "bias", u)
                        pe.matmul(O.tile[:, 0:D], ohT[:, t, :], W["b2"], start=True, stop=True).then_inc(O.full, 1)
                        drained(O, "hidden", u)
                        for n, bank, what in ((0, T0, "ya"), (1, T1, "yb")):
                            free(bank, what, u)
                            for j in range(2):
                                last = pe.matmul(bank.tile[:, :], hid[:, u % 2, j, :],
                                                 W["w2"][:, j * E0 * D + n * 512:j * E0 * D + (n + 1) * 512],
                                                 start=(j == 0), stop=(j == 1))
                            last.then_inc(bank.full, 1)
                    elif k in ("A2", "A3"):
                        drained(O, "values", u)
                        free(X, "vT", u)
                        pe.transpose(X.tile[:, 0:P], cv[:, u % 2, :], ident).then_inc(X.full, 1)
                    elif k == "F2":
                        wait("weighted_F2a", t)
                        wait("weighted_F2b", t)
                        hc = [(n * P, (n + 1) * P) for n in range(9)]
                        for bank, what, cs in ((T0, "ha", hc[0:4]), (T1, "hb", hc[4:8]), (T0, "hc", hc[8:9])):
                            free(bank, what, u)
                            transposes(bank.tile, hh[:, u % 3, :], cs).then_inc(bank.full, 1)
                    elif k == "F3":
                        wait("dm_ready", t)
                        free(X, "downT", u)
                        pe.transpose(X.tile[0:R, 0:P], dm[:, t, :], ident).then_inc(X.full, 1)

                def middle(k, u, t):
                    if k == "A0":
                        pe.wait_ge(loaded["ff0"], 16)
                        for n, bank, what in ((1, T0, "gate"), (0, T1, "up")):
                            free(bank, what, u)
                            pe.matmul(bank.tile[:, :], xT[:, t, :], W["wff1"][:, n * FF0:(n + 1) * FF0],
                                      start=True, stop=True).then_inc(bank.full, 1)
                    elif k == "F0":
                        pe.wait_ge(loaded["top1"], 16)
                        drained(S, "masks", u)
                        free(O, "hidden", u)
                        for j in range(2):
                            for e in range(E0):
                                pe.matmul(O.tile[:, j * P:(j + 1) * P],
                                          W["w1"][:, e * H0 + j * P:e * H0 + (j + 1) * P],
                                          xm[:, u % 2, e, :], start=(e == 0), stop=False)
                            last = pe.matmul(O.tile[:, j * P:(j + 1) * P], W["b1"][:, j * P:(j + 1) * P],
                                             ohT[:, t, :], start=False, stop=True)
                        last.then_inc(O.full, 1)
                    elif k == "A1":
                        drained(S, "scores", u)
                        free(T0, "pT", u)
                        pe.transpose(T0.tile[0:CTX, 0:P], pr[:, u % 3, 0:CTX], ident).then_inc(T0.full, 1)
                    elif k == "F1":
                        wait("hq_ready", t)
                        free(T0, "hT", u)
                        for n in range(4):
                            last = pe.transpose(T0.tile[:, n * 64:(n + 1) * 64].bitcast(BF16),
                                                hq[:, u % 2, n * P:(n + 1) * P], ident_b[:, :])
                        last.then_inc(T0.full, 1)
                    elif k in ("A2", "A3"):
                        wait("probs_" + k, t)
                        for bank, what, cs in zip((T0, T1, T0), ("pa", "pb", "pc"), trio):
                            free(bank, what, u)
                            transposes(bank.tile, pr[:, u % 3, :], cs).then_inc(bank.full, 1)
                    elif k == "F2":
                        for c, bank, what in ((2, T0, "gate"), (5, T1, "up")):
                            free(bank, what, u)
                            pe.matmul(bank.tile[:, 0:GW], xT[:, t, :], W["w13"][:, c * GW:(c + 1) * GW],
                                      start=True, stop=True).then_inc(bank.full, 1)
                    elif k == "F3":
                        drained(X, "projT", u)
                        pe.wait_ge(s_prel, 4)
                        free(X, "logits", u)
                        pe.matmul(X.tile[:, 0:4 + R], pjT[:, u % 2, :], sim_n[:, :], start=True, stop=True)\
                          .then_inc(X.full, 1)

                def extra(k, u, t):
                    if k == "F0":
                        wait("pick_ready", t)
                        free(X, "pickT", u)
                        pe.transpose(X.tile[0:E0, 0:P], oh[:, t, 0:E0], ident).then_inc(X.full, 1)
                    elif k == "F1":
                        pe.wait_ge(s_quant, 1)
                        drained(X, "xT", u)
                        for n, bank, what in ((0, T0, "gate"), (1, T1, "up")):
                            free(bank, what, u)
                            pe.matmul(bank.tile[:, :], xTq[:, t, :], wt_q[:, n * FB:(n + 1) * FB],
                                      start=True, stop=True).then_inc(bank.full, 1)
                    elif k == "F3":
                        wait("pj_ready", t)
                        free(X, "projT", u)
                        pe.transpose(X.tile[0:PROJ, 0:P], pj[:, t, :], ident).then_inc(X.full, 1)

                def project(k, u, t):
                    if k == "F0":
                        pe.wait_ge(loaded["top1"], 16)
                        drained(X, "xT", u)
                        free(X, "logits", u)
                        pe.matmul(X.tile[:, 0:E0], xT[:, t, :], W["wr"], start=True, stop=True).then_inc(X.full, 1)
                    elif k in ("A2", "A3"):
                        drained(X, "xT", u)
                        free(X, "q", u)
                        pe.matmul(X.tile[:, 0:P], W["wq2" if k == "A2" else "wq3"], xT[:, t, :],
                                  start=True, stop=True).then_inc(X.full, 1)
                    elif k == "F2":
                        pe.wait_ge(loaded["top4"], 16)
                        drained(X, "xT", u)
                        free(X, "gate", u)
                        pe.matmul(X.tile[:, 0:E2], xT[:, t, :], W["wg"], start=True, stop=True).then_inc(X.full, 1)

                def output(k, u, t):
                    if k == "A0":
                        free(O, "out", u)
                        drained(T0, "hT", u)
                        for n in range(4):
                            pe.matmul(O.tile[:, 0:D], hT[:, u % 2, n, :], W["wff2"][:, n * D:(n + 1) * D],
                                      start=(n == 0), stop=False)
                        drained(T0, "pb", u)
                        drained(T1, "pc", u)
                        for n, (lo, hi) in enumerate(cuts):
                            last = pe.matmul(O.tile[:, 0:D], pT[0:hi - lo, u % 2, n, :], B0[0:hi - lo, n, :],
                                             start=False, stop=(n == NCH - 1))
                        last.then_inc(O.full, 1)
                    elif k in ("A2", "A3"):
                        drained(X, "vT", u)
                        free(O, "out", u)
                        last = pe.matmul(O.tile[:, 0:D], cvT[:, u % 2, :], W["wo2" if k == "A2" else "wo3"],
                                         start=True, stop=(k == "A3"))
                        if k == "A2":
                            last = pe.matmul(O.tile[:, 0:D], ones[0:1, :], W["bo2"], start=False, stop=True)
                        last.then_inc(O.full, 1)
                    elif k == "F2":
                        free(O, "out", u)
                        drained(T1, "hb", u)
                        drained(T0, "hc", u)
                        for n in range(9):
                            last = pe.matmul(O.tile[:, 0:D], hT[:, u % 2, n, :], W["w2s"][:, n * D:(n + 1) * D],
                                             start=(n == 0), stop=(n == 8))
                        last.then_inc(O.full, 1)
                    elif k == "F3":
                        drained(X, "downT", u)
                        free(O, "out", u)
                        pe.matmul(O.tile[:, 0:D], dmT[:, u % 2, :], W["wu"], start=True, stop=True).then_inc(O.full, 1)

                def values(k, u, t):
                    if k == "A1":
                        drained(T0, "pT", u)
                        free(O, "out", u)
                        pe.matmul(O.tile[:, 0:D], pT[0:CTX, u % 2, 0, :], ctx[:, :], start=True, stop=True)\
                          .then_inc(O.full, 1)
                    elif k == "F1":
                        drained(T0, "hT", u)
                        free(O, "out", u)
                        for n in range(4):
                            last = pe.matmul(O.tile[:, 0:D], hqT[:, u % 2, n, :],
                                             wt_q[:, 2 * FB + n * D:2 * FB + (n + 1) * D],
                                             start=(n == 0), stop=(n == 3))
                        last.then_inc(O.full, 1)
                    elif k in ("A2", "A3"):
                        V = V2 if k == "A2" else V3
                        drained(T1, "pb", u)
                        drained(T0, "pc", u)
                        free(O, "values", u)
                        for n, (lo, hi) in enumerate(cuts):
                            h0, h1 = lo // CTX, -(-hi // CTX)
                            last = pe.matmul(O.tile[:, h0 * VW:h1 * VW], pT[0:hi - lo, u % 2, n, :],
                                             V[0:hi - lo, n, h0:h1, :].rearrange("p h v -> p (h v)"),
                                             start=(n == 0), stop=(n == NCH - 1), skip_group_check=True)
                        last.then_inc(O.full, 1)

                def spread(k, u, t):
                    if k == "F0":
                        drained(X, "pickT", u)
                        free(S, "masks", u)
                        for e in range(E0):
                            last = pe.matmul(S.tile[:, e // 4, e % 4 * P:(e % 4 + 1) * P], pick_row[:, e, :],
                                             ohTb[:, u % 2, :], start=True, stop=True)
                        last.then_inc(S.full, 1)

                parts = dict(first=first, late_transpose=late_transpose, xT=xT_, middle=middle, extra=extra,
                             project=project, output=output, values=values, spread=spread)
                for part, u in steps():
                    parts[part](UNITS[u][0], u, UNITS[u][1])

        @block.scalar
        def _(act):
            Copy, Exp, Tanh, Relu, Ident = ACT.Copy, ACT.Exp, ACT.Tanh, ACT.Relu, ACT.Identity
            act.sem_inc(X.drained, 1)
            act.sem_inc(T0.drained, 1)
            act.sem_inc(T1.drained, 1)
            act.wait_ge(loaded["base"], 16)
            act.activation(tg[:, :], W["gates"], Tanh).then_inc(s_tg, 1)
            act.wait_ge(s_prel, 3)
            act.activation(sim_s[:, :], sim_s[:, :], Exp).then_inc(s_temp, 1)
            act.wait_ge(loaded["att23"], 16)

            with act.Fori(0, B) as it:
                full, free, drained, wait = helpers(act, it)

                def evac4(bank, what, u, dst):
                    full(bank, what, u)
                    act.activation(dst, bank.tile[:, 0:dst.free_size()], Copy).then_inc(bank.drained, 1)

                full(X, "cT")
                act.activation(ctxnT[:, :], X.tile[:, 0:CTX], Copy, scale=W["ln_gamma"][:, 1:2]).then_inc(X.drained, 1)
                full(X, "kv")
                act.activation(k2[:, :], X.tile[:, 0:CTX], Ident, bias=W["b2qkv"][:, 1:2])
                act.activation(v2[:, :], X.tile[:, P:P + CTX], Ident, bias=W["b2qkv"][:, 2:3])
                act.activation(k3[:, :], X.tile[:, 2 * P:2 * P + CTX], Copy).then_inc(X.drained, 1)
                full(X, "kv0")
                act.wait_ge(s_const, 9)
                wait("ctx_used", 0)
                for g in range(2):
                    rows = slice(g * DH0, (g + 1) * DH0)
                    act.activation(k0[rows, g, :], X.tile[rows, 0:CTX], Copy, scale=float(DH0) ** -0.5)
                    last = act.activation(v0[rows, g, :], X.tile[rows, P:P + CTX], Copy, scale=anyseen[rows, 2:3])
                last.then_inc(X.drained, 1)
                full(S, "a")
                act.activation(A0[:, :].rearrange("p (b n) -> p b n", b=4), S.tile[:, :, 0:SB], Copy)\
                   .then_inc(S.drained, 1)
                groups = ((0, 4), (4, 8), (8, NCH))
                for bank, what, (lo, hi) in zip((T0, T1, T0), ("ba", "bb", "bc"), groups):
                    full(bank, what)
                    act.activation(B0[:, lo:hi, :], bank.tile[:, 0:(hi - lo) * P].rearrange("p (n d) -> p n d", d=P),
                                   Copy).then_inc(bank.drained, 1)
                for V, names in ((V2, ("va", "vb", "vc")), (V3, ("ka", "kb", "kc"))):
                    for bank, what, (lo, hi) in zip((T0, T1, T0), names, groups):
                        full(bank, what)
                        src = bank.tile[:, 0:(hi - lo) * P].rearrange("p (n h v) -> p n h v", h=H, v=DH)
                        for n in range(lo, hi):
                            last = act.activation(V[:, n, :, 0:DH], src[:, n - lo, :, :], Copy)
                        last.then_inc(bank.drained, 1)

                def evac_probs(bank, what, u, t, lo, hi):
                    full(bank, what, u)
                    act.activation(pT[:, u % 2, lo:hi, :], bank.tile[:, 0:(hi - lo) * P].rearrange("p (n d) -> p n d", d=P),
                                   Copy).then_inc(bank.drained, 1)

                def phase3(k, u, t):
                    if k == "A0":
                        full(T0, "hT", u)
                        act.activation(hT[:, u % 2, 0:4, :], T0.tile[:, :].rearrange("p (n d) -> p n d", d=P), Copy)\
                           .then_inc(T0.drained, 1)
                        for bank, what, (lo, hi) in zip((T1, T0, T1), ("pa", "pb", "pc"), groups):
                            evac_probs(bank, what, u, t, lo, hi)
                    elif k in ("A2", "A3"):
                        full(X, "vT", u)
                        act.activation(cvT[:, u % 2, :], X.tile[:, 0:P], Copy).then_inc(X.drained, 1)
                    elif k == "F2":
                        for bank, what, lo, hi in ((T0, "ha", 0, 4), (T1, "hb", 4, 8), (T0, "hc", 8, 9)):
                            full(bank, what, u)
                            act.activation(hT[:, u % 2, lo:hi, :],
                                           bank.tile[:, 0:(hi - lo) * P].rearrange("p (n d) -> p n d", d=P), Copy)\
                               .then_inc(bank.drained, 1)
                    elif k == "F3":
                        full(X, "downT", u)
                        act.activation(dmT[:, u % 2, :], X.tile[0:R, 0:P], Copy).then_inc(X.drained, 1)

                def phase0(k, u, t):
                    full(X, "xT", u)
                    if k == "A0":
                        act.activation(xT[:, t, :], X.tile[:, 0:P], Copy, scale=W["ln_gamma"][:, 0:1])\
                           .then_inc(X.drained, 1)
                    elif k == "F1":
                        act.activation(xTq[:, t, :], X.tile[:, 0:P // 2].bitcast(BF16), Copy).then_inc(X.drained, 1)
                    else:
                        act.activation(xT[:, t, :], X.tile[:, 0:P], Copy).then_inc(X.drained, 1)

                def phase2(k, u, t):
                    if k == "A0":
                        full(T0, "gate", u)
                        inc(act.activation(th[:, u % 2, 0:FF0], T0.tile[:, :], Tanh, scale=0.5), "tanh_A0")
                    elif k == "F0":
                        full(O, "hidden", u)
                        act.activation(hid[:, u % 2, :, :], O.tile[:, 0:2 * P].rearrange("p (j n) -> p j n", j=2), Relu)\
                           .then_inc(O.drained, 1)
                    elif k == "A1":
                        full(T0, "pT", u)
                        act.activation(pT[0:CTX, u % 2, 0, :], T0.tile[0:CTX, 0:P], Copy).then_inc(T0.drained, 1)
                    elif k == "F1":
                        full(T0, "hT", u)
                        act.activation(hqT[:, u % 2, :, :], T0.tile[:, 0:256].bitcast(BF16).rearrange("p (n d) -> p n d", d=P),
                                       Copy).then_inc(T0.drained, 1)
                    elif k in ("A2", "A3"):
                        for bank, what, (lo, hi) in zip((T0, T1, T0), ("pa", "pb", "pc"), groups):
                            evac_probs(bank, what, u, t, lo, hi)
                    elif k == "F2":
                        full(T0, "gate", u)
                        inc(act.activation(th[:, u % 2, 2 * GW:3 * GW], T0.tile[:, 0:GW], Tanh, scale=0.5), "tanh_F2b")

                def phase1_extra(k, u, t):
                    if k == "F0":
                        full(X, "pickT", u)
                        act.activation(ohT[:, t, :], X.tile[0:E0, 0:P], Copy)
                        act.activation(ohTb[:, u % 2, :], X.tile[0:E0, 0:P], Copy).then_inc(X.drained, 1)
                    elif k == "F1":
                        full(T0, "gate", u)
                        inc(act.activation(th[:, u % 2, 0:FB], T0.tile[:, :], Tanh, scale=sc[:, t, 3:4]), "tanh_F1")
                    elif k == "F3":
                        full(X, "projT", u)
                        act.activation(pjT[:, u % 2, :], X.tile[0:PROJ, 0:P], Copy).then_inc(X.drained, 1)

                def phase0_project(k, u, t):
                    if k == "A2":
                        full(X, "q", u)
                        act.wait_ge(s_tg, 2)
                        act.activation(qT[:, u % 2, :], X.tile[:, 0:P], Ident, bias=sq2[:, :], scale=float(DH) ** -0.5)\
                           .then_inc(X.drained, 1)
                    elif k == "A3":
                        full(X, "q", u)
                        act.activation(qT[:, u % 2, :], X.tile[:, 0:P], Copy, scale=float(DH) ** -0.5)\
                           .then_inc(X.drained, 1)
                    elif k == "F2":
                        full(X, "gate", u)
                        act.activation(sg[:, t, :], X.tile[:, 0:E2], Tanh, scale=0.5).then_inc(X.drained, 1)

                def phase1(k, u, t):
                    if k in ("A0", "A2", "A3"):
                        drained(S, "scores", u)
                        inc(act.activation(pr[:, u % 3, :], pr[:, u % 3, :], Exp), "probs_" + k)
                    elif k == "A1":
                        wait("nmax_A1", t)
                        act.activation(pr[:, u % 3, 0:CTX], S.tile[:, 0, 0:CTX], Exp, bias=sc[:, t, 0:1],
                                       accum_out=sc[:, t, 1:2]).then_inc(S.drained, 1)
                    elif k == "F0":
                        wait("centred_F0", t)
                        inc(act.activation(ex[:, t, :], lg[:, t, 0:E0], Exp, accum_out=sc[:, t, 1:2]), "expsum_F0")
                    elif k == "F2":
                        full(S, "gu", u)
                        inc(act.activation(th[:, u % 2, 0:2 * GW].rearrange("p (b n) -> p b n", b=2),
                                           S.tile[:, 0:2, 0:GW], Tanh, scale=0.5), "tanh_F2a")

                def phase2_end(k, u, t):
                    if k == "F3":
                        wait("centred_F3", t)
                        inc(act.activation(ex[:, t, 0:4], lg[:, t, 0:4], Exp, accum_out=sc[:, t, 1:2]), "expsum_F3")

                for s in range(U + 3):
                    for work, phase in ((phase3, 3), (phase0, 0), (phase2, 2), (phase1_extra, 1),
                                        (phase0_project, 0), (phase1, 1), (phase2_end, 2)):
                        if 0 <= s - phase < U:
                            work(UNITS[s - phase][0], s - phase, UNITS[s - phase][1])

        @block.gpsimd
        def _(pool):
            def carry():
                pool.sem_inc(s_carry, 1)

            pool.memset(half[:, :], -0.5).then_inc(s_const, 1)
            pool.wait_ge(loaded["base"], 16)
            for V in (V2, V3):
                pool.tensor_copy(V[:, :, :, DH:VW].rearrange("p n h o -> p n (h o)"),
                                 W["ones_col"].rearrange("p (n h) -> p n h", h=H)).then_inc(s_const, 1)
            pool.wait_ge(s_const, 9)
            pool.wait_ge(X.drained, 3)
            pool.tensor_tensor(sim_sq[:, :], sim_sq[:, :], half[0:PROJ, 0:1].broadcast_to([PROJ, 4 + R]), ALU.pow)\
                .then_inc(s_simpow, 1)
            with pool.Fori(0, B) as it:
                full, free, drained, wait = helpers(pool, it)
                wait("var_ready", 0)
                inc(pool.tensor_tensor(crs[:, :], cve[:, :], half[0:CTX, 0:1], ALU.pow), "rstd_ready")
                pool.wait_ge(s_c_loaded, (it + 1) * 48)
                carry()
                pool.tensor_copy(ctx[:, :], ctx_st[:, :])
                inc(pool.tensor_copy(ctxT[:, :], ctxT_st[:, :]), "x_copied")
                pool.wait_ge(s_x_loaded, (it + 1) * 16)
                carry()
                inc(pool.tensor_copy(x[:, :, :], x_st[:, :, :]), "x_copied")
                drained(X, "kv")
                delta = W["delta"].unsqueeze(2).broadcast_to([P, H, CTX])
                for dst, src in ((K2[:, :, :], k2), (V2x, v2), (K3[:, :, :], k3)):
                    inc(pool.tensor_tensor(dst, src[:, :].unsqueeze(1).broadcast_to([P, H, CTX]), delta,
                                           ALU.mult), "expanded")

                def phase0(k, u, t):
                    wait("var_ready", u + 1)
                    inc(pool.tensor_tensor(rstd[:, t:t + 1], ve[:, t:t + 1], half[:, 0:1], ALU.pow), "rstd_ready")

                def weigh(u, t, e0, e1):
                    h = hh[:, u % 3, e0 * F2W:e1 * F2W].rearrange("p (e f) -> p e f", f=F2W)
                    return pool.tensor_tensor(h, h, comb[:, t, e0:e1].unsqueeze(2).broadcast_to([P, e1 - e0, F2W]),
                                              ALU.mult)

                def phase1(k, u, t):
                    if k == "F3":
                        wait("ss_ready", t)
                        inc(pool.tensor_tensor(sc[:, t, 5:6], sc[:, t, 4:5], half[:, 0:1], ALU.pow), "rn_ready")
                    elif k == "F2":
                        drained(S, "gu", u)
                        wait("comb_ready", t)
                        inc(weigh(u, t, 0, 12), "weighted_F2a")

                def phase2(k, u, t):
                    if k == "A0":
                        wait("inv0", t)
                        p = pr[:, u % 3, :].rearrange("p (h c) -> p h c", c=CTX)
                        inc(pool.tensor_tensor(p, p, ri[:, t, :].unsqueeze(2).broadcast_to([P, H, CTX]), ALU.mult),
                            "probs0")
                    elif k == "F2":
                        drained(T1, "up", u)
                        inc(weigh(u, t, 12, E2), "weighted_F2b")

                for s in range(U + 3):
                    for work, phase in ((phase0, 0), (phase1, 1), (phase2, 2)):
                        if 0 <= s - phase < U:
                            work(UNITS[s - phase][0], s - phase, UNITS[s - phase][1])

        @block.vector
        def _(dve):
            steps_done = [0]

            def link(ins):
                steps_done[0] += 1
                ins.then_inc(s_dve, 1)
                dve.wait_ge(s_dve, at[0] * DVE_STEPS + (BEFORE_LOOP[0] + steps_done[0]) if at else steps_done[0])

            def carry():
                dve.sem_inc(s_carry, 1)

            at, BEFORE_LOOP = [], [0]
            tanh_gate = {k: tg[:, GATE[k]:GATE[k] + 1] for k in BLOCKS}
            for bank in (S, O):
                dve.sem_inc(bank.drained, 1)
            dve.memset(ones[:, :], 1.0).then_inc(s_const, 1)
            dve.memset(ones_b[:, :], 1.0).then_inc(s_const, 1)
            dve.memset(k0[:, :, :], 0.0).then_inc(s_const, 1)
            dve.memset(v0[:, :, :], 0.0).then_inc(s_const, 1)
            dve.wait_ge(loaded["base"], 16)
            dve.tensor_copy(ident_b[:, :], ident).then_inc(s_const, 1)
            dve.tensor_copy(pick_row[:, :, :], W["ident"][0:E0, 0:E0].unsqueeze(2).broadcast_to([E0, E0, P]))\
               .then_inc(s_const, 1)
            dve.wait_ge(loaded["tern"], 16)
            dve.tensor_reduce(wt_sum[:, :], W["wt"].rearrange("p (w n) -> p w n", w=3), AX.X, ALU.add,
                              apply_absolute_value=True).then_inc(s_prel, 1)
            dve.wait_ge(loaded["low"], 16)
            dve.tensor_tensor(sim_sq[:, :], W["sim"], W["sim"], ALU.mult).then_inc(s_prel, 1)
            dve.tensor_scalar(sim_s[:, :], W["temp"], CLAMP, None, ALU.min).then_inc(s_prel, 1)
            dve.wait_ge(X.full, 1)
            dve.tensor_scalar(wt_mean[:, :], X.tile[:, 0:3], 1.0 / (FB * D), 1e-5, ALU.mult, ALU.max)\
               .then_inc(X.drained, 1)
            dve.wait_ge(X.drained, 2)
            link(dve.reciprocal(wt_inv[:, :], wt_mean[:, :]))
            for n in range(3):
                cols = slice(n * FB, (n + 1) * FB)
                last = dve.tensor_scalar(wt_r[:, cols], W["wt"][:, cols], wt_inv[:, n:n + 1], MAGIC, ALU.mult, ALU.add)
            link(last)
            link(dve.tensor_scalar(wt_r, wt_r, -MAGIC, 1.0, ALU.add, ALU.min))
            dve.tensor_scalar(wt_q[:, :], wt_r, -1.0, None, ALU.max).then_inc(s_quant, 1)
            dve.wait_ge(s_tg, 1)
            dve.tensor_scalar(tgh[:, :], tanh_gate.get("F2", tg[:, 6:7]), 0.5, None, ALU.mult)
            dve.tensor_scalar(wt_c[:, 0:1], wt_mean[:, 0:1], 0.5 / 127.0, None, ALU.mult)
            dve.tensor_scalar(wt_c[:, 1:2], wt_mean[:, 0:1], wt_mean[:, 1:2], 0.5 / 127.0 ** 2, ALU.mult, ALU.mult)
            dve.tensor_scalar(wt_c[:, 2:3], wt_mean[:, 2:3], tg[:, 5:6], 1.0 / 127.0, ALU.mult, ALU.mult)
            dve.wait_ge(loaded["att23"], 16)
            dve.tensor_scalar(sq2[:, :], W["b2qkv"][:, 0:1], float(DH) ** -0.5, None, ALU.mult).then_inc(s_tg, 1)
            dve.wait_ge(X.full, 2)
            dve.tensor_scalar(sim_sq[:, :], X.tile[0:PROJ, 0:4 + R], 1e-24, None, ALU.max).then_inc(X.drained, 1)
            dve.wait_ge(s_simpow, 1)
            link(dve.tensor_tensor(sim_n[:, :], W["sim"], sim_sq[:, :], ALU.mult))
            dve.wait_ge(s_temp, 1)
            dve.tensor_scalar(sim_n[:, :], sim_n[:, :], sim_s[:, 0:1], None, ALU.mult).then_inc(s_prel, 1)
            dve.wait_ge(s_prel, 4)
            dve.wait_ge(s_const, 9)
            BEFORE_LOOP[0], steps_done[0] = steps_done[0], 0

            with dve.Fori(0, B) as it:
                at.append(it)
                full, free, drained, wait = helpers(dve, it)

                dve.wait_ge(s_c_loaded, (it + 1) * 48)
                link(dve.bn_stats(cstat[:, :], ctx_st[:, :]))
                carry()
                link(dve.bn_aggr(cmv[:, :], cstat[:, :]))
                inc(dve.tensor_scalar(cve[:, :], cmv[:, 1:2], LN_EPS, None, ALU.add), "var_ready")
                link(dve.tensor_scalar(seen[:, :], mask_st[:, :], 0.0, None, ALU.not_equal))
                link(dve.tensor_reduce(anyseen[:, 0:1], seen[:, :], AX.X, ALU.max))
                link(dve.reciprocal(anyseen[:, 1:2], anyseen[:, 0:1]))
                inc(dve.tensor_scalar(mask_row[:, :, :], mask_st[0:1, :].unsqueeze(1).broadcast_to([1, HB, CTX]),
                                      0.0, MASKED, ALU.is_equal, ALU.mult), "mask_ready")
                wait("rstd_ready", 0)
                inc(dve.tensor_scalar(ctxn[:, :], ctx_st[:, :], cmv[:, 0:1], crs[:, 0:1], ALU.subtract, ALU.mult),
                    "xh_ready")
                inc(dve.tensor_tensor(anyseen[:, 2:3], anyseen[:, 0:1], anyseen[:, 1:2], ALU.mult), "ctx_used")
                full(S, "b")
                dve.tensor_copy(B0T.rearrange("p (b n) -> p b n", b=4), S.tile[:, :, 0:SB]).then_inc(S.drained, 1)

                def phase0_stats(k, u, t):
                    if u == 0:
                        wait("x_copied", 1)
                    link(dve.bn_stats(stat[:, :], x[:, t, :]))
                    carry()
                    link(dve.bn_aggr(mv[:, t, :], stat[:, :]))
                    a, b_ = (1.0 + LN_EPS, LN_EPS * LN_EPS) if k == "A0" else (1.0, LN_EPS)
                    inc(dve.tensor_scalar(ve[:, t:t + 1], mv[:, t, 1:2], a, b_, ALU.mult, ALU.add), "var_ready")

                def phase0_norm(k, u, t):
                    wait("rstd_ready", u + 1)
                    norm = dve.tensor_scalar(xh[:, t, :], x[:, t, :], mv[:, t, 0:1], rstd[:, t:t + 1],
                                             ALU.subtract, ALU.mult)
                    if k != "F1":
                        inc(norm, "xh_ready")
                        return
                    link(norm)
                    link(dve.tensor_reduce(sc[:, t, 4:5], xh[:, t, :], AX.X, ALU.max, apply_absolute_value=True))
                    link(dve.tensor_scalar(sc[:, t, 4:5], sc[:, t, 4:5], 1e-5, None, ALU.max))
                    link(dve.reciprocal(sc[:, t, 5:6], sc[:, t, 4:5]))
                    link(dve.tensor_scalar(sc[:, t, 5:6], sc[:, t, 5:6], 127.0, None, ALU.mult))
                    dve.tensor_scalar(sc[:, t, 3:4], sc[:, t, 4:5], wt_c[:, 0:1], None, ALU.mult)
                    dve.tensor_scalar(sc[:, t, 6:7], sc[:, t, 4:5], sc[:, t, 4:5], wt_c[:, 1:2], ALU.mult, ALU.mult)
                    link(dve.tensor_scalar(xhq[:, u % 2, :], xh[:, t, :], sc[:, t, 5:6], MAGIC, ALU.mult, ALU.add))
                    inc(dve.tensor_scalar(xq[:, t, :], xhq[:, u % 2, :], -MAGIC, 127.0, ALU.add, ALU.min), "xh_ready")

                def residual(k, t, src, scale):
                    return dve.scalar_tensor_tensor(out=x[:, t, :], in0=src, scalar=scale, in1=x[:, t, :],
                                                    op0=ALU.mult, op1=ALU.add)

                def inverse_sum(k, t):
                    link(dve.reciprocal(sc[:, t, 2:3], sc[:, t, 1:2]))
                    link(dve.tensor_scalar(sc[:, t, 3:4], sc[:, t, 2:3], tanh_gate[k], None, ALU.mult))

                def store(k, u, t):
                    if k == BLOCKS[-1]:
                        if t == 0:
                            dve.wait_ge(s_stored, (it + 1) * (16 * TILES))
                        inc(dve.tensor_copy(y[:, t, :], x[:, t, :]), "y_ready")

                def phase3_early(k, u, t):
                    if k == "F0":
                        wait("expsum_F0", t)
                        inverse_sum(k, t)
                        link(dve.tensor_scalar(ri[:, t, 0:E0], oh[:, t, 0:E0], sc[:, t, 3:4], None, ALU.mult))
                        full(O, "bias", u)
                        residual(k, t, O.tile[:, 0:D], sc[:, t, 3:4]).then_inc(O.drained, 1)
                    elif k == "A1":
                        drained(S, "scores", u)
                        inverse_sum(k, t)
                        full(O, "out", u)
                        residual(k, t, O.tile[:, 0:D], sc[:, t, 3:4]).then_inc(O.drained, 1)
                        drained(O, "out", u)
                        store(k, u, t)
                    elif k == "F1":
                        full(O, "out", u)
                        residual(k, t, O.tile[:, 0:D], sc[:, t, 7:8]).then_inc(O.drained, 1)
                        drained(O, "out", u)
                        store(k, u, t)
                    elif k in ("A2", "A3"):
                        full(O, "values", u)
                        o = O.tile[:, 0:H * VW].rearrange("p (h v) -> p h v", v=VW)
                        link(dve.reciprocal(ri[:, t, :], o[:, :, DH:VW].rearrange("p h o -> p (h o)")))
                        dve.tensor_tensor(cv[:, u % 2, :].rearrange("p (h v) -> p h v", v=DH), o[:, :, 0:DH],
                                          ri[:, t, :].unsqueeze(2).broadcast_to([P, H, DH]), ALU.mult)\
                           .then_inc(O.drained, 1)

                def phase1(k, u, t):
                    if k in ("A0", "A2", "A3"):
                        full(S, "scores", u)
                        s4 = S.tile[:, :, 0:SB].rearrange("p b (h c) -> p b h c", c=CTX)
                        link(dve.tensor_reduce(mx[:, t, :].rearrange("p (b h) -> p b h", b=4), s4, AX.X, ALU.max))
                        m4 = mx[:, t, :].rearrange("p (b h) -> p b h", b=4).unsqueeze(3)
                        dve.tensor_tensor(pr[:, u % 3, :].rearrange("p (b h c) -> p b h c", b=4, c=CTX), s4,
                                          m4.broadcast_to([P, 4, HB, CTX]), ALU.subtract).then_inc(S.drained, 1)
                    elif k == "A1":
                        full(S, "scores", u)
                        inc(dve.tensor_reduce(sc[:, t, 0:1], S.tile[:, 0, 0:CTX], AX.X, ALU.max, negate=True),
                            "nmax_A1")
                    elif k == "F0":
                        full(X, "logits", u)
                        dve.tensor_tensor(lg[:, t, 0:E0], X.tile[:, 0:E0], W["br"], ALU.add).then_inc(X.drained, 1)
                        drained(X, "logits", u)
                        link(dve.tensor_reduce(sc[:, t, 0:1], lg[:, t, 0:E0], AX.X, ALU.max, negate=True))
                        inc(dve.tensor_scalar(lg[:, t, 0:E0], lg[:, t, 0:E0], sc[:, t, 0:1], None, ALU.add),
                            "centred_F0")
                        wait("centred_F0", t)
                        link(dve.scalar_tensor_tensor(out=tt[:, t, 0:E0], in0=lg[:, t, 0:E0], scalar=0.0,
                                                      in1=W["desc0"], op0=ALU.is_ge, op1=ALU.mult))
                        link(dve.tensor_reduce(sc[:, t, 5:6], tt[:, t, 0:E0], AX.X, ALU.max))
                        inc(dve.tensor_scalar(oh[:, t, 0:E0], tt[:, t, 0:E0], sc[:, t, 5:6], None, ALU.is_equal),
                            "pick_ready")
                    elif k == "F2":
                        wait("tanh_F2a", t)
                        def two(a, n):
                            return a[:, u % n, 0:2 * GW].rearrange("p (b n) -> p b n", b=2)

                        link(dve.scalar_tensor_tensor(out=two(g1, 2), in0=two(th, 2), scalar=1.0, in1=S.tile[:, 0:2, 0:GW],
                                                      op0=ALU.add, op1=ALU.mult))
                        dve.tensor_tensor(two(hh, 3), two(g1, 2), S.tile[:, 2:4, 0:GW], ALU.mult).then_inc(S.drained, 1)
                        route(u, t)
                    elif k == "F3":
                        full(S, "all", u)
                        inc(dve.tensor_tensor(pj[:, t, :], S.tile[:, 0, 0:PROJ], W["bp"], ALU.add), "pj_ready")
                        dve.tensor_copy(dn[:, t, :], S.tile[:, 0, PROJ:PROJ + R])
                        residual(k, t, S.tile[:, 0, PROJ + R:PROJ + R + D], tanh_gate[k]).then_inc(S.drained, 1)
                        wait("pj_ready", t)
                        link(dve.tensor_tensor(pj2[:, :], pj[:, t, :], pj[:, t, :], ALU.mult))
                        link(dve.tensor_reduce(sc[:, t, 4:5], pj2[:, :], AX.X, ALU.add))
                        inc(dve.tensor_scalar(sc[:, t, 4:5], sc[:, t, 4:5], 1e-24, None, ALU.max), "ss_ready")

                def ranks(rank, work, v, n, tri):
                    vj = v.unsqueeze(1).broadcast_to([P, n, n])
                    vi = v.unsqueeze(2).broadcast_to([P, n, n])
                    dve.tensor_tensor(work[:, :, 0, :], vj, vi, ALU.is_gt)
                    link(dve.tensor_tensor(work[:, :, 1, :], vj, vi, ALU.is_equal))
                    link(dve.tensor_tensor(work[:, :, 1, :], work[:, :, 1, :],
                                           tri.rearrange("p (i j) -> p i j", i=n), ALU.mult))
                    link(dve.tensor_reduce(rank, work[:, :, :, :], AX.XY, ALU.add))

                def route(u, t):
                    drained(X, "gate", u)
                    link(dve.tensor_scalar(sig[:, t, :], sg[:, t, :], 0.5, 0.5, ALU.mult, ALU.add))
                    s4 = sig[:, t, :].rearrange("p (g e) -> p g e", g=4)
                    dve.tensor_tensor(pairs[:, :, 0:3], s4[:, :, 0:3], s4[:, :, 1:4], ALU.add)
                    dve.tensor_tensor(pairs[:, :, 3:5], s4[:, :, 0:2], s4[:, :, 2:4], ALU.add)
                    link(dve.tensor_tensor(pairs[:, :, 5:6], s4[:, :, 0:1], s4[:, :, 3:4], ALU.add))
                    link(dve.tensor_reduce(gs[:, :], pairs[:, :, :], AX.X, ALU.max))
                    ranks(rank4[:, :], cmp4, gs[:, :], 4, W["tri4"])
                    link(dve.tensor_scalar(allow[:, :], rank4[:, :], 2.0, None, ALU.is_lt))
                    link(dve.tensor_scalar(allow1[:, :], allow[:, :], -1.0, None, ALU.add))
                    m4 = msk[:, :].rearrange("p (g e) -> p g e", g=4)
                    link(dve.tensor_tensor(m4, s4, allow[:, :].unsqueeze(2).broadcast_to([P, 4, 4]), ALU.mult))
                    link(dve.tensor_tensor(m4, m4, allow1[:, :].unsqueeze(2).broadcast_to([P, 4, 4]), ALU.add))
                    ranks(rank16[:, :], cmp16, msk[:, :], E2, W["tri16"])
                    link(dve.scalar_tensor_tensor(out=picked[:, :], in0=rank16[:, :], scalar=4.0, in1=sig[:, t, :],
                                                  op0=ALU.is_lt, op1=ALU.mult))
                    link(dve.tensor_reduce(psc[:, 0:1], picked[:, :], AX.X, ALU.add))
                    link(dve.tensor_scalar(psc[:, 1:2], psc[:, 0:1], 1e-6, None, ALU.add))
                    link(dve.reciprocal(psc[:, 2:3], psc[:, 1:2]))
                    inc(dve.tensor_scalar(comb[:, t, :], picked[:, :], psc[:, 2:3], None, ALU.mult), "comb_ready")

                def silu_times_up(k, u, t, cols, gate, up, factor):
                    n = gate.free_size()
                    dve.scalar_tensor_tensor(out=g1[:, u % 2, cols], in0=th[:, u % 2, cols], scalar=1.0, in1=gate,
                                             op0=ALU.add, op1=ALU.mult).then_inc(T0.drained, 1)
                    drained(T0, "gate", u)
                    full(T1, "up", u)
                    dve.scalar_tensor_tensor(out=hh[:, u % 3, cols], in0=g1[:, u % 2, cols], scalar=factor, in1=up,
                                             op0=ALU.mult, op1=ALU.mult).then_inc(T1.drained, 1)

                def phase2(k, u, t):
                    if k == "A0":
                        wait("probs_A0", t)
                        link(dve.tensor_reduce(rs[:, t, :], pr[:, u % 3, :].rearrange("p (h c) -> p h c", c=CTX),
                                               AX.X, ALU.add))
                        inc(dve.reciprocal(ri[:, t, :], rs[:, t, :]), "inv0")
                        wait("tanh_A0", t)
                        silu_times_up(k, u, t, slice(0, FF0), T0.tile[:, :], T1.tile[:, :], 0.5)
                    elif k == "F2":
                        wait("tanh_F2b", t)
                        silu_times_up(k, u, t, slice(2 * GW, 3 * GW), T0.tile[:, 0:GW], T1.tile[:, 0:GW], 1.0)
                    elif k == "F3":
                        full(X, "logits", u)
                        wait("rn_ready", t)
                        dve.tensor_scalar(lg[:, t, :], X.tile[:, 0:4 + R], sc[:, t, 5:6], None, ALU.mult)\
                           .then_inc(X.drained, 1)
                        drained(X, "logits", u)
                        link(dve.tensor_reduce(sc[:, t, 0:1], lg[:, t, 0:4], AX.X, ALU.max, negate=True))
                        inc(dve.tensor_scalar(lg[:, t, :], lg[:, t, :], sc[:, t, 0:1], None, ALU.add), "centred_F3")
                        wait("centred_F3", t)
                        link(dve.scalar_tensor_tensor(out=tt[:, t, :], in0=lg[:, t, :], scalar=0.0, in1=W["desc3"],
                                                      op0=ALU.is_ge, op1=ALU.mult))
                        link(dve.tensor_reduce(sc[:, t, 6:7], tt[:, t, 0:4], AX.X, ALU.max))
                        inc(dve.scalar_tensor_tensor(out=dm[:, t, :], in0=tt[:, t, 4:4 + R], scalar=sc[:, t, 6:7],
                                                     in1=dn[:, t, :], op0=ALU.is_equal, op1=ALU.mult), "dm_ready")

                def phase3(k, u, t):
                    if k == "F0":
                        drained(O, "bias", u)
                        for e in range(E0):
                            bank, what = (T0, "ya") if e < 4 else (T1, "yb")
                            if e % 4 == 0:
                                full(bank, what, u)
                            r = residual(k, t, bank.tile[:, e % 4 * D:(e % 4 + 1) * D], ri[:, t, e:e + 1])
                            if e % 4 == 3:
                                r.then_inc(bank.drained, 1)
                                drained(bank, what, u)
                            else:
                                link(r)
                        store(k, u, t)
                        return
                    if k in ("A1", "F1"):
                        return
                    scale = tgh[:, 0:1] if k == "F2" else tanh_gate[k]
                    if k == "F3":
                        wait("expsum_F3", t)
                        inverse_sum(k, t)
                        scale = sc[:, t, 3:4]
                    full(O, "out", u)
                    residual(k, t, O.tile[:, 0:D], scale).then_inc(O.drained, 1)
                    drained(O, "out", u)
                    store(k, u, t)

                def phase1_extra(k, u, t):
                    if k == "F1":
                        wait("tanh_F1", t)
                        silu_times_up(k, u, t, slice(0, FB), T0.tile[:, :], T1.tile[:, :], 1.0)
                        drained(T1, "up", u)
                        h = hh[:, u % 3, 0:FB]
                        link(dve.tensor_reduce(sc[:, t, 8:9], h, AX.X, ALU.max, apply_absolute_value=True))
                        link(dve.tensor_scalar(sc[:, t, 8:9], sc[:, t, 8:9], sc[:, t, 6:7], 1e-5, ALU.mult, ALU.max))
                        link(dve.reciprocal(sc[:, t, 9:10], sc[:, t, 8:9]))
                        link(dve.tensor_scalar(sc[:, t, 9:10], sc[:, t, 9:10], sc[:, t, 6:7], 127.0, ALU.mult, ALU.mult))
                        dve.tensor_scalar(sc[:, t, 7:8], sc[:, t, 8:9], wt_c[:, 2:3], None, ALU.mult)
                        link(dve.tensor_scalar(h, h, sc[:, t, 9:10], MAGIC, ALU.mult, ALU.add))
                        inc(dve.tensor_scalar(hq[:, u % 2, :], h, -MAGIC, 127.0, ALU.add, ALU.min), "hq_ready")

                def phase1_late(k, u, t):
                    if k == "F0":
                        full(S, "masks", u)
                        dve.tensor_tensor(xm[:, u % 2, :, :].rearrange("p (b e) n -> p b e n", b=2),
                                          S.tile[:, 0:2, :].rearrange("p b (e n) -> p b e n", n=P),
                                          xT[:, t, :].unsqueeze(1).unsqueeze(1).broadcast_to([P, 2, 4, P]), ALU.mult)\
                           .then_inc(S.drained, 1)

                for s in range(U + 3):
                    for work, phase in ((phase0_stats, 0), (phase3_early, 3), (phase0_norm, 0), (phase1, 1),
                                        (phase2, 2), (phase1_extra, 1), (phase3, 3), (phase1_late, 1)):
                        if 0 <= s - phase < U:
                            work(UNITS[s - phase][0], s - phase, UNITS[s - phase][1])
            assert steps_done[0] == DVE_STEPS, steps_done[0]


def _columns(a, rows=P):
    return np.broadcast_to(np.asarray(a).reshape(1, -1), (rows, a.size))


def _pack(parts, given):
    out = np.zeros((P, sum(c for _, _, c in parts)), np.float32)
    at = 0
    for name, rows, cols in parts:
        out[0:rows, at:at + cols] = np.asarray(given[name]).reshape(rows, cols)
        at += cols
    return out


def kernel(**inputs):
    import concourse.bacc as _bacc
    from concourse.bass_utils import run_bass_kernel_spmd as _run

    a = {k: np.asarray(v) for k, v in inputs.items()}
    g = {}
    rows = np.arange(NCH * P)
    g["ident"] = np.eye(P)
    g["delta"] = np.arange(P)[:, None] // DH == np.arange(H)[None, :]
    g["ones_col"] = (rows.reshape(NCH, P, 1) // CTX == np.arange(H)).transpose(1, 0, 2)
    g["desc0"] = _columns(np.arange(E0, 0, -1))
    expert = [e for e, r in enumerate(RANKS) for _ in range(r)]
    cols3 = list(range(4)) + expert
    g["desc3"] = _columns(4 - np.array(cols3))
    g["tri4"] = _columns(np.tril(np.ones((4, 4)), -1))
    g["tri16"] = _columns(np.tril(np.ones((E2, E2)), -1))
    g["gates"] = np.concatenate([_columns(a["g_xattn"]), _columns(a["g_ffn"])], axis=1)
    g["ln_gamma"] = np.stack([a["L0_xattn_gamma"], a["L0_xattn_ctx_gamma"]], axis=1)
    wkv = a["L0_xattn_Wkv"]
    g["wk0"] = np.concatenate([wkv[:, :DH0]] * 2, axis=1)
    g["wv0"] = np.concatenate([wkv[:, DH0:]] * 2, axis=1)
    g["wq0"] = a["L0_xattn_Wq"].T.reshape(8, P, D).transpose(1, 0, 2)
    g["wo0"] = a["L0_xattn_Wout"].reshape(8, P, D).transpose(1, 0, 2)
    g["wff1"] = a["L0_xattn_Wff1"]
    g["wff2"] = a["L0_xattn_Wff2"].reshape(4, P, D).transpose(1, 0, 2)
    g["wr"] = a["L0_ffn_Wr"]
    g["br"] = _columns(a["L0_ffn_br"])
    g["w1"] = a["L0_ffn_W1"].transpose(1, 0, 2)
    g["b1"] = a["L0_ffn_b1"]
    g["w2"] = a["L0_ffn_W2"].reshape(E0, 2, P, D).transpose(2, 1, 0, 3)
    g["b2"] = a["L0_ffn_b2"]
    g["wt"] = np.concatenate([a["L1_ffn_w_gate"].T, a["L1_ffn_w_up"].T,
                              a["L1_ffn_w_down"].T.reshape(4, P, D).transpose(1, 0, 2).reshape(P, FB)], axis=1)
    for n, name in (("wq2", "Wq"), ("wk2", "Wk"), ("wv2", "Wv")):
        g[n] = a["L2_xattn_" + name].transpose(1, 0, 2)
    g["b2qkv"] = np.stack([a["L2_xattn_b" + n].reshape(P) for n in "qkv"], axis=1)
    g["wo2"], g["bo2"] = a["L2_xattn_Wo"], a["L2_xattn_bo"]
    g["wg"] = a["L2_ffn_w_gate"].T
    g["w13"] = np.concatenate([m for e, s in (("w1_e", "w1_s"), ("w3_e", "w3_s"))
                               for m in (a["L2_ffn_" + e].reshape(E2 * F2W, D).T, a["L2_ffn_" + s].T)], axis=1)
    g["w2s"] = np.concatenate([a["L2_ffn_w2_e"].transpose(0, 2, 1).reshape(8, P, D),
                               a["L2_ffn_w2_s"].T[None]]).transpose(1, 0, 2)
    by_head = np.arange(D).reshape(DH, H).T.reshape(-1)
    g["wq3"], g["wk3"] = a["L3_xattn_Wq"][by_head].T, a["L3_xattn_Wk"][by_head].T
    g["wo3"] = a["L3_xattn_Wo"][:, by_head].T
    g["w3"] = np.concatenate([a["L3_ffn_Wp"].T] + [a[f"L3_ffn_Wd{i}"].T for i in range(4)] + [a["L3_ffn_W"].T], axis=1)
    g["bp"] = _columns(a["L3_ffn_bp"])
    g["sim"] = a["L3_ffn_sim"][:, cols3]
    g["temp"] = _columns(a["L3_ffn_temp"], PROJ)
    g["wu"] = np.concatenate([a[f"L3_ffn_Wu{i}"].T for i in range(4)], axis=0)

    nc = _bacc.Bacc("TRN2", target_bir_lowering=False, num_devices=1)
    arrays = {"x": a["x"], "ctx": a["ctx_1024"], "ctxT": np.ascontiguousarray(a["ctx_1024"].transpose(0, 2, 1)),
              "mask": np.ascontiguousarray(np.broadcast_to(a["mask_BxS2_ik0"][:, None, :], (B, P, CTX)))}
    for pack, parts in PACKS.items():
        arrays["w_" + pack] = _pack(parts, g)
    aps = {n: nc.dram_tensor("in_" + n, v.shape, mybir.dt.from_np(v.dtype), kind="ExternalInput").ap()
           for n, v in arrays.items()}
    out = nc.dram_tensor("out_0", (B, SEQ, D), F32, kind="ExternalOutput").ap()
    gated_flamingo(nc, aps["x"], aps["ctx"], aps["ctxT"], aps["mask"], {p: aps["w_" + p] for p in PACKS}, out)
    r = _run(nc, [{"in_" + n: v for n, v in arrays.items()}], core_ids=[0])
    return r.results[0]["out_0"]
```

```python
from contextlib import ExitStack

import numpy as np
import concourse.bass as bass
from concourse import mybir

F32, BF16, I32 = mybir.dt.float32, mybir.dt.bfloat16, mybir.dt.int32
ALU, ACT, AX = mybir.AluOpType, mybir.ActivationFunctionType, mybir.AxisListType

P = 128
D = 128
B, SEQ, CTX = 4, 512, 77
TILES = SEQ // P
H = 16
HC = H * CTX
HB = H // 4
SB = HB * CTX
NCH = -(-HC // P)
LASTROWS = HC - (NCH - 1) * P
DH0 = 64
DH = D // H
VW = DH + 1
FF0 = 512
E0, H0 = 8, 256
FB = 512
E2, F2W, FS2 = 16, 64, 128
GW = 384
RANKS = (1, 2, 4, 8)
R = sum(RANKS)
PROJ = 32
LN_EPS = 1e-5
MASKED = -1e30
MAGIC = 1.5 * 2.0 ** 23
CLAMP = float(np.log(1.0 / 0.01))

DVE_STEPS = 293
BLOCKS = ("A0", "F0", "A1", "F1", "A2", "F2", "A3", "F3")
NB = len(BLOCKS)
GATE = {k: (int(k[1]) if k[0] == "A" else 4 + int(k[1])) for k in BLOCKS}
UNITS = [(BLOCKS[u // TILES], u % TILES) for u in range(NB * TILES)]

PE_PARTS = (("first", 1), ("late_transpose", 3), ("xT", 0), ("middle", 2), ("extra", 1),
            ("project", 0), ("output", 3), ("values", 2), ("spread", 1), ("prepare", 0))
FILLS = {
    "A0": {"xT": ("X xT",), "first": ("S scores",), "middle": ("T0 gate", "T1 up"),
           "late_transpose": ("T0 hT", "T1 pa", "T0 pb", "T1 pc"), "output": ("O out",)},
    "F0": {"xT": ("X xT",), "project": ("X logits",), "extra": ("X pickT",), "spread": ("S masks",),
           "middle": ("O hidden",), "late_transpose": ("O bias", "T0 ya", "T1 yb")},
    "A1": {"xT": ("X xT",), "first": ("S scores",), "middle": ("T0 pT",), "values": ("O out",)},
    "F1": {"xT": ("X xT",), "extra": ("T0 gate", "T1 up"), "middle": ("T0 hT",), "values": ("O out",)},
    "A2": {"xT": ("X xT",), "project": ("X q",), "first": ("S scores",),
           "middle": ("T0 pa", "T1 pb", "T0 pc"), "values": ("O values",),
           "late_transpose": ("X vT",), "output": ("X out",)},
    "F2": {"xT": ("X xT",), "project": ("X gate",), "first": ("S gu",), "middle": ("T0 gate", "T1 up"),
           "late_transpose": ("T0 ha", "T1 hb", "T0 hc"), "output": ("O out",)},
    "F3": {"xT": ("X xT",), "first": ("S all",), "extra": ("X projT",), "middle": ("X logits",),
           "late_transpose": ("X downT",), "output": ("O out",)},
}
FILLS["A3"] = FILLS["A2"]
PREPARE = {13: ("X cT",),
           14: ("X kv", "X kv0"),
           15: ("S a", "S b"),
           16: ("T0 va", "T1 vb", "T0 vc", "T0 ba", "T1 bb", "T0 bc"),
           17: ("T0 ka", "T1 kb", "T0 kc")}
PRELUDE = ("X cT", "X kv0", "S a", "S b", "T0 ba", "T1 bb", "T0 bc", "X wmean", "X simnorm")


U = len(UNITS)


def steps(parts, first, last, next_only=False):
    for s in range(first, last):
        for part, phase in parts:
            v = s - phase
            if 0 <= v < U + 3 and not (next_only and v < U) and (part != "prepare" or s in PREPARE):
                yield part, v


class Bank:

    def __init__(self, name, tile, full, drained):
        self.name, self.tile, self.full, self.drained = name, tile, full, drained
        self.prelude = [f.split()[1] for f in PRELUDE if f.split()[0] == name]
        self.order, tail = {}, None
        for part, v in steps(PE_PARTS, 3, U + 3):
            if tail is None and (part, v) == (PE_PARTS[0][0], U - PE_PARTS[0][1]):
                tail = len(self.order)
            for f in fillings(part, v):
                if f.split()[0] == name:
                    self.order[f.split()[1], None if part == "prepare" else v] = len(self.order)
        self.per_pass = len(self.order)
        self.base = len(self.prelude) + self.per_pass - tail

    def number(self, it, what, v=None):
        if isinstance(it, int) and v is None:
            return self.prelude.index(what) + 1
        at = self.order.get((what, v))
        if at is None:
            at = self.order[what, v + U] - self.per_pass
        return it * self.per_pass + (self.base + at + 1)


def fillings(part, v):
    return PREPARE[v] if part == "prepare" else FILLS[UNITS[v % U][0]].get(part, ())


PACKS = {
    "base": [("ident", P, P), ("delta", P, H), ("ones_col", P, NCH * H), ("desc0", P, E0),
             ("desc3", P, 4 + R), ("gates", P, 8), ("tri4", P, 16), ("tri16", P, 256), ("ln_gamma", P, 2)],
    "att0": [("wk0", P, 2 * DH0), ("wv0", P, 2 * DH0), ("wq0", P, 8 * D), ("wo0", P, 8 * D)],
    "tern": [("wt", P, 3 * FB)],
    "low": [("w3", P, PROJ + R + D), ("bp", P, PROJ), ("sim", PROJ, 4 + R), ("temp", PROJ, 1),
            ("wu", R, D)],
    "ff0": [("wff1", P, 2 * FF0), ("wff2", P, 4 * D)],
    "top1": [("wr", P, E0), ("br", P, E0), ("w1", P, E0 * H0), ("b1", E0, H0), ("w2", P, 2 * E0 * D),
             ("b2", E0, D)],
    "att23": [("wq2", P, D), ("wk2", P, D), ("wv2", P, D), ("b2qkv", P, 3), ("wo2", P, D),
              ("bo2", 1, D), ("wq3", P, D), ("wk3", P, D), ("wo3", P, D)],
    "top4": [("wg", P, E2), ("w13", P, 6 * GW), ("w2s", P, 9 * D)],
}
WIDTH = {k: sum(c for _, _, c in v) for k, v in PACKS.items()}


def gated_flamingo(nc, x_in, ctx_in, ctxT_in, mask_in, packs, out):
    with ExitStack() as stack:
        def sb(name, shape, dt=F32):
            return stack.enter_context(nc.sbuf_tensor(name, shape, dt))

        def psum(name, shape):
            return stack.enter_context(nc.psum_tensor(name, shape, F32))

        def sem(name):
            return stack.enter_context(nc.semaphore(name))

        hh = sb("hh", [P, 3, 3 * GW])
        W, loaded = {}, {}
        for pack, parts in PACKS.items():
            tile = hh[:, :, :].rearrange("p b n -> p (b n)") if pack == "tern" else sb("pack_" + pack, [P, WIDTH[pack]])
            loaded[pack] = sem("loaded_" + pack)
            at = 0
            for name, rows, cols in parts:
                W[name] = tile[0:rows, at:at + cols]
                at += cols
            W["pack_" + pack] = tile[:, 0:WIDTH[pack]]
        ident = W["ident"]
        ident_b = sb("ident_b", [P, P], BF16)
        ones = sb("ones", [P, P])
        ones_b = sb("ones_b", [1, P], BF16)
        pick_row = sb("pick_row", [E0, E0, P], BF16)
        half = sb("half", [P, 4])
        tg = sb("tg", [P, 8])
        tgh = sb("tgh", [P, 1])
        sq2 = sb("sq2", [P, 1])
        wt_q = sb("wt_q", [P, 3 * FB], BF16)
        wt_sum = sb("wt_sum", [P, 3])
        wt_mean = sb("wt_mean", [P, 3])
        wt_inv = sb("wt_inv", [P, 3])
        wt_c = sb("wt_c", [P, 3])
        sim_sq = sb("sim_sq", [PROJ, 4 + R])
        sim_n = sb("sim_n", [PROJ, 4 + R])
        sim_s = sb("sim_s", [PROJ, 1])

        ctx_st = sb("ctx_st", [CTX, D])
        ctxT_st = sb("ctxT_st", [D, CTX])
        mask_st = sb("mask_st", [P, CTX], I32)
        x_st = sb("x_st", [P, TILES, D])
        ctx = sb("ctx", [CTX, D])
        ctxT = sb("ctxT", [D, CTX])
        mask_row = sb("mask_row", [1, HB, CTX], BF16)
        seen = sb("seen", [P, CTX])
        anyseen = sb("anyseen", [P, 3])
        cstat = sb("cstat", [CTX, 6])
        cmv = sb("cmv", [CTX, 2])
        cve = sb("cve", [CTX, 1])
        crs = sb("crs", [CTX, 1])
        ctxn = sb("ctxn", [CTX, D])
        ctxnT = sb("ctxnT", [D, CTX])
        k0 = sb("k0", [P, 2, CTX])
        v0 = sb("v0", [P, 2, CTX])
        A0 = sb("A0", [D, HC])
        B0 = sb("B0", [P, NCH, D])
        k2 = sb("k2", [P, CTX])
        v2 = sb("v2", [P, CTX])
        k3 = sb("k3", [P, CTX])
        K2 = sb("K2", [P, H, CTX])
        K3 = sb("K3", [P, H, CTX])
        V2 = sb("V2", [P, NCH, H, VW])
        V3 = sb("V3", [P, NCH, H, VW])

        x = sb("x", [P, TILES, D])
        y = sb("y", [P, TILES, D])
        stat = sb("stat", [P, 6])
        mv = sb("mv", [P, TILES, 2])
        ve = sb("ve", [P, TILES])
        rstd = sb("rstd", [P, TILES])
        xh = sb("xh", [P, TILES, D])
        xhq = sb("xhq", [P, 2, D])
        xq = sb("xq", [P, TILES, D], BF16)
        xT = sb("xT", [D, TILES, P])
        qT = sb("qT", [D, 2, P])
        xTq = sb("xTq", [D, TILES, P], BF16)
        mx = sb("mx", [P, TILES, H])
        pr = sb("pr", [P, 3, HC])
        wt_r = pr[:, :, :].rearrange("p b n -> p (b n)")[:, 0:3 * FB]
        pT = sb("pT", [P, 2, NCH, P])
        B0T = pT[:, 0, :, :].rearrange("p n d -> p (n d)")[:, 0:HC]
        V2x = pT[:, 1, :, :].rearrange("p n d -> p (n d)")[:, 0:HC].rearrange("p (h c) -> p h c", c=CTX)
        rs = sb("rs", [P, TILES, H])
        ri = sb("ri", [P, TILES, H])
        cv = sb("cv", [P, 2, D])
        cvT = sb("cvT", [D, 2, P])
        th = sb("th", [P, 2, 3 * GW])
        g1 = sb("g1", [P, 2, 3 * GW])
        hT = sb("hT", [P, 2, 9, P])
        hq = sb("hq", [P, 2, FB], BF16)
        hqT = sb("hqT", [P, 2, 4, P], BF16)
        sc = sb("sc", [P, TILES, 16])
        lg = sb("lg", [P, TILES, 4 + R])
        tt = sb("tt", [P, TILES, 4 + R])
        oh = sb("oh", [P, TILES, 4 + R])
        ex = sb("ex", [P, TILES, E0])
        ohT = sb("ohT", [E0, TILES, P])
        ohTb = sb("ohTb", [E0, 2, P], BF16)
        xm = sb("xm", [D, 2, E0, P])
        hid = sb("hid", [P, 2, 2, P])
        sg = sb("sg", [P, TILES, E2])
        sig = sb("sig", [P, TILES, E2])
        pairs = sb("pairs", [P, 4, 6])
        gs = sb("gs", [P, 4])
        cmp4 = sb("cmp4", [P, 4, 2, 4])
        rank4 = sb("rank4", [P, 4])
        cmp16 = sb("cmp16", [P, E2, 2, E2])
        rank16 = sb("rank16", [P, E2])
        picked = sb("picked", [P, E2])
        allow1 = sb("allow1", [P, 4])
        psc = sb("psc", [P, 4])
        allow = sb("allow", [P, 4])
        msk = sb("msk", [P, E2])
        comb = sb("comb", [P, TILES, E2])
        pj = sb("pj", [P, TILES, PROJ])
        pj2 = sb("pj2", [P, PROJ])
        pjT = sb("pjT", [PROJ, 2, P])
        dn = sb("dn", [P, TILES, R])
        dm = sb("dm", [P, TILES, R])
        dmT = sb("dmT", [R, 2, P])

        S, T0, T1, O, X = (Bank(n, psum("psum_" + n, s), sem(n + "_full"), sem(n + "_drained")) for n, s in
                           (("S", [P, 4, 512]), ("T0", [P, 512]), ("T1", [P, 512]), ("O", [P, 512]), ("X", [P, 512])))
        banks = (S, T0, T1, O, X)

        events = {}

        def event(name, per_pass, before=0):
            events[name] = (sem(name), per_pass, before)

        event("var_ready", U)
        event("rstd_ready", U)
        event("xh_ready", U)
        event("ctx_var", 1, 1)
        event("ctx_rstd", 1, 1)
        event("ctx_norm", 1, 1)
        event("ctx_copied", 1, 1)
        event("ctx_used", 1, 1)
        event("mask_ready", 1, 1)
        event("expanded", 3)
        event("inv0", TILES)
        event("probs0", TILES)
        for name in ("probs_A0", "probs_A2", "probs_A3",
                     "tanh_A0", "tanh_F1", "tanh_F2a", "tanh_F2b",
                     "nmax_A1",
                     "centred_F0", "centred_F3",
                     "expsum_F0", "expsum_F3",
                     "pick_ready",
                     "hq_ready",
                     "comb_ready",
                     "weighted_F2a", "weighted_F2b",
                     "pj_ready", "ss_ready",
                     "rn_ready",
                     "dm_ready"):
            event(name, TILES)
        s_x_loaded, s_c_loaded, s_stored = sem("x_loaded"), sem("c_loaded"), sem("stored")
        s_const, s_tg, s_prel = sem("const_ready"), sem("tanh_gates"), sem("prelude")
        s_dve, s_simpow, s_temp, s_quant = sem("dve_step"), sem("sim_pow"), sem("temp_exp"), sem("ternary_ready")
        s_carry = sem("wait_carrier")
        block = stack.enter_context(nc.Block())

        def helpers(eng, it):
            def full(bank, what, v=None):
                eng.wait_ge(bank.full, bank.number(it, what, v))

            def free(bank, what, v=None):
                eng.wait_ge(bank.drained, bank.number(it, what, v))

            def drained(bank, what, v=None):
                eng.wait_ge(bank.drained, bank.number(it, what, v) + 1)

            def wait(name, n, v=0):
                s, per, before = events[name]
                eng.wait_ge(s, it * per + (before + n + 1 + v // U * per))
            return full, free, drained, wait

        def inc(ins, name):
            return ins.then_inc(events[name][0], 1)

        @block.sync
        def _(sp):
            def load_ctx(b):
                sp.dma_start(ctx_st[:, :], ctx_in[b]).then_inc(s_c_loaded, 16)
                sp.dma_start(ctxT_st[:, :], ctxT_in[b]).then_inc(s_c_loaded, 16)
                sp.dma_start(mask_st[:, :], mask_in[b]).then_inc(s_c_loaded, 16)

            def load_x(b):
                sp.dma_start(x_st[:, :, :], x_in[b].rearrange("(t p) d -> p t d", p=P)).then_inc(s_x_loaded, 16)

            sp.sem_inc(s_stored, 16 * TILES)
            for pack in PACKS:
                sp.dma_start(W["pack_" + pack], packs[pack]).then_inc(loaded[pack], 16)
                if pack == "base":
                    load_ctx(0)
                    load_x(0)
            def next_ctx(n):
                sp.wait_ge(events["ctx_copied"][0], n)
                sp.wait_ge(events["ctx_used"][0], n)
                load_ctx(n % B)

            next_ctx(1)
            for b in range(B):
                full, free, drained, wait = helpers(sp, b)
                drained(O, "out", TILES - 1)
                load_x((b + 1) % B)
                if b + 2 <= B:
                    next_ctx(b + 2)
                for t in range(TILES):
                    drained(O, "out", U - TILES + t)
                    sp.dma_start(out[b, t * P:(t + 1) * P, :], y[:, t, :]).then_inc(s_stored, 16)
            sp.wait_ge(s_stored, 16 * B * TILES + 16 * TILES)

        @block.tensor
        def _(pe):
            def transposes(dst, src, chunks):
                for n, (lo, hi) in enumerate(chunks):
                    last = pe.transpose(dst[0:hi - lo, n * P:(n + 1) * P], src[:, lo:hi], ident)
                return last

            cuts = [(n * P, min((n + 1) * P, HC)) for n in range(NCH)]
            trio = (cuts[0:4], cuts[4:8], cuts[8:NCH])

            def keys_values(full, free, drained, wait):
                def cT():
                    wait("ctx_norm", 0)
                    free(X, "cT")
                    pe.transpose(X.tile[:, 0:CTX], ctxn[:, :], ident[0:CTX, 0:CTX]).then_inc(X.full, 1)

                def kv():
                    free(X, "kv")
                    pe.matmul(X.tile[:, 0:CTX], W["wk2"], ctxT[:, :], start=True, stop=True)
                    pe.matmul(X.tile[:, P:P + CTX], W["wv2"], ctxT[:, :], start=True, stop=True)
                    pe.matmul(X.tile[:, 2 * P:2 * P + CTX], W["wk3"], ctxT[:, :], start=True, stop=True)\
                      .then_inc(X.full, 1)

                def kv0():
                    drained(X, "cT")
                    free(X, "kv0")
                    pe.matmul(X.tile[:, 0:CTX], W["wk0"], ctxnT[:, :], start=True, stop=True)
                    pe.matmul(X.tile[:, P:P + CTX], W["wv0"], ctxnT[:, :], start=True, stop=True).then_inc(X.full, 1)

                def ab():
                    drained(X, "kv0")
                    for what, w, kv_ in (("a", "wq0", k0), ("b", "wo0", v0)):
                        free(S, what)
                        for g in range(H // 2):
                            last = pe.matmul(S.tile[:, g // 2, g % 2 * 2 * CTX:(g % 2 + 1) * 2 * CTX],
                                             W[w][:, g * D:(g + 1) * D], kv_[:, :, :], start=True, stop=True)
                        last.then_inc(S.full, 1)

                def turn(src, names):
                    for bank, what, cs in zip((T0, T1, T0), names, trio):
                        free(bank, what)
                        transposes(bank.tile, src, cs).then_inc(bank.full, 1)

                def vb():
                    wait("expanded", 1)
                    turn(V2x.rearrange("p h c -> p (h c)"), ("va", "vb", "vc"))
                    bT()

                def bT():
                    drained(S, "b")
                    turn(B0T, ("ba", "bb", "bc"))

                def kT():
                    wait("expanded", 2)
                    turn(K3[:, :, :].rearrange("p h c -> p (h c)"), ("ka", "kb", "kc"))
                return {13: (cT,), 14: (kv, kv0), 15: (ab,), 16: (vb,), 17: (kT,)}, (cT, kv0, ab, bT)

            pe.wait_ge(s_const, 9)
            pe.wait_ge(loaded["att0"], 16)
            full, free, drained, wait = helpers(pe, -1)
            for part in keys_values(full, free, drained, wait)[1]:
                part()
            pe.wait_ge(s_prel, 1)
            free(X, "wmean")
            pe.matmul(X.tile[:, 0:3], ones[:, :], wt_sum[:, :], start=True, stop=True).then_inc(X.full, 1)
            pe.wait_ge(s_prel, 2)
            free(X, "simnorm")
            pe.matmul(X.tile[0:PROJ, 0:4 + R], ones[0:PROJ, 0:PROJ], sim_sq[:, :], start=True, stop=True)\
              .then_inc(X.full, 1)
            drained(S, "a")
            drained(T0, "bc")

            def one_pass(it):
                full, free, drained, wait = helpers(pe, it)

                def xT_(k, u, t):
                    wait("xh_ready", u)
                    free(X, "xT", u)
                    if k == "F1":
                        pe.transpose(X.tile[:, 0:P // 2].bitcast(BF16), xq[:, t, :], ident_b[:, :])\
                          .then_inc(X.full, 1)
                    else:
                        pe.transpose(X.tile[:, 0:P], xh[:, t, :], ident).then_inc(X.full, 1)

                def first(k, u, t):
                    n = 4 * int(k[1]) + t
                    if k == "A0":
                        wait("mask_ready", -1, u)
                        drained(X, "xT", u)
                        free(S, "scores", u)
                        for q in range(4):
                            pe.matmul(S.tile[:, q, 0:SB], xT[:, t, :], A0[:, q * SB:(q + 1) * SB],
                                      start=True, stop=False)
                            last = pe.matmul(S.tile[:, q, 0:SB], ones_b[:, :],
                                             mask_row[:, :, :].rearrange("o h c -> o (h c)"),
                                             start=False, stop=True)
                        last.then_inc(S.full, 1)
                    elif k in ("A2", "A3"):
                        K = (K2 if k == "A2" else K3)[:, :, :].rearrange("p h c -> p (h c)")
                        drained(X, "q", u)
                        wait("expanded", 0 if k == "A2" else 2)
                        free(S, "scores", u)
                        for q in range(4):
                            last = pe.matmul(S.tile[:, q, 0:SB], qT[:, u % 2, :], K[:, q * SB:(q + 1) * SB],
                                             start=True, stop=True)
                        last.then_inc(S.full, 1)
                    elif k == "A1":
                        wait("ctx_copied", -1)
                        drained(X, "xT", u)
                        free(S, "scores", u)
                        pe.matmul(S.tile[:, 0, 0:CTX], xT[:, t, :], ctxT[:, :], start=True, stop=True)\
                          .then_inc(S.full, 1)
                    elif k == "F2":
                        pe.wait_ge(loaded["top4"], 16)
                        drained(X, "xT", u)
                        free(S, "gu", u)
                        for q, c in enumerate((0, 1, 3, 4)):
                            last = pe.matmul(S.tile[:, q, 0:GW], xT[:, t, :], W["w13"][:, c * GW:(c + 1) * GW],
                                             start=True, stop=True)
                        last.then_inc(S.full, 1)
                    elif k == "F3":
                        pe.wait_ge(loaded["low"], 16)
                        drained(X, "xT", u)
                        free(S, "all", u)
                        pe.matmul(S.tile[:, 0, 0:PROJ + R + D], xT[:, t, :], W["w3"], start=True, stop=True)\
                          .then_inc(S.full, 1)

                def late_transpose(k, u, t):
                    if k == "A0":
                        drained(T1, "up", u)
                        free(T0, "hT", u)
                        transposes(T0.tile, hh[:, u % U % 3, :], cuts[0:4]).then_inc(T0.full, 1)
                        wait("probs0", t, u)
                        for bank, what, cs in zip((T1, T0, T1), ("pa", "pb", "pc"), trio):
                            free(bank, what, u)
                            transposes(bank.tile, pr[:, u % U % 3, :], cs).then_inc(bank.full, 1)
                    elif k == "F0":
                        free(O, "bias", u)
                        pe.matmul(O.tile[:, 0:D], ohT[:, t, :], W["b2"], start=True, stop=True).then_inc(O.full, 1)
                        drained(O, "hidden", u)
                        for n, bank, what in ((0, T0, "ya"), (1, T1, "yb")):
                            free(bank, what, u)
                            for j in range(2):
                                last = pe.matmul(bank.tile[:, :], hid[:, u % 2, j, :],
                                                 W["w2"][:, j * E0 * D + n * 512:j * E0 * D + (n + 1) * 512],
                                                 start=(j == 0), stop=(j == 1))
                            last.then_inc(bank.full, 1)
                    elif k in ("A2", "A3"):
                        drained(O, "values", u)
                        free(X, "vT", u)
                        pe.transpose(X.tile[:, 0:P], cv[:, u % 2, :], ident).then_inc(X.full, 1)
                    elif k == "F2":
                        wait("weighted_F2a", t, u)
                        wait("weighted_F2b", t, u)
                        hc = [(n * P, (n + 1) * P) for n in range(9)]
                        for bank, what, cs in ((T0, "ha", hc[0:4]), (T1, "hb", hc[4:8]), (T0, "hc", hc[8:9])):
                            free(bank, what, u)
                            transposes(bank.tile, hh[:, u % U % 3, :], cs).then_inc(bank.full, 1)
                    elif k == "F3":
                        wait("dm_ready", t, u)
                        free(X, "downT", u)
                        pe.transpose(X.tile[0:R, 0:P], dm[:, t, :], ident).then_inc(X.full, 1)

                def middle(k, u, t):
                    if k == "A0":
                        pe.wait_ge(loaded["ff0"], 16)
                        for n, bank, what in ((1, T0, "gate"), (0, T1, "up")):
                            free(bank, what, u)
                            pe.matmul(bank.tile[:, :], xT[:, t, :], W["wff1"][:, n * FF0:(n + 1) * FF0],
                                      start=True, stop=True).then_inc(bank.full, 1)
                    elif k == "F0":
                        pe.wait_ge(loaded["top1"], 16)
                        drained(S, "masks", u)
                        free(O, "hidden", u)
                        for j in range(2):
                            for e in range(E0):
                                pe.matmul(O.tile[:, j * P:(j + 1) * P],
                                          W["w1"][:, e * H0 + j * P:e * H0 + (j + 1) * P],
                                          xm[:, u % 2, e, :], start=(e == 0), stop=False)
                            last = pe.matmul(O.tile[:, j * P:(j + 1) * P], W["b1"][:, j * P:(j + 1) * P],
                                             ohT[:, t, :], start=False, stop=True)
                        last.then_inc(O.full, 1)
                    elif k == "A1":
                        drained(S, "scores", u)
                        free(T0, "pT", u)
                        pe.transpose(T0.tile[0:CTX, 0:P], pr[:, u % U % 3, 0:CTX], ident).then_inc(T0.full, 1)
                    elif k == "F1":
                        wait("hq_ready", t, u)
                        free(T0, "hT", u)
                        for n in range(4):
                            last = pe.transpose(T0.tile[:, n * 64:(n + 1) * 64].bitcast(BF16),
                                                hq[:, u % 2, n * P:(n + 1) * P], ident_b[:, :])
                        last.then_inc(T0.full, 1)
                    elif k in ("A2", "A3"):
                        wait("probs_" + k, t, u)
                        for bank, what, cs in zip((T0, T1, T0), ("pa", "pb", "pc"), trio):
                            free(bank, what, u)
                            transposes(bank.tile, pr[:, u % U % 3, :], cs).then_inc(bank.full, 1)
                    elif k == "F2":
                        for c, bank, what in ((2, T0, "gate"), (5, T1, "up")):
                            free(bank, what, u)
                            pe.matmul(bank.tile[:, 0:GW], xT[:, t, :], W["w13"][:, c * GW:(c + 1) * GW],
                                      start=True, stop=True).then_inc(bank.full, 1)
                    elif k == "F3":
                        drained(X, "projT", u)
                        pe.wait_ge(s_prel, 4)
                        free(X, "logits", u)
                        pe.matmul(X.tile[:, 0:4 + R], pjT[:, u % 2, :], sim_n[:, :], start=True, stop=True)\
                          .then_inc(X.full, 1)

                def extra(k, u, t):
                    if k == "F0":
                        wait("pick_ready", t, u)
                        free(X, "pickT", u)
                        pe.transpose(X.tile[0:E0, 0:P], oh[:, t, 0:E0], ident).then_inc(X.full, 1)
                    elif k == "F1":
                        pe.wait_ge(s_quant, 1)
                        drained(X, "xT", u)
                        for n, bank, what in ((0, T0, "gate"), (1, T1, "up")):
                            free(bank, what, u)
                            pe.matmul(bank.tile[:, :], xTq[:, t, :], wt_q[:, n * FB:(n + 1) * FB],
                                      start=True, stop=True).then_inc(bank.full, 1)
                    elif k == "F3":
                        wait("pj_ready", t, u)
                        free(X, "projT", u)
                        pe.transpose(X.tile[0:PROJ, 0:P], pj[:, t, :], ident).then_inc(X.full, 1)

                def project(k, u, t):
                    if k == "F0":
                        pe.wait_ge(loaded["top1"], 16)
                        drained(X, "xT", u)
                        free(X, "logits", u)
                        pe.matmul(X.tile[:, 0:E0], xT[:, t, :], W["wr"], start=True, stop=True).then_inc(X.full, 1)
                    elif k in ("A2", "A3"):
                        drained(X, "xT", u)
                        free(X, "q", u)
                        pe.matmul(X.tile[:, 0:P], W["wq2" if k == "A2" else "wq3"], xT[:, t, :],
                                  start=True, stop=True).then_inc(X.full, 1)
                    elif k == "F2":
                        pe.wait_ge(loaded["top4"], 16)
                        drained(X, "xT", u)
                        free(X, "gate", u)
                        pe.matmul(X.tile[:, 0:E2], xT[:, t, :], W["wg"], start=True, stop=True).then_inc(X.full, 1)

                def output(k, u, t):
                    if k == "A0":
                        free(O, "out", u)
                        drained(T0, "hT", u)
                        for n in range(4):
                            pe.matmul(O.tile[:, 0:D], hT[:, u % 2, n, :], W["wff2"][:, n * D:(n + 1) * D],
                                      start=(n == 0), stop=False)
                        drained(T0, "pb", u)
                        drained(T1, "pc", u)
                        for n, (lo, hi) in enumerate(cuts):
                            last = pe.matmul(O.tile[:, 0:D], pT[0:hi - lo, u % 2, n, :], B0[0:hi - lo, n, :],
                                             start=False, stop=(n == NCH - 1))
                        last.then_inc(O.full, 1)
                    elif k in ("A2", "A3"):
                        drained(X, "vT", u)
                        free(X, "out", u)
                        last = pe.matmul(X.tile[:, 0:D], cvT[:, u % 2, :], W["wo2" if k == "A2" else "wo3"],
                                         start=True, stop=(k == "A3"))
                        if k == "A2":
                            last = pe.matmul(X.tile[:, 0:D], ones[0:1, :], W["bo2"], start=False, stop=True)
                        last.then_inc(X.full, 1)
                    elif k == "F2":
                        free(O, "out", u)
                        drained(T1, "hb", u)
                        drained(T0, "hc", u)
                        for n in range(9):
                            last = pe.matmul(O.tile[:, 0:D], hT[:, u % 2, n, :], W["w2s"][:, n * D:(n + 1) * D],
                                             start=(n == 0), stop=(n == 8))
                        last.then_inc(O.full, 1)
                    elif k == "F3":
                        drained(X, "downT", u)
                        free(O, "out", u)
                        pe.matmul(O.tile[:, 0:D], dmT[:, u % 2, :], W["wu"], start=True, stop=True).then_inc(O.full, 1)

                def values(k, u, t):
                    if k == "A1":
                        drained(T0, "pT", u)
                        free(O, "out", u)
                        pe.matmul(O.tile[:, 0:D], pT[0:CTX, u % 2, 0, :], ctx[:, :], start=True, stop=True)\
                          .then_inc(O.full, 1)
                    elif k == "F1":
                        drained(T0, "hT", u)
                        free(O, "out", u)
                        for n in range(4):
                            last = pe.matmul(O.tile[:, 0:D], hqT[:, u % 2, n, :],
                                             wt_q[:, 2 * FB + n * D:2 * FB + (n + 1) * D],
                                             start=(n == 0), stop=(n == 3))
                        last.then_inc(O.full, 1)
                    elif k in ("A2", "A3"):
                        V = V2 if k == "A2" else V3
                        drained(T0, "vc" if k == "A2" else "kc")
                        drained(T1, "pb", u)
                        drained(T0, "pc", u)
                        free(O, "values", u)
                        for n, (lo, hi) in enumerate(cuts):
                            h0, h1 = lo // CTX, -(-hi // CTX)
                            last = pe.matmul(O.tile[:, h0 * VW:h1 * VW], pT[0:hi - lo, u % 2, n, :],
                                             V[0:hi - lo, n, h0:h1, :].rearrange("p h v -> p (h v)"),
                                             start=(n == 0), stop=(n == NCH - 1), skip_group_check=True)
                        last.then_inc(O.full, 1)

                def spread(k, u, t):
                    if k == "F0":
                        drained(X, "pickT", u)
                        free(S, "masks", u)
                        for e in range(E0):
                            last = pe.matmul(S.tile[:, e // 4, e % 4 * P:(e % 4 + 1) * P], pick_row[:, e, :],
                                             ohTb[:, u % 2, :], start=True, stop=True)
                        last.then_inc(S.full, 1)

                parts = dict(first=first, late_transpose=late_transpose, xT=xT_, middle=middle, extra=extra,
                             project=project, output=output, values=values, spread=spread)
                prepare = keys_values(full, free, drained, wait)[0]

                def work(part, v):
                    if part == "prepare":
                        for do in prepare[v]:
                            do()
                    else:
                        parts[part](UNITS[v % U][0], v, UNITS[v % U][1])
                return free, work

            free, work = one_pass(-1)
            for part, v in steps(PE_PARTS, U, U + 3):
                if v >= U:
                    work(part, v)
                    continue
                for f in fillings(part, v):
                    bank = next(b for b in banks if b.name == f.split()[0])
                    free(bank, f.split()[1], v)
                    pe.sem_inc(bank.full, 1)
                    pe.sem_inc(bank.drained, 1)

            with pe.Fori(0, B) as it:
                free, work = one_pass(it)
                for part, v in steps(PE_PARTS, 3, U + 3):
                    work(part, v)

        @block.scalar
        def _(act):
            Copy, Exp, Tanh, Relu, Ident = ACT.Copy, ACT.Exp, ACT.Tanh, ACT.Relu, ACT.Identity
            act.sem_inc(X.drained, 1)
            act.sem_inc(T0.drained, 1)
            act.sem_inc(T1.drained, 1)
            act.wait_ge(loaded["base"], 16)
            act.activation(tg[:, :], W["gates"], Tanh).then_inc(s_tg, 1)

            groups = ((0, 4), (4, 8), (8, NCH))

            def keys_values(full, free, drained, wait):
                def cT():
                    full(X, "cT")
                    act.activation(ctxnT[:, :], X.tile[:, 0:CTX], Copy, scale=W["ln_gamma"][:, 1:2])\
                       .then_inc(X.drained, 1)

                def kv():
                    full(X, "kv")
                    act.activation(k2[:, :], X.tile[:, 0:CTX], Ident, bias=W["b2qkv"][:, 1:2])
                    act.activation(v2[:, :], X.tile[:, P:P + CTX], Ident, bias=W["b2qkv"][:, 2:3])
                    act.activation(k3[:, :], X.tile[:, 2 * P:2 * P + CTX], Copy).then_inc(X.drained, 1)

                def kv0():
                    full(X, "kv0")
                    wait("ctx_used", 0)
                    for g in range(2):
                        rows = slice(g * DH0, (g + 1) * DH0)
                        act.activation(k0[rows, g, :], X.tile[rows, 0:CTX], Copy, scale=float(DH0) ** -0.5)
                        last = act.activation(v0[rows, g, :], X.tile[rows, P:P + CTX], Copy, scale=anyseen[rows, 2:3])
                    last.then_inc(X.drained, 1)

                def ab():
                    for what, dst in (("a", A0[:, :]), ("b", B0T)):
                        full(S, what)
                        act.activation(dst.rearrange("p (b n) -> p b n", b=4), S.tile[:, :, 0:SB], Copy)\
                           .then_inc(S.drained, 1)

                def bT():
                    for bank, what, (lo, hi) in zip((T0, T1, T0), ("ba", "bb", "bc"), groups):
                        full(bank, what)
                        act.activation(B0[:, lo:hi, :], bank.tile[:, 0:(hi - lo) * P].rearrange("p (n d) -> p n d", d=P),
                                       Copy).then_inc(bank.drained, 1)

                def turned(V, names):
                    for bank, what, (lo, hi) in zip((T0, T1, T0), names, groups):
                        full(bank, what)
                        src = bank.tile[:, 0:(hi - lo) * P].rearrange("p (n h v) -> p n h v", h=H, v=DH)
                        for n in range(lo, hi):
                            last = act.activation(V[:, n, :, 0:DH], src[:, n - lo, :, :], Copy)
                        last.then_inc(bank.drained, 1)

                def vb():
                    turned(V2, ("va", "vb", "vc"))
                    bT()

                def kT():
                    turned(V3, ("ka", "kb", "kc"))
                return {13: (cT,), 14: (kv, kv0), 15: (ab,), 16: (vb,), 17: (kT,)}, (cT, kv0, ab, bT)

            act.wait_ge(s_const, 9)
            for part in keys_values(*helpers(act, -1))[1]:
                part()
            act.wait_ge(s_prel, 3)
            act.activation(sim_s[:, :], sim_s[:, :], Exp).then_inc(s_temp, 1)

            def one_pass(it, first):
                full, free, drained, wait = helpers(act, it)
                prepare = keys_values(full, free, drained, wait)[0]

                def evac_probs(bank, what, u, t, lo, hi):
                    full(bank, what, u)
                    act.activation(pT[:, u % 2, lo:hi, :], bank.tile[:, 0:(hi - lo) * P].rearrange("p (n d) -> p n d", d=P),
                                   Copy).then_inc(bank.drained, 1)

                def phase3(k, u, t):
                    if k == "A0":
                        full(T0, "hT", u)
                        act.activation(hT[:, u % 2, 0:4, :], T0.tile[:, :].rearrange("p (n d) -> p n d", d=P), Copy)\
                           .then_inc(T0.drained, 1)
                        for bank, what, (lo, hi) in zip((T1, T0, T1), ("pa", "pb", "pc"), groups):
                            evac_probs(bank, what, u, t, lo, hi)
                    elif k in ("A2", "A3"):
                        full(X, "vT", u)
                        act.activation(cvT[:, u % 2, :], X.tile[:, 0:P], Copy).then_inc(X.drained, 1)
                    elif k == "F2":
                        for bank, what, lo, hi in ((T0, "ha", 0, 4), (T1, "hb", 4, 8), (T0, "hc", 8, 9)):
                            full(bank, what, u)
                            act.activation(hT[:, u % 2, lo:hi, :],
                                           bank.tile[:, 0:(hi - lo) * P].rearrange("p (n d) -> p n d", d=P), Copy)\
                               .then_inc(bank.drained, 1)
                    elif k == "F3":
                        full(X, "downT", u)
                        act.activation(dmT[:, u % 2, :], X.tile[0:R, 0:P], Copy).then_inc(X.drained, 1)

                def phase0(k, u, t):
                    full(X, "xT", u)
                    if k == "A0":
                        act.activation(xT[:, t, :], X.tile[:, 0:P], Copy, scale=W["ln_gamma"][:, 0:1])\
                           .then_inc(X.drained, 1)
                    elif k == "F1":
                        act.activation(xTq[:, t, :], X.tile[:, 0:P // 2].bitcast(BF16), Copy).then_inc(X.drained, 1)
                    else:
                        act.activation(xT[:, t, :], X.tile[:, 0:P], Copy).then_inc(X.drained, 1)

                def phase2(k, u, t):
                    if k == "A0":
                        full(T0, "gate", u)
                        inc(act.activation(th[:, u % 2, 0:FF0], T0.tile[:, :], Tanh, scale=0.5), "tanh_A0")
                    elif k == "F0":
                        full(O, "hidden", u)
                        act.activation(hid[:, u % 2, :, :], O.tile[:, 0:2 * P].rearrange("p (j n) -> p j n", j=2), Relu)\
                           .then_inc(O.drained, 1)
                    elif k == "A1":
                        full(T0, "pT", u)
                        act.activation(pT[0:CTX, u % 2, 0, :], T0.tile[0:CTX, 0:P], Copy).then_inc(T0.drained, 1)
                    elif k == "F1":
                        full(T0, "hT", u)
                        act.activation(hqT[:, u % 2, :, :], T0.tile[:, 0:256].bitcast(BF16).rearrange("p (n d) -> p n d", d=P),
                                       Copy).then_inc(T0.drained, 1)
                    elif k in ("A2", "A3"):
                        for bank, what, (lo, hi) in zip((T0, T1, T0), ("pa", "pb", "pc"), groups):
                            evac_probs(bank, what, u, t, lo, hi)
                    elif k == "F2":
                        full(T0, "gate", u)
                        inc(act.activation(th[:, u % 2, 2 * GW:3 * GW], T0.tile[:, 0:GW], Tanh, scale=0.5), "tanh_F2b")

                def phase1_extra(k, u, t):
                    if k == "F0":
                        full(X, "pickT", u)
                        act.activation(ohT[:, t, :], X.tile[0:E0, 0:P], Copy)
                        act.activation(ohTb[:, u % 2, :], X.tile[0:E0, 0:P], Copy).then_inc(X.drained, 1)
                    elif k == "F1":
                        full(T0, "gate", u)
                        inc(act.activation(th[:, u % 2, 0:FB], T0.tile[:, :], Tanh, scale=sc[:, t, 3:4]), "tanh_F1")
                    elif k == "F3":
                        full(X, "projT", u)
                        act.activation(pjT[:, u % 2, :], X.tile[0:PROJ, 0:P], Copy).then_inc(X.drained, 1)

                def phase0_project(k, u, t):
                    if k == "A2":
                        full(X, "q", u)
                        act.wait_ge(s_tg, 2)
                        act.activation(qT[:, u % 2, :], X.tile[:, 0:P], Ident, bias=sq2[:, :], scale=float(DH) ** -0.5)\
                           .then_inc(X.drained, 1)
                    elif k == "A3":
                        full(X, "q", u)
                        act.activation(qT[:, u % 2, :], X.tile[:, 0:P], Copy, scale=float(DH) ** -0.5)\
                           .then_inc(X.drained, 1)
                    elif k == "F2":
                        full(X, "gate", u)
                        act.activation(sg[:, t, :], X.tile[:, 0:E2], Tanh, scale=0.5).then_inc(X.drained, 1)

                def phase1(k, u, t):
                    if k in ("A0", "A2", "A3"):
                        drained(S, "scores", u)
                        inc(act.activation(pr[:, u % U % 3, :], pr[:, u % U % 3, :], Exp), "probs_" + k)
                    elif k == "A1":
                        wait("nmax_A1", t, u)
                        act.activation(pr[:, u % U % 3, 0:CTX], S.tile[:, 0, 0:CTX], Exp, bias=sc[:, t, 0:1],
                                       accum_out=sc[:, t, 1:2]).then_inc(S.drained, 1)
                    elif k == "F0":
                        wait("centred_F0", t, u)
                        inc(act.activation(ex[:, t, :], lg[:, t, 0:E0], Exp, accum_out=sc[:, t, 1:2]), "expsum_F0")

                def phase1_first(k, u, t):
                    if k == "F2":
                        full(S, "gu", u)
                        inc(act.activation(th[:, u % 2, 0:2 * GW].rearrange("p (b n) -> p b n", b=2),
                                           S.tile[:, 0:2, 0:GW], Tanh, scale=0.5), "tanh_F2a")

                def phase2_end(k, u, t):
                    if k == "F3":
                        wait("centred_F3", t, u)
                        inc(act.activation(ex[:, t, 0:4], lg[:, t, 0:4], Exp, accum_out=sc[:, t, 1:2]), "expsum_F3")

                order = ((phase1_first, 1), (phase3, 3), (phase0, 0), (phase2, 2), (phase1_extra, 1),
                         (phase0_project, 0), (phase1, 1), (phase2_end, 2), ("prepare", 0))
                for work, v in steps(order, first, U + 3, next_only=first == U):
                    if work == "prepare":
                        for do in prepare[v]:
                            do()
                    else:
                        work(UNITS[v % U][0], v, UNITS[v % U][1])

            one_pass(-1, U)
            with act.Fori(0, B) as it:
                one_pass(it, 3)

        @block.gpsimd
        def _(pool):
            def carry():
                pool.sem_inc(s_carry, 1)

            pool.memset(half[:, :], -0.5).then_inc(s_const, 1)
            pool.wait_ge(loaded["base"], 16)
            for V in (V2, V3):
                pool.tensor_copy(V[:, :, :, DH:VW].rearrange("p n h o -> p n (h o)"),
                                 W["ones_col"].rearrange("p (n h) -> p n h", h=H)).then_inc(s_const, 1)
            pool.wait_ge(s_const, 9)

            def context(it):
                full, free, drained, wait = helpers(pool, it)
                def ctx_rstd():
                    wait("ctx_var", 0)
                    inc(pool.tensor_tensor(crs[:, :], cve[:, :], half[0:CTX, 0:1], ALU.pow), "ctx_rstd")

                def ctx_copy():
                    pool.wait_ge(s_c_loaded, it * 48 + 96)
                    carry()
                    pool.tensor_copy(ctx[:, :], ctx_st[:, :])
                    inc(pool.tensor_copy(ctxT[:, :], ctxT_st[:, :]), "ctx_copied")

                def expand(dst, src):
                    inc(pool.tensor_tensor(dst, src[:, :].unsqueeze(1).broadcast_to([P, H, CTX]),
                                           W["delta"].unsqueeze(2).broadcast_to([P, H, CTX]), ALU.mult), "expanded")

                def k2_():
                    drained(X, "kv")
                    expand(K2[:, :, :], k2)
                    ctx_copy()
                return {13: (ctx_rstd,), 14: (k2_,), 15: (lambda: expand(V2x, v2),),
                        16: (lambda: expand(K3[:, :, :], k3),), 17: ()}, (ctx_rstd, ctx_copy)

            for part in context(-1)[1]:
                part()
            pool.wait_ge(X.drained, X.prelude.index("simnorm") + 2)
            pool.tensor_tensor(sim_sq[:, :], sim_sq[:, :], half[0:PROJ, 0:1].broadcast_to([PROJ, 4 + R]), ALU.pow)\
                .then_inc(s_simpow, 1)

            def one_pass(it, first):
                full, free, drained, wait = helpers(pool, it)
                prepare = context(it)[0]

                def phase0(k, u, t):
                    wait("var_ready", u)
                    inc(pool.tensor_tensor(rstd[:, t:t + 1], ve[:, t:t + 1], half[:, 0:1], ALU.pow), "rstd_ready")

                def weigh(u, t, e0, e1):
                    h = hh[:, u % U % 3, e0 * F2W:e1 * F2W].rearrange("p (e f) -> p e f", f=F2W)
                    return pool.tensor_tensor(h, h, comb[:, t, e0:e1].unsqueeze(2).broadcast_to([P, e1 - e0, F2W]),
                                              ALU.mult)

                def phase1(k, u, t):
                    if k == "F3":
                        wait("ss_ready", t, u)
                        inc(pool.tensor_tensor(sc[:, t, 5:6], sc[:, t, 4:5], half[:, 0:1], ALU.pow), "rn_ready")
                    elif k == "F2":
                        drained(S, "gu", u)
                        wait("comb_ready", t, u)
                        inc(weigh(u, t, 0, 12), "weighted_F2a")

                def phase2(k, u, t):
                    if k == "A0":
                        wait("inv0", t, u)
                        p = pr[:, u % U % 3, :].rearrange("p (h c) -> p h c", c=CTX)
                        inc(pool.tensor_tensor(p, p, ri[:, t, :].unsqueeze(2).broadcast_to([P, H, CTX]), ALU.mult),
                            "probs0")
                    elif k == "F2":
                        drained(T1, "up", u)
                        inc(weigh(u, t, 12, E2), "weighted_F2b")

                order = ((phase0, 0), (phase2, 2), (phase1, 1), ("prepare", 0))
                for work, v in steps(order, first, U + 3, next_only=first == U):
                    if work == "prepare":
                        for do in prepare[v]:
                            do()
                    else:
                        work(UNITS[v % U][0], v, UNITS[v % U][1])

            one_pass(-1, U)
            with pool.Fori(0, B) as it:
                one_pass(it, 3)

        @block.vector
        def _(dve):
            steps_done = [0]

            def link(ins):
                steps_done[0] += 1
                ins.then_inc(s_dve, 1)
                dve.wait_ge(s_dve, at[0] * DVE_STEPS + (BEFORE_LOOP[0] + steps_done[0]) if at else steps_done[0])

            def carry():
                dve.sem_inc(s_carry, 1)

            at, BEFORE_LOOP = [], [0]
            tanh_gate = {k: tg[:, GATE[k]:GATE[k] + 1] for k in BLOCKS}
            for bank in (S, O):
                dve.sem_inc(bank.drained, 1)
            dve.memset(ones[:, :], 1.0).then_inc(s_const, 1)
            dve.memset(ones_b[:, :], 1.0).then_inc(s_const, 1)
            dve.memset(k0[:, :, :], 0.0).then_inc(s_const, 1)
            dve.memset(v0[:, :, :], 0.0).then_inc(s_const, 1)
            dve.wait_ge(loaded["base"], 16)
            dve.tensor_copy(ident_b[:, :], ident).then_inc(s_const, 1)
            dve.tensor_copy(pick_row[:, :, :], W["ident"][0:E0, 0:E0].unsqueeze(2).broadcast_to([E0, E0, P]))\
               .then_inc(s_const, 1)

            def context(it):
                full, free, drained, wait = helpers(dve, it)
                dve.wait_ge(s_c_loaded, it * 48 + 96)
                link(dve.bn_stats(cstat[:, :], ctx_st[:, :]))
                carry()
                link(dve.bn_aggr(cmv[:, :], cstat[:, :]))
                inc(dve.tensor_scalar(cve[:, :], cmv[:, 1:2], LN_EPS, None, ALU.add), "ctx_var")
                link(dve.tensor_scalar(seen[:, :], mask_st[:, :], 0.0, None, ALU.not_equal))
                link(dve.tensor_reduce(anyseen[:, 0:1], seen[:, :], AX.X, ALU.max))
                link(dve.reciprocal(anyseen[:, 1:2], anyseen[:, 0:1]))
                inc(dve.tensor_scalar(mask_row[:, :, :], mask_st[0:1, :].unsqueeze(1).broadcast_to([1, HB, CTX]),
                                      0.0, MASKED, ALU.is_equal, ALU.mult), "mask_ready")
                wait("ctx_rstd", 0)
                inc(dve.tensor_scalar(ctxn[:, :], ctx_st[:, :], cmv[:, 0:1], crs[:, 0:1], ALU.subtract, ALU.mult),
                    "ctx_norm")
                inc(dve.tensor_tensor(anyseen[:, 2:3], anyseen[:, 0:1], anyseen[:, 1:2], ALU.mult), "ctx_used")

            context(-1)
            dve.wait_ge(loaded["tern"], 16)
            dve.tensor_reduce(wt_sum[:, :], W["wt"].rearrange("p (w n) -> p w n", w=3), AX.X, ALU.add,
                              apply_absolute_value=True).then_inc(s_prel, 1)
            dve.wait_ge(loaded["low"], 16)
            dve.tensor_tensor(sim_sq[:, :], W["sim"], W["sim"], ALU.mult).then_inc(s_prel, 1)
            dve.tensor_scalar(sim_s[:, :], W["temp"], CLAMP, None, ALU.min).then_inc(s_prel, 1)
            full, free, drained, wait = helpers(dve, -1)
            full(X, "wmean")
            dve.tensor_scalar(wt_mean[:, :], X.tile[:, 0:3], 1.0 / (FB * D), 1e-5, ALU.mult, ALU.max)\
               .then_inc(X.drained, 1)
            drained(X, "wmean")
            link(dve.reciprocal(wt_inv[:, :], wt_mean[:, :]))
            for n in range(3):
                cols = slice(n * FB, (n + 1) * FB)
                last = dve.tensor_scalar(wt_r[:, cols], W["wt"][:, cols], wt_inv[:, n:n + 1], MAGIC, ALU.mult, ALU.add)
            link(last)
            link(dve.tensor_scalar(wt_r, wt_r, -MAGIC, 1.0, ALU.add, ALU.min))
            dve.tensor_scalar(wt_q[:, :], wt_r, -1.0, None, ALU.max).then_inc(s_quant, 1)
            dve.wait_ge(s_tg, 1)
            dve.tensor_scalar(tgh[:, :], tanh_gate.get("F2", tg[:, 6:7]), 0.5, None, ALU.mult)
            dve.tensor_scalar(wt_c[:, 0:1], wt_mean[:, 0:1], 0.5 / 127.0, None, ALU.mult)
            dve.tensor_scalar(wt_c[:, 1:2], wt_mean[:, 0:1], wt_mean[:, 1:2], 0.5 / 127.0 ** 2, ALU.mult, ALU.mult)
            dve.tensor_scalar(wt_c[:, 2:3], wt_mean[:, 2:3], tg[:, 5:6], 1.0 / 127.0, ALU.mult, ALU.mult)
            dve.wait_ge(loaded["att23"], 16)
            dve.tensor_scalar(sq2[:, :], W["b2qkv"][:, 0:1], float(DH) ** -0.5, None, ALU.mult).then_inc(s_tg, 1)
            full(X, "simnorm")
            dve.tensor_scalar(sim_sq[:, :], X.tile[0:PROJ, 0:4 + R], 1e-24, None, ALU.max).then_inc(X.drained, 1)
            dve.wait_ge(s_simpow, 1)
            link(dve.tensor_tensor(sim_n[:, :], W["sim"], sim_sq[:, :], ALU.mult))
            dve.wait_ge(s_temp, 1)
            dve.tensor_scalar(sim_n[:, :], sim_n[:, :], sim_s[:, 0:1], None, ALU.mult).then_inc(s_prel, 1)
            dve.wait_ge(s_prel, 4)
            dve.wait_ge(s_const, 9)
            dve.wait_ge(s_quant, 1)

            def one_pass(it, first):
                full, free, drained, wait = helpers(dve, it)

                def now(k, t):
                    return x_st[:, t, :] if k == "A0" else x[:, t, :]

                def phase0_stats(k, u, t):
                    if k == "A0" and t == 0:
                        dve.wait_ge(s_x_loaded, it * 16 + (u // U + 1) * 16)
                    link(dve.bn_stats(stat[:, :], now(k, t)))
                    carry()
                    link(dve.bn_aggr(mv[:, t, :], stat[:, :]))
                    a, b_ = (1.0 + LN_EPS, LN_EPS * LN_EPS) if k == "A0" else (1.0, LN_EPS)
                    inc(dve.tensor_scalar(ve[:, t:t + 1], mv[:, t, 1:2], a, b_, ALU.mult, ALU.add), "var_ready")

                def phase0_norm(k, u, t):
                    wait("rstd_ready", u)
                    norm = dve.tensor_scalar(xh[:, t, :], now(k, t), mv[:, t, 0:1], rstd[:, t:t + 1],
                                             ALU.subtract, ALU.mult)
                    if k != "F1":
                        inc(norm, "xh_ready")
                        return
                    link(norm)
                    link(dve.tensor_reduce(sc[:, t, 4:5], xh[:, t, :], AX.X, ALU.max, apply_absolute_value=True))
                    link(dve.tensor_scalar(sc[:, t, 4:5], sc[:, t, 4:5], 1e-5, None, ALU.max))
                    link(dve.reciprocal(sc[:, t, 5:6], sc[:, t, 4:5]))
                    link(dve.tensor_scalar(sc[:, t, 5:6], sc[:, t, 5:6], 127.0, None, ALU.mult))
                    dve.tensor_scalar(sc[:, t, 3:4], sc[:, t, 4:5], wt_c[:, 0:1], None, ALU.mult)
                    dve.tensor_scalar(sc[:, t, 6:7], sc[:, t, 4:5], sc[:, t, 4:5], wt_c[:, 1:2], ALU.mult, ALU.mult)
                    link(dve.tensor_scalar(xhq[:, u % 2, :], xh[:, t, :], sc[:, t, 5:6], MAGIC, ALU.mult, ALU.add))
                    inc(dve.tensor_scalar(xq[:, t, :], xhq[:, u % 2, :], -MAGIC, 127.0, ALU.add, ALU.min), "xh_ready")

                def residual(k, t, src, scale, out=None):
                    return dve.scalar_tensor_tensor(out=x[:, t, :] if out is None else out, in0=src, scalar=scale,
                                                    in1=now(k, t), op0=ALU.mult, op1=ALU.add)

                def inverse_sum(k, t):
                    link(dve.reciprocal(sc[:, t, 2:3], sc[:, t, 1:2]))
                    link(dve.tensor_scalar(sc[:, t, 3:4], sc[:, t, 2:3], tanh_gate[k], None, ALU.mult))

                def phase3_early(k, u, t):
                    if k == "F0":
                        wait("expsum_F0", t, u)
                        inverse_sum(k, t)
                        link(dve.tensor_scalar(ri[:, t, 0:E0], oh[:, t, 0:E0], sc[:, t, 3:4], None, ALU.mult))
                        full(O, "bias", u)
                        residual(k, t, O.tile[:, 0:D], sc[:, t, 3:4]).then_inc(O.drained, 1)
                    elif k == "A1":
                        drained(S, "scores", u)
                        inverse_sum(k, t)
                        full(O, "out", u)
                        residual(k, t, O.tile[:, 0:D], sc[:, t, 3:4]).then_inc(O.drained, 1)
                        drained(O, "out", u)
                    elif k == "F1":
                        full(O, "out", u)
                        residual(k, t, O.tile[:, 0:D], sc[:, t, 7:8]).then_inc(O.drained, 1)
                        drained(O, "out", u)
                    elif k in ("A2", "A3"):
                        full(O, "values", u)
                        o = O.tile[:, 0:H * VW].rearrange("p (h v) -> p h v", v=VW)
                        link(dve.reciprocal(ri[:, t, :], o[:, :, DH:VW].rearrange("p h o -> p (h o)")))
                        dve.tensor_tensor(cv[:, u % 2, :].rearrange("p (h v) -> p h v", v=DH), o[:, :, 0:DH],
                                          ri[:, t, :].unsqueeze(2).broadcast_to([P, H, DH]), ALU.mult)\
                           .then_inc(O.drained, 1)

                def phase1(k, u, t):
                    if k in ("A0", "A2", "A3"):
                        full(S, "scores", u)
                        s4 = S.tile[:, :, 0:SB].rearrange("p b (h c) -> p b h c", c=CTX)
                        link(dve.tensor_reduce(mx[:, t, :].rearrange("p (b h) -> p b h", b=4), s4, AX.X, ALU.max))
                        m4 = mx[:, t, :].rearrange("p (b h) -> p b h", b=4).unsqueeze(3)
                        dve.tensor_tensor(pr[:, u % U % 3, :].rearrange("p (b h c) -> p b h c", b=4, c=CTX), s4,
                                          m4.broadcast_to([P, 4, HB, CTX]), ALU.subtract).then_inc(S.drained, 1)
                    elif k == "A1":
                        full(S, "scores", u)
                        inc(dve.tensor_reduce(sc[:, t, 0:1], S.tile[:, 0, 0:CTX], AX.X, ALU.max, negate=True),
                            "nmax_A1")
                    elif k == "F0":
                        full(X, "logits", u)
                        dve.tensor_tensor(lg[:, t, 0:E0], X.tile[:, 0:E0], W["br"], ALU.add).then_inc(X.drained, 1)
                        drained(X, "logits", u)
                        link(dve.tensor_reduce(sc[:, t, 0:1], lg[:, t, 0:E0], AX.X, ALU.max, negate=True))
                        inc(dve.tensor_scalar(lg[:, t, 0:E0], lg[:, t, 0:E0], sc[:, t, 0:1], None, ALU.add),
                            "centred_F0")
                        wait("centred_F0", t, u)
                        link(dve.scalar_tensor_tensor(out=tt[:, t, 0:E0], in0=lg[:, t, 0:E0], scalar=0.0,
                                                      in1=W["desc0"], op0=ALU.is_ge, op1=ALU.mult))
                        link(dve.tensor_reduce(sc[:, t, 5:6], tt[:, t, 0:E0], AX.X, ALU.max))
                        inc(dve.tensor_scalar(oh[:, t, 0:E0], tt[:, t, 0:E0], sc[:, t, 5:6], None, ALU.is_equal),
                            "pick_ready")
                    elif k == "F2":
                        wait("tanh_F2a", t, u)
                        def two(a, n):
                            return a[:, u % n, 0:2 * GW].rearrange("p (b n) -> p b n", b=2)

                        link(dve.scalar_tensor_tensor(out=two(g1, 2), in0=two(th, 2), scalar=1.0, in1=S.tile[:, 0:2, 0:GW],
                                                      op0=ALU.add, op1=ALU.mult))
                        dve.tensor_tensor(two(hh, 3), two(g1, 2), S.tile[:, 2:4, 0:GW], ALU.mult).then_inc(S.drained, 1)
                    elif k == "F3":
                        full(S, "all", u)
                        inc(dve.tensor_tensor(pj[:, t, :], S.tile[:, 0, 0:PROJ], W["bp"], ALU.add), "pj_ready")
                        dve.tensor_copy(dn[:, t, :], S.tile[:, 0, PROJ:PROJ + R])
                        residual(k, t, S.tile[:, 0, PROJ + R:PROJ + R + D], tanh_gate[k]).then_inc(S.drained, 1)
                        wait("pj_ready", t, u)
                        link(dve.tensor_tensor(pj2[:, :], pj[:, t, :], pj[:, t, :], ALU.mult))
                        link(dve.tensor_reduce(sc[:, t, 4:5], pj2[:, :], AX.X, ALU.add))
                        inc(dve.tensor_scalar(sc[:, t, 4:5], sc[:, t, 4:5], 1e-24, None, ALU.max), "ss_ready")

                def ranks(rank, work, v, n, tri):
                    vj = v.unsqueeze(1).broadcast_to([P, n, n])
                    vi = v.unsqueeze(2).broadcast_to([P, n, n])
                    dve.tensor_tensor(work[:, :, 0, :], vj, vi, ALU.is_gt)
                    link(dve.tensor_tensor(work[:, :, 1, :], vj, vi, ALU.is_equal))
                    link(dve.tensor_tensor(work[:, :, 1, :], work[:, :, 1, :],
                                           tri.rearrange("p (i j) -> p i j", i=n), ALU.mult))
                    link(dve.tensor_reduce(rank, work[:, :, :, :], AX.XY, ALU.add))

                def route(u, t):
                    drained(X, "gate", u)
                    link(dve.tensor_scalar(sig[:, t, :], sg[:, t, :], 0.5, 0.5, ALU.mult, ALU.add))
                    s4 = sig[:, t, :].rearrange("p (g e) -> p g e", g=4)
                    dve.tensor_tensor(pairs[:, :, 0:3], s4[:, :, 0:3], s4[:, :, 1:4], ALU.add)
                    dve.tensor_tensor(pairs[:, :, 3:5], s4[:, :, 0:2], s4[:, :, 2:4], ALU.add)
                    link(dve.tensor_tensor(pairs[:, :, 5:6], s4[:, :, 0:1], s4[:, :, 3:4], ALU.add))
                    link(dve.tensor_reduce(gs[:, :], pairs[:, :, :], AX.X, ALU.max))
                    ranks(rank4[:, :], cmp4, gs[:, :], 4, W["tri4"])
                    link(dve.tensor_scalar(allow[:, :], rank4[:, :], 2.0, None, ALU.is_lt))
                    link(dve.tensor_scalar(allow1[:, :], allow[:, :], -1.0, None, ALU.add))
                    m4 = msk[:, :].rearrange("p (g e) -> p g e", g=4)
                    link(dve.tensor_tensor(m4, s4, allow[:, :].unsqueeze(2).broadcast_to([P, 4, 4]), ALU.mult))
                    link(dve.tensor_tensor(m4, m4, allow1[:, :].unsqueeze(2).broadcast_to([P, 4, 4]), ALU.add))
                    ranks(rank16[:, :], cmp16, msk[:, :], E2, W["tri16"])
                    link(dve.scalar_tensor_tensor(out=picked[:, :], in0=rank16[:, :], scalar=4.0, in1=sig[:, t, :],
                                                  op0=ALU.is_lt, op1=ALU.mult))
                    link(dve.tensor_reduce(psc[:, 0:1], picked[:, :], AX.X, ALU.add))
                    link(dve.tensor_scalar(psc[:, 1:2], psc[:, 0:1], 1e-6, None, ALU.add))
                    link(dve.reciprocal(psc[:, 2:3], psc[:, 1:2]))
                    inc(dve.tensor_scalar(comb[:, t, :], picked[:, :], psc[:, 2:3], None, ALU.mult), "comb_ready")

                def silu_times_up(k, u, t, cols, gate, up, factor):
                    n = gate.free_size()
                    dve.scalar_tensor_tensor(out=g1[:, u % 2, cols], in0=th[:, u % 2, cols], scalar=1.0, in1=gate,
                                             op0=ALU.add, op1=ALU.mult).then_inc(T0.drained, 1)
                    drained(T0, "gate", u)
                    full(T1, "up", u)
                    dve.scalar_tensor_tensor(out=hh[:, u % U % 3, cols], in0=g1[:, u % 2, cols], scalar=factor, in1=up,
                                             op0=ALU.mult, op1=ALU.mult).then_inc(T1.drained, 1)

                def phase2(k, u, t):
                    if k == "A0":
                        wait("probs_A0", t, u)
                        link(dve.tensor_reduce(rs[:, t, :], pr[:, u % U % 3, :].rearrange("p (h c) -> p h c", c=CTX),
                                               AX.X, ALU.add))
                        inc(dve.reciprocal(ri[:, t, :], rs[:, t, :]), "inv0")
                        wait("tanh_A0", t, u)
                        silu_times_up(k, u, t, slice(0, FF0), T0.tile[:, :], T1.tile[:, :], 0.5)
                    elif k == "F2":
                        wait("tanh_F2b", t, u)
                        silu_times_up(k, u, t, slice(2 * GW, 3 * GW), T0.tile[:, 0:GW], T1.tile[:, 0:GW], 1.0)
                    elif k == "F3":
                        full(X, "logits", u)
                        wait("rn_ready", t, u)
                        dve.tensor_scalar(lg[:, t, :], X.tile[:, 0:4 + R], sc[:, t, 5:6], None, ALU.mult)\
                           .then_inc(X.drained, 1)
                        drained(X, "logits", u)
                        link(dve.tensor_reduce(sc[:, t, 0:1], lg[:, t, 0:4], AX.X, ALU.max, negate=True))
                        inc(dve.tensor_scalar(lg[:, t, :], lg[:, t, :], sc[:, t, 0:1], None, ALU.add), "centred_F3")
                        wait("centred_F3", t, u)
                        link(dve.scalar_tensor_tensor(out=tt[:, t, :], in0=lg[:, t, :], scalar=0.0, in1=W["desc3"],
                                                      op0=ALU.is_ge, op1=ALU.mult))
                        link(dve.tensor_reduce(sc[:, t, 6:7], tt[:, t, 0:4], AX.X, ALU.max))
                        inc(dve.scalar_tensor_tensor(out=dm[:, t, :], in0=tt[:, t, 4:4 + R], scalar=sc[:, t, 6:7],
                                                     in1=dn[:, t, :], op0=ALU.is_equal, op1=ALU.mult), "dm_ready")

                def phase3(k, u, t):
                    if k == "F0":
                        drained(O, "bias", u)
                        for e in range(E0):
                            bank, what = (T0, "ya") if e < 4 else (T1, "yb")
                            if e % 4 == 0:
                                full(bank, what, u)
                            r = residual(k, t, bank.tile[:, e % 4 * D:(e % 4 + 1) * D], ri[:, t, e:e + 1])
                            if e % 4 == 3:
                                r.then_inc(bank.drained, 1)
                                drained(bank, what, u)
                            else:
                                link(r)
                        return
                    if k in ("A1", "F1"):
                        return
                    scale = tgh[:, 0:1] if k == "F2" else tanh_gate[k]
                    if k == "F3":
                        wait("expsum_F3", t, u)
                        inverse_sum(k, t)
                        scale = sc[:, t, 3:4]
                    bank = X if k in ("A2", "A3") else O
                    if k == "F3" and t == 0:
                        dve.wait_ge(s_stored, (it + 1) * (16 * TILES))
                    full(bank, "out", u)
                    residual(k, t, bank.tile[:, 0:D], scale, y[:, t, :] if k == "F3" else None).then_inc(bank.drained, 1)
                    drained(bank, "out", u)

                def phase1_extra(k, u, t):
                    if k == "F2":
                        route(u, t)
                    elif k == "F1":
                        wait("tanh_F1", t, u)
                        silu_times_up(k, u, t, slice(0, FB), T0.tile[:, :], T1.tile[:, :], 1.0)
                        drained(T1, "up", u)
                        h = hh[:, u % U % 3, 0:FB]
                        link(dve.tensor_reduce(sc[:, t, 8:9], h, AX.X, ALU.max, apply_absolute_value=True))
                        link(dve.tensor_scalar(sc[:, t, 8:9], sc[:, t, 8:9], sc[:, t, 6:7], 1e-5, ALU.mult, ALU.max))
                        link(dve.reciprocal(sc[:, t, 9:10], sc[:, t, 8:9]))
                        link(dve.tensor_scalar(sc[:, t, 9:10], sc[:, t, 9:10], sc[:, t, 6:7], 127.0, ALU.mult, ALU.mult))
                        dve.tensor_scalar(sc[:, t, 7:8], sc[:, t, 8:9], wt_c[:, 2:3], None, ALU.mult)
                        link(dve.tensor_scalar(h, h, sc[:, t, 9:10], MAGIC, ALU.mult, ALU.add))
                        inc(dve.tensor_scalar(hq[:, u % 2, :], h, -MAGIC, 127.0, ALU.add, ALU.min), "hq_ready")

                def phase1_late(k, u, t):
                    if k == "F0":
                        full(S, "masks", u)
                        dve.tensor_tensor(xm[:, u % 2, :, :].rearrange("p (b e) n -> p b e n", b=2),
                                          S.tile[:, 0:2, :].rearrange("p b (e n) -> p b e n", n=P),
                                          xT[:, t, :].unsqueeze(1).unsqueeze(1).broadcast_to([P, 2, 4, P]), ALU.mult)\
                           .then_inc(S.drained, 1)

                order = ((phase0_stats, 0), (phase3_early, 3), (phase0_norm, 0), (phase1, 1), (phase2, 2),
                         (phase1_extra, 1), (phase3, 3), (phase1_late, 1), ("prepare", 0))
                for work, v in steps(order, first, U + 3, next_only=first == U):
                    if work != "prepare":
                        work(UNITS[v % U][0], v, UNITS[v % U][1])
                    elif v == min(PREPARE):
                        context(it)

            one_pass(-1, U)
            BEFORE_LOOP[0], steps_done[0] = steps_done[0], 0
            with dve.Fori(0, B) as it:
                at.append(it)
                one_pass(it, 3)
            assert steps_done[0] == DVE_STEPS, steps_done[0]


def _columns(a, rows=P):
    return np.broadcast_to(np.asarray(a).reshape(1, -1), (rows, a.size))


def _pack(parts, given):
    out = np.zeros((P, sum(c for _, _, c in parts)), np.float32)
    at = 0
    for name, rows, cols in parts:
        out[0:rows, at:at + cols] = np.asarray(given[name]).reshape(rows, cols)
        at += cols
    return out


def kernel(**inputs):
    import concourse.bacc as _bacc
    from concourse.bass_utils import run_bass_kernel_spmd as _run

    a = {k: np.asarray(v) for k, v in inputs.items()}
    g = {}
    rows = np.arange(NCH * P)
    g["ident"] = np.eye(P)
    g["delta"] = np.arange(P)[:, None] // DH == np.arange(H)[None, :]
    g["ones_col"] = (rows.reshape(NCH, P, 1) // CTX == np.arange(H)).transpose(1, 0, 2)
    g["desc0"] = _columns(np.arange(E0, 0, -1))
    expert = [e for e, r in enumerate(RANKS) for _ in range(r)]
    cols3 = list(range(4)) + expert
    g["desc3"] = _columns(4 - np.array(cols3))
    g["tri4"] = _columns(np.tril(np.ones((4, 4)), -1))
    g["tri16"] = _columns(np.tril(np.ones((E2, E2)), -1))
    g["gates"] = np.concatenate([_columns(a["g_xattn"]), _columns(a["g_ffn"])], axis=1)
    g["ln_gamma"] = np.stack([a["L0_xattn_gamma"], a["L0_xattn_ctx_gamma"]], axis=1)
    wkv = a["L0_xattn_Wkv"]
    g["wk0"] = np.concatenate([wkv[:, :DH0]] * 2, axis=1)
    g["wv0"] = np.concatenate([wkv[:, DH0:]] * 2, axis=1)
    g["wq0"] = a["L0_xattn_Wq"].T.reshape(8, P, D).transpose(1, 0, 2)
    g["wo0"] = a["L0_xattn_Wout"].reshape(8, P, D).transpose(1, 0, 2)
    g["wff1"] = a["L0_xattn_Wff1"]
    g["wff2"] = a["L0_xattn_Wff2"].reshape(4, P, D).transpose(1, 0, 2)
    g["wr"] = a["L0_ffn_Wr"]
    g["br"] = _columns(a["L0_ffn_br"])
    g["w1"] = a["L0_ffn_W1"].transpose(1, 0, 2)
    g["b1"] = a["L0_ffn_b1"]
    g["w2"] = a["L0_ffn_W2"].reshape(E0, 2, P, D).transpose(2, 1, 0, 3)
    g["b2"] = a["L0_ffn_b2"]
    g["wt"] = np.concatenate([a["L1_ffn_w_gate"].T, a["L1_ffn_w_up"].T,
                              a["L1_ffn_w_down"].T.reshape(4, P, D).transpose(1, 0, 2).reshape(P, FB)], axis=1)
    for n, name in (("wq2", "Wq"), ("wk2", "Wk"), ("wv2", "Wv")):
        g[n] = a["L2_xattn_" + name].transpose(1, 0, 2)
    g["b2qkv"] = np.stack([a["L2_xattn_b" + n].reshape(P) for n in "qkv"], axis=1)
    g["wo2"], g["bo2"] = a["L2_xattn_Wo"], a["L2_xattn_bo"]
    g["wg"] = a["L2_ffn_w_gate"].T
    g["w13"] = np.concatenate([m for e, s in (("w1_e", "w1_s"), ("w3_e", "w3_s"))
                               for m in (a["L2_ffn_" + e].reshape(E2 * F2W, D).T, a["L2_ffn_" + s].T)], axis=1)
    g["w2s"] = np.concatenate([a["L2_ffn_w2_e"].transpose(0, 2, 1).reshape(8, P, D),
                               a["L2_ffn_w2_s"].T[None]]).transpose(1, 0, 2)
    by_head = np.arange(D).reshape(DH, H).T.reshape(-1)
    g["wq3"], g["wk3"] = a["L3_xattn_Wq"][by_head].T, a["L3_xattn_Wk"][by_head].T
    g["wo3"] = a["L3_xattn_Wo"][:, by_head].T
    g["w3"] = np.concatenate([a["L3_ffn_Wp"].T] + [a[f"L3_ffn_Wd{i}"].T for i in range(4)] + [a["L3_ffn_W"].T], axis=1)
    g["bp"] = _columns(a["L3_ffn_bp"])
    g["sim"] = a["L3_ffn_sim"][:, cols3]
    g["temp"] = _columns(a["L3_ffn_temp"], PROJ)
    g["wu"] = np.concatenate([a[f"L3_ffn_Wu{i}"].T for i in range(4)], axis=0)

    nc = _bacc.Bacc("TRN2", target_bir_lowering=False, num_devices=1)
    arrays = {"x": a["x"], "ctx": a["ctx_1024"], "ctxT": np.ascontiguousarray(a["ctx_1024"].transpose(0, 2, 1)),
              "mask": np.ascontiguousarray(np.broadcast_to(a["mask_BxS2_ik0"][:, None, :], (B, P, CTX)))}
    for pack, parts in PACKS.items():
        arrays["w_" + pack] = _pack(parts, g)
    aps = {n: nc.dram_tensor("in_" + n, v.shape, mybir.dt.from_np(v.dtype), kind="ExternalInput").ap()
           for n, v in arrays.items()}
    out = nc.dram_tensor("out_0", (B, SEQ, D), F32, kind="ExternalOutput").ap()
    gated_flamingo(nc, aps["x"], aps["ctx"], aps["ctxT"], aps["mask"], {p: aps["w_" + p] for p in PACKS}, out)
    r = _run(nc, [{"in_" + n: v for n, v in arrays.items()}], core_ids=[0])
    return r.results[0]["out_0"]
```

```python
from contextlib import ExitStack

import numpy as np
import concourse.bass as bass
from concourse import mybir

F32, BF16, I32 = mybir.dt.float32, mybir.dt.bfloat16, mybir.dt.int32
ALU, ACT, AX = mybir.AluOpType, mybir.ActivationFunctionType, mybir.AxisListType

P = 128
D = 128
B, SEQ, CTX = 4, 512, 77
TILES = SEQ // P
H = 16
HC = H * CTX
HB = H // 4
SB = HB * CTX
NCH = -(-HC // P)
LASTROWS = HC - (NCH - 1) * P
DH0 = 64
DH = D // H
VW = DH + 1
FF0 = 512
E0, H0 = 8, 256
FB = 512
E2, F2W, FS2 = 16, 64, 128
GW = 384
RANKS = (1, 2, 4, 8)
R = sum(RANKS)
PROJ = 32
LN_EPS = 1e-5
MASKED = -1e30
MAGIC = 1.5 * 2.0 ** 23
TAKEN = -8.0
CLAMP = float(np.log(1.0 / 0.01))

DVE_STEPS = 289
BLOCKS = ("A0", "F0", "A1", "F1", "A2", "F2", "A3", "F3")
NB = len(BLOCKS)
GATE = {k: (int(k[1]) if k[0] == "A" else 4 + int(k[1])) for k in BLOCKS}
UNITS = [(BLOCKS[u // TILES], u % TILES) for u in range(NB * TILES)]

PE_PARTS = (("first", 1), ("late_transpose", 3), ("transpose", 2), ("xT_early", 0), ("late_rest", 3),
            ("rest", 2), ("middle", 2), ("extra", 1), ("xT", 0), ("output", 3), ("query", 0), ("values", 2),
            ("spread", 1), ("project", 0), ("prepare", 0))
FILLS = {
    "A0": {"first": ("S scores",), "middle": ("T0 gate", "T1 up"),
           "late_transpose": ("T0 hT", "T1 pa"), "late_rest": ("T0 pb", "T1 pc"), "output": ("O out",)},
    "F0": {"project": ("X logits",), "extra": ("X pickT",), "spread": ("S masks",),
           "middle": ("O hidden",), "late_transpose": ("O bias", "T0 ya", "T1 yb")},
    "A1": {"first": ("S scores",), "middle": ("T0 pT",), "values": ("O out",)},
    "F1": {"first": ("S gu",), "middle": ("T0 hT",), "values": ("O out",)},
    "A2": {"query": ("X q",), "first": ("S scores",),
           "transpose": ("T0 pa", "T1 pb"), "rest": ("T0 pc",), "values": ("O values",),
           "late_transpose": ("X vT",), "output": ("T1 out",)},
    "F2": {"project": ("X gate",), "first": ("S gu",), "middle": ("T0 gate", "T1 up"),
           "late_transpose": ("T0 ha", "T1 hb"), "late_rest": ("T0 hc",), "output": ("O out",)},
    "F3": {"first": ("S all",), "extra": ("X projT",), "middle": ("X logits",),
           "late_transpose": ("X downT",), "output": ("O out",)},
}
FILLS["A3"] = FILLS["A2"]
XT_EARLY = ("A2", "A3", "F2", )
PREPARE = {12: ("X cT",),
           13: ("X kv", "X kv0"),
           14: ("S a",),
           15: ("S b",),
           16: ("T0 va", "T1 vb", "T0 vc"),
           17: ("T0 ba", "T1 bb", "T0 bc"),
           19: ("T0 ka", "T1 kb", "T0 kc")}
PRELUDE = ("X cT", "X kv0", "S a", "X wmean", "X simnorm", "S b", "T0 ba", "T1 bb", "T0 bc")


U = len(UNITS)


def steps(parts, first, last, next_only=False):
    for s in range(first, last):
        for part, phase in parts:
            v = s - phase
            if 0 <= v < U + 3 and not (next_only and v < U) and (part != "prepare" or s in PREPARE):
                yield part, v


class Bank:

    def __init__(self, name, tile, full, drained):
        self.name, self.tile, self.full, self.drained = name, tile, full, drained
        self.prelude = [f.split()[1] for f in PRELUDE if f.split()[0] == name]
        self.order, tail = {}, None
        for part, v in steps(PE_PARTS, 3, U + 3):
            if tail is None and (part, v) == (PE_PARTS[0][0], U - PE_PARTS[0][1]):
                tail = len(self.order)
            for f in fillings(part, v):
                if f.split()[0] == name:
                    self.order[f.split()[1], None if part == "prepare" else v] = len(self.order)
        self.per_pass = len(self.order)
        self.base = len(self.prelude) + self.per_pass - tail

    def number(self, it, what, v=None):
        if isinstance(it, int) and v is None:
            return self.prelude.index(what) + 1
        at = self.order.get((what, v))
        if at is None:
            at = self.order[what, v + U] - self.per_pass
        return it * self.per_pass + (self.base + at + 1)


def fillings(part, v):
    if part == "prepare":
        return PREPARE[v]
    k = UNITS[v % U][0]
    if part in ("xT", "xT_early"):
        return ("X xT",) if (part == "xT_early") == (k in XT_EARLY) else ()
    return FILLS[k].get(part, ())


PACKS = {
    "base": [("ident", P, P), ("delta", P, H), ("ones_col", P, NCH * H), ("desc0", P, E0),
             ("desc3", P, 4 + R), ("gates", P, 8), ("ln_gamma", P, 2)],
    "att0": [("wk0", P, 2 * DH0), ("wv0", P, 2 * DH0), ("wq0", P, 8 * D), ("wo0", P, 8 * D)],
    "tern": [("wt", P, 3 * FB)],
    "low": [("w3", P, PROJ + R + D), ("bp", P, PROJ), ("sim", PROJ, 4 + R), ("temp", PROJ, 1),
            ("wu", R, D)],
    "ff0": [("wff1", P, 2 * FF0), ("wff2", P, 4 * D)],
    "top1": [("wr", P, E0), ("br", P, E0), ("w1", P, E0 * H0), ("b1", E0, H0), ("w2", P, 2 * E0 * D),
             ("b2", E0, D)],
    "att23": [("wq2", P, D), ("wk2", P, D), ("wv2", P, D), ("b2qkv", P, 3), ("wo2", P, D),
              ("bo2", 1, D), ("wq3", P, D), ("wk3", P, D), ("wo3", P, D)],
    "top4": [("wg", P, E2), ("w13", P, 6 * GW), ("w2s", P, 9 * D)],
}
WIDTH = {k: sum(c for _, _, c in v) for k, v in PACKS.items()}


def gated_flamingo(nc, x_in, ctx_in, ctxT_in, mask_in, packs, out):
    with ExitStack() as stack:
        def sb(name, shape, dt=F32):
            return stack.enter_context(nc.sbuf_tensor(name, shape, dt))

        def psum(name, shape):
            return stack.enter_context(nc.psum_tensor(name, shape, F32))

        def sem(name):
            return stack.enter_context(nc.semaphore(name))

        hh = sb("hh", [P, 3, 3 * GW])
        W, loaded = {}, {}
        for pack, parts in PACKS.items():
            tile = hh[:, :, :].rearrange("p b n -> p (b n)") if pack == "tern" else sb("pack_" + pack, [P, WIDTH[pack]])
            loaded[pack] = sem("loaded_" + pack)
            at = 0
            for name, rows, cols in parts:
                W[name] = tile[0:rows, at:at + cols]
                at += cols
            W["pack_" + pack] = tile[:, 0:WIDTH[pack]]
        ident = W["ident"]
        ident_b = sb("ident_b", [P, P], BF16)
        ones = sb("ones", [P, P])
        ones_b = sb("ones_b", [1, P], BF16)
        pick_row = sb("pick_row", [E0, E0, P], BF16)
        half = sb("half", [P, 4])
        tg = sb("tg", [P, 8])
        tgh = sb("tgh", [P, 1])
        sq2 = sb("sq2", [P, 1])
        wt_q = sb("wt_q", [P, 3 * FB], BF16)
        wt_sum = sb("wt_sum", [P, 3])
        wt_mean = sb("wt_mean", [P, 3])
        wt_inv = sb("wt_inv", [P, 3])
        wt_c = sb("wt_c", [P, 3])
        sim_sq = sb("sim_sq", [PROJ, 4 + R])
        sim_n = sb("sim_n", [PROJ, 4 + R])
        sim_s = sb("sim_s", [PROJ, 1])

        ctx_st = sb("ctx_st", [CTX, D])
        ctxT_st = sb("ctxT_st", [D, CTX])
        mask_st = sb("mask_st", [P, CTX], I32)
        x_st = sb("x_st", [P, TILES, D])
        ctx = sb("ctx", [CTX, D])
        ctxT = sb("ctxT", [D, CTX])
        mask_row = sb("mask_row", [1, HB, CTX], BF16)
        seen = sb("seen", [P, CTX])
        anyseen = sb("anyseen", [P, 3])
        cstat = sb("cstat", [CTX, 6])
        cmv = sb("cmv", [CTX, 2])
        cve = sb("cve", [CTX, 1])
        crs = sb("crs", [CTX, 1])
        ctxn = sb("ctxn", [CTX, D])
        ctxnT = sb("ctxnT", [D, CTX])
        k0 = sb("k0", [P, 2, CTX])
        v0 = sb("v0", [P, 2, CTX])
        A0 = sb("A0", [D, HC])
        B0 = sb("B0", [P, NCH, D])
        k2 = sb("k2", [P, CTX])
        v2 = sb("v2", [P, CTX])
        k3 = sb("k3", [P, CTX])
        K2 = sb("K2", [P, H, CTX])
        K3 = sb("K3", [P, H, CTX])
        V2 = sb("V2", [P, NCH, H, VW])
        V3 = sb("V3", [P, NCH, H, VW])

        x = sb("x", [P, TILES, D])
        y = sb("y", [P, TILES, D])
        stat = sb("stat", [P, 6])
        mv = sb("mv", [P, TILES, 2])
        ve = sb("ve", [P, TILES])
        rstd = sb("rstd", [P, TILES])
        xh = sb("xh", [P, TILES, D])
        xhq = sb("xhq", [P, 2, D])
        xq = sb("xq", [P, TILES, D], BF16)
        xT = sb("xT", [D, TILES, P])
        qT = sb("qT", [D, 2, P])
        xTq = sb("xTq", [D, TILES, P], BF16)
        mx = sb("mx", [P, TILES, H])
        pr = sb("pr", [P, 3, HC])
        wt_r = pr[:, :, :].rearrange("p b n -> p (b n)")[:, 0:3 * FB]
        pT = sb("pT", [P, 2, NCH, P])
        B0T = pT[:, 0, :, :].rearrange("p n d -> p (n d)")[:, 0:HC]
        V2x = pT[:, 1, :, :].rearrange("p n d -> p (n d)")[:, 0:HC].rearrange("p (h c) -> p h c", c=CTX)
        rs = sb("rs", [P, TILES, H])
        ri = sb("ri", [P, TILES, H])
        cv = sb("cv", [P, 2, D])
        cvT = sb("cvT", [D, 2, P])
        th = sb("th", [P, 2, 3 * GW])
        g1 = sb("g1", [P, 2, 3 * GW])
        hT = sb("hT", [P, 2, 9, P])
        hq = sb("hq", [P, 2, FB], BF16)
        hqT = sb("hqT", [P, 2, 4, P], BF16)
        sc = sb("sc", [P, TILES, 16])
        lg = sb("lg", [P, TILES, 4 + R])
        tt = sb("tt", [P, TILES, 4 + R])
        oh = sb("oh", [P, TILES, 4 + R])
        ex = sb("ex", [P, TILES, E0])
        ohT = sb("ohT", [E0, TILES, P])
        ohTb = sb("ohTb", [E0, 2, P], BF16)
        xm = sb("xm", [D, 2, E0, P])
        hid = sb("hid", [P, 2, 2, P])
        sg = sb("sg", [P, TILES, E2])
        sig = sb("sig", [P, TILES, E2])
        pairs = sb("pairs", [P, 4, 6])
        gs = sb("gs", [P, 8])
        best = sb("best", [P, 8])
        taken = {n: sb(f"taken{n}", [P, 8]) for n in (2, 4)}
        left = sb("left", [P, E2])
        picked = sb("picked", [P, E2])
        cap = sb("cap", [P, 4])
        psc = sb("psc", [P, 4])
        msk = sb("msk", [P, E2])
        comb = sb("comb", [P, TILES, E2])
        pj = sb("pj", [P, TILES, PROJ])
        pj2 = sb("pj2", [P, PROJ])
        pjT = sb("pjT", [PROJ, 2, P])
        dn = sb("dn", [P, TILES, R])
        dm = sb("dm", [P, TILES, R])
        dmT = sb("dmT", [R, 2, P])

        S, T0, T1, O, X = (Bank(n, psum("psum_" + n, s), sem(n + "_full"), sem(n + "_drained")) for n, s in
                           (("S", [P, 4, 512]), ("T0", [P, 512]), ("T1", [P, 512]), ("O", [P, 512]), ("X", [P, 512])))
        banks = (S, T0, T1, O, X)

        events = {}

        def event(name, per_pass, before=0):
            events[name] = (sem(name), per_pass, before)

        event("var_ready", U)
        event("rstd_ready", U)
        event("xh_ready", U)
        event("ctx_var", 1, 1)
        event("ctx_rstd", 1, 1)
        event("ctx_norm", 1, 1)
        event("ctx_copied", 1, 1)
        event("ctx_used", 1, 1)
        event("mask_ready", 1, 1)
        event("expanded", 3)
        event("inv0", TILES)
        event("probs0", TILES)
        for name in ("probs_A0", "probs_A2", "probs_A3",
                     "tanh_A0", "tanh_F1", "tanh_F2a", "tanh_F2b",
                     "nmax_A1",
                     "centred_F0", "centred_F3",
                     "expsum_F0", "expsum_F3",
                     "pick_ready",
                     "hq_ready",
                     "comb_ready",
                     "weighted_F2a", "weighted_F2b",
                     "pj_ready", "ss_ready",
                     "rn_ready",
                     "dm_ready"):
            event(name, TILES)
        s_x_loaded, s_c_loaded, s_stored = sem("x_loaded"), sem("c_loaded"), sem("stored")
        s_const, s_tg, s_prel = sem("const_ready"), sem("tanh_gates"), sem("prelude")
        s_dve, s_simpow, s_temp, s_quant = sem("dve_step"), sem("sim_pow"), sem("temp_exp"), sem("ternary_ready")
        s_carry = sem("wait_carrier")
        block = stack.enter_context(nc.Block())

        def helpers(eng, it):
            def full(bank, what, v=None):
                eng.wait_ge(bank.full, bank.number(it, what, v))

            def free(bank, what, v=None):
                eng.wait_ge(bank.drained, bank.number(it, what, v))

            def drained(bank, what, v=None):
                eng.wait_ge(bank.drained, bank.number(it, what, v) + 1)

            def wait(name, n, v=0):
                s, per, before = events[name]
                eng.wait_ge(s, it * per + (before + n + 1 + v // U * per))
            return full, free, drained, wait

        def inc(ins, name):
            return ins.then_inc(events[name][0], 1)

        @block.sync
        def _(sp):
            def load_ctx(b):
                sp.dma_start(ctx_st[:, :], ctx_in[b]).then_inc(s_c_loaded, 16)
                sp.dma_start(ctxT_st[:, :], ctxT_in[b]).then_inc(s_c_loaded, 16)
                sp.dma_start(mask_st[:, :], mask_in[b]).then_inc(s_c_loaded, 16)

            def load_x(b):
                sp.dma_start(x_st[:, :, :], x_in[b].rearrange("(t p) d -> p t d", p=P)).then_inc(s_x_loaded, 16)

            sp.sem_inc(s_stored, 16 * TILES)
            for pack in PACKS:
                sp.dma_start(W["pack_" + pack], packs[pack]).then_inc(loaded[pack], 16)
                if pack == "base":
                    load_ctx(0)
                elif pack == "att0":
                    load_x(0)
            def next_ctx(n):
                sp.wait_ge(events["ctx_copied"][0], n)
                sp.wait_ge(events["ctx_used"][0], n)
                load_ctx(n % B)

            next_ctx(1)
            for b in range(B):
                full, free, drained, wait = helpers(sp, b)
                drained(O, "out", TILES - 1)
                load_x((b + 1) % B)
                if b + 2 <= B:
                    next_ctx(b + 2)
                for t in range(TILES):
                    drained(O, "out", U - TILES + t)
                    sp.dma_start(out[b, t * P:(t + 1) * P, :], y[:, t, :]).then_inc(s_stored, 16)
            sp.wait_ge(s_stored, 16 * B * TILES + 16 * TILES)

        @block.tensor
        def _(pe):
            def transposes(dst, src, chunks):
                for n, (lo, hi) in enumerate(chunks):
                    last = pe.transpose(dst[0:hi - lo, n * P:(n + 1) * P], src[:, lo:hi], ident)
                return last

            cuts = [(n * P, min((n + 1) * P, HC)) for n in range(NCH)]
            trio = (cuts[0:4], cuts[4:8], cuts[8:NCH])
            chunks = [(n * P, (n + 1) * P) for n in range(3 * GW // P)]

            def keys_values(full, free, drained, wait):
                def cT():
                    wait("ctx_norm", 0)
                    free(X, "cT")
                    pe.transpose(X.tile[:, 0:CTX], ctxn[:, :], ident[0:CTX, 0:CTX]).then_inc(X.full, 1)

                def kv():
                    free(X, "kv")
                    pe.matmul(X.tile[:, 0:CTX], W["wk2"], ctxT[:, :], start=True, stop=True)
                    pe.matmul(X.tile[:, P:P + CTX], W["wv2"], ctxT[:, :], start=True, stop=True)
                    pe.matmul(X.tile[:, 2 * P:2 * P + CTX], W["wk3"], ctxT[:, :], start=True, stop=True)\
                      .then_inc(X.full, 1)

                def kv0():
                    drained(X, "cT")
                    free(X, "kv0")
                    pe.matmul(X.tile[:, 0:CTX], W["wk0"], ctxnT[:, :], start=True, stop=True)
                    pe.matmul(X.tile[:, P:P + CTX], W["wv0"], ctxnT[:, :], start=True, stop=True).then_inc(X.full, 1)

                def product(what, w, kv_):
                    free(S, what)
                    for g in range(H // 2):
                        last = pe.matmul(S.tile[:, g // 2, g % 2 * 2 * CTX:(g % 2 + 1) * 2 * CTX],
                                         W[w][:, g * D:(g + 1) * D], kv_[:, :, :], start=True, stop=True)
                    last.then_inc(S.full, 1)

                def a():
                    drained(X, "kv0")
                    product("a", "wq0", k0)

                def b():
                    product("b", "wo0", v0)

                def turn(src, names):
                    for bank, what, cs in zip((T0, T1, T0), names, trio):
                        free(bank, what)
                        transposes(bank.tile, src, cs).then_inc(bank.full, 1)

                def vb():
                    wait("expanded", 1)
                    turn(V2x.rearrange("p h c -> p (h c)"), ("va", "vb", "vc"))

                def bT():
                    drained(S, "b")
                    turn(B0T, ("ba", "bb", "bc"))

                def kT():
                    wait("expanded", 2)
                    turn(K3[:, :, :].rearrange("p h c -> p (h c)"), ("ka", "kb", "kc"))
                return {12: (cT,), 13: (kv, kv0), 14: (a,), 15: (b,), 16: (vb,), 17: (bT,), 19: (kT,)}, \
                    (cT, kv0, a, b, bT)

            pe.wait_ge(loaded["base"], 16)
            full, free, drained, wait = helpers(pe, -1)
            first_parts = keys_values(full, free, drained, wait)[1]
            first_parts[0]()
            pe.wait_ge(s_const, 12)
            pe.wait_ge(loaded["att0"], 16)
            for part in first_parts[1:3]:
                part()
            pe.wait_ge(s_prel, 1)
            free(X, "wmean")
            pe.matmul(X.tile[:, 0:3], ones[:, :], wt_sum[:, :], start=True, stop=True).then_inc(X.full, 1)
            pe.wait_ge(s_prel, 2)
            free(X, "simnorm")
            pe.matmul(X.tile[0:PROJ, 0:4 + R], ones[0:PROJ, 0:PROJ], sim_sq[:, :], start=True, stop=True)\
              .then_inc(X.full, 1)
            for part in first_parts[3:]:
                part()
            drained(S, "a")
            drained(T0, "bc")

            def one_pass(it):
                full, free, drained, wait = helpers(pe, it)

                def xT_early(k, u, t):
                    if k in XT_EARLY:
                        turn_x(k, u, t)

                def xT_late(k, u, t):
                    if k not in XT_EARLY:
                        turn_x(k, u, t)

                def turn_x(k, u, t):
                    wait("xh_ready", u)
                    free(X, "xT", u)
                    if k == "F1":
                        pe.transpose(X.tile[:, 0:P // 2].bitcast(BF16), xq[:, t, :], ident_b[:, :])\
                          .then_inc(X.full, 1)
                    else:
                        pe.transpose(X.tile[:, 0:P], xh[:, t, :], ident).then_inc(X.full, 1)

                def first(k, u, t):
                    n = 4 * int(k[1]) + t
                    if k == "A0":
                        wait("mask_ready", -1, u)
                        drained(X, "xT", u)
                        free(S, "scores", u)
                        for q in range(4):
                            pe.matmul(S.tile[:, q, 0:SB], xT[:, t, :], A0[:, q * SB:(q + 1) * SB],
                                      start=True, stop=False)
                            last = pe.matmul(S.tile[:, q, 0:SB], ones_b[:, :],
                                             mask_row[:, :, :].rearrange("o h c -> o (h c)"),
                                             start=False, stop=True)
                        last.then_inc(S.full, 1)
                    elif k in ("A2", "A3"):
                        K = (K2 if k == "A2" else K3)[:, :, :].rearrange("p h c -> p (h c)")
                        drained(X, "q", u)
                        wait("expanded", 0 if k == "A2" else 2)
                        free(S, "scores", u)
                        for q in range(4):
                            last = pe.matmul(S.tile[:, q, 0:SB], qT[:, u % 2, :], K[:, q * SB:(q + 1) * SB],
                                             start=True, stop=True)
                        last.then_inc(S.full, 1)
                    elif k == "A1":
                        wait("ctx_copied", -1)
                        drained(X, "xT", u)
                        free(S, "scores", u)
                        pe.matmul(S.tile[:, 0, 0:CTX], xT[:, t, :], ctxT[:, :], start=True, stop=True)\
                          .then_inc(S.full, 1)
                    elif k == "F1":
                        pe.wait_ge(s_quant, 1)
                        drained(X, "xT", u)
                        free(S, "gu", u)
                        for n in range(2):
                            last = pe.matmul(S.tile[:, n, :], xTq[:, t, :], wt_q[:, n * FB:(n + 1) * FB],
                                             start=True, stop=True)
                        last.then_inc(S.full, 1)
                    elif k == "F2":
                        pe.wait_ge(loaded["top4"], 16)
                        drained(X, "xT", u)
                        free(S, "gu", u)
                        for q, c in enumerate((0, 1, 3, 4)):
                            last = pe.matmul(S.tile[:, q, 0:GW], xT[:, t, :], W["w13"][:, c * GW:(c + 1) * GW],
                                             start=True, stop=True)
                        last.then_inc(S.full, 1)
                    elif k == "F3":
                        pe.wait_ge(loaded["low"], 16)
                        drained(X, "xT", u)
                        free(S, "all", u)
                        pe.matmul(S.tile[:, 0, 0:PROJ + R + D], xT[:, t, :], W["w3"], start=True, stop=True)\
                          .then_inc(S.full, 1)

                def late_transpose(k, u, t):
                    if k == "A0":
                        drained(T1, "up", u)
                        free(T0, "hT", u)
                        transposes(T0.tile, hh[:, u % U % 3, :], cuts[0:4]).then_inc(T0.full, 1)
                        wait("probs0", t, u)
                        free(T1, "pa", u)
                        transposes(T1.tile, pr[:, u % U % 3, :], trio[0]).then_inc(T1.full, 1)
                    elif k == "F0":
                        free(O, "bias", u)
                        pe.matmul(O.tile[:, 0:D], ohT[:, t, :], W["b2"], start=True, stop=True).then_inc(O.full, 1)
                        drained(O, "hidden", u)
                        for n, bank, what in ((0, T0, "ya"), (1, T1, "yb")):
                            free(bank, what, u)
                            for j in range(2):
                                last = pe.matmul(bank.tile[:, :], hid[:, u % 2, j, :],
                                                 W["w2"][:, j * E0 * D + n * 512:j * E0 * D + (n + 1) * 512],
                                                 start=(j == 0), stop=(j == 1))
                            last.then_inc(bank.full, 1)
                    elif k in ("A2", "A3"):
                        drained(O, "values", u)
                        free(X, "vT", u)
                        pe.transpose(X.tile[:, 0:P], cv[:, u % 2, :], ident).then_inc(X.full, 1)
                    elif k == "F2":
                        wait("weighted_F2a", t, u)
                        wait("weighted_F2b", t, u)
                        for bank, what, cs in ((T0, "ha", chunks[0:4]), (T1, "hb", chunks[4:8])):
                            free(bank, what, u)
                            transposes(bank.tile, hh[:, u % U % 3, :], cs).then_inc(bank.full, 1)
                    elif k == "F3":
                        wait("dm_ready", t, u)
                        free(X, "downT", u)
                        pe.transpose(X.tile[0:R, 0:P], dm[:, t, :], ident).then_inc(X.full, 1)

                def late_rest(k, u, t):
                    if k == "A0":
                        for bank, what, cs in ((T0, "pb", trio[1]), (T1, "pc", trio[2])):
                            free(bank, what, u)
                            transposes(bank.tile, pr[:, u % U % 3, :], cs).then_inc(bank.full, 1)
                    elif k == "F2":
                        free(T0, "hc", u)
                        transposes(T0.tile, hh[:, u % U % 3, :], chunks[8:9]).then_inc(T0.full, 1)

                def transpose(k, u, t):
                    if k in ("A2", "A3"):
                        wait("probs_" + k, t, u)
                        for bank, what, cs in ((T0, "pa", trio[0]), (T1, "pb", trio[1])):
                            free(bank, what, u)
                            transposes(bank.tile, pr[:, u % U % 3, :], cs).then_inc(bank.full, 1)

                def rest(k, u, t):
                    if k in ("A2", "A3"):
                        free(T0, "pc", u)
                        transposes(T0.tile, pr[:, u % U % 3, :], trio[2]).then_inc(T0.full, 1)

                def middle(k, u, t):
                    if k == "A0":
                        pe.wait_ge(loaded["ff0"], 16)
                        for n, bank, what in ((1, T0, "gate"), (0, T1, "up")):
                            free(bank, what, u)
                            pe.matmul(bank.tile[:, :], xT[:, t, :], W["wff1"][:, n * FF0:(n + 1) * FF0],
                                      start=True, stop=True).then_inc(bank.full, 1)
                    elif k == "F0":
                        pe.wait_ge(loaded["top1"], 16)
                        drained(S, "masks", u)
                        free(O, "hidden", u)
                        for j in range(2):
                            for e in range(E0):
                                pe.matmul(O.tile[:, j * P:(j + 1) * P],
                                          W["w1"][:, e * H0 + j * P:e * H0 + (j + 1) * P],
                                          xm[:, u % 2, e, :], start=(e == 0), stop=False)
                            last = pe.matmul(O.tile[:, j * P:(j + 1) * P], W["b1"][:, j * P:(j + 1) * P],
                                             ohT[:, t, :], start=False, stop=True)
                        last.then_inc(O.full, 1)
                    elif k == "A1":
                        drained(S, "scores", u)
                        free(T0, "pT", u)
                        pe.transpose(T0.tile[0:CTX, 0:P], pr[:, u % U % 3, 0:CTX], ident).then_inc(T0.full, 1)
                    elif k == "F1":
                        wait("hq_ready", t, u)
                        free(T0, "hT", u)
                        for n in range(4):
                            last = pe.transpose(T0.tile[:, n * 64:(n + 1) * 64].bitcast(BF16),
                                                hq[:, u % 2, n * P:(n + 1) * P], ident_b[:, :])
                        last.then_inc(T0.full, 1)
                    elif k == "F2":
                        for c, bank, what in ((2, T0, "gate"), (5, T1, "up")):
                            free(bank, what, u)
                            pe.matmul(bank.tile[:, 0:GW], xT[:, t, :], W["w13"][:, c * GW:(c + 1) * GW],
                                      start=True, stop=True).then_inc(bank.full, 1)
                    elif k == "F3":
                        drained(X, "projT", u)
                        pe.wait_ge(s_prel, 4)
                        free(X, "logits", u)
                        pe.matmul(X.tile[:, 0:4 + R], pjT[:, u % 2, :], sim_n[:, :], start=True, stop=True)\
                          .then_inc(X.full, 1)

                def extra(k, u, t):
                    if k == "F0":
                        wait("pick_ready", t, u)
                        free(X, "pickT", u)
                        pe.transpose(X.tile[0:E0, 0:P], oh[:, t, 0:E0], ident).then_inc(X.full, 1)
                    elif k == "F3":
                        wait("pj_ready", t, u)
                        free(X, "projT", u)
                        pe.transpose(X.tile[0:PROJ, 0:P], pj[:, t, :], ident).then_inc(X.full, 1)

                def project(k, u, t):
                    if k == "F0":
                        pe.wait_ge(loaded["top1"], 16)
                        drained(X, "xT", u)
                        free(X, "logits", u)
                        pe.matmul(X.tile[:, 0:E0], xT[:, t, :], W["wr"], start=True, stop=True).then_inc(X.full, 1)
                    elif k == "F2":
                        pe.wait_ge(loaded["top4"], 16)
                        drained(X, "xT", u)
                        free(X, "gate", u)
                        pe.matmul(X.tile[:, 0:E2], xT[:, t, :], W["wg"], start=True, stop=True).then_inc(X.full, 1)

                def query(k, u, t):
                    if k in ("A2", "A3"):
                        drained(X, "xT", u)
                        free(X, "q", u)
                        pe.matmul(X.tile[:, 0:P], W["wq2" if k == "A2" else "wq3"], xT[:, t, :],
                                  start=True, stop=True).then_inc(X.full, 1)

                def output(k, u, t):
                    if k == "A0":
                        free(O, "out", u)
                        drained(T0, "hT", u)
                        for n in range(4):
                            pe.matmul(O.tile[:, 0:D], hT[:, u % 2, n, :], W["wff2"][:, n * D:(n + 1) * D],
                                      start=(n == 0), stop=False)
                        drained(T0, "pb", u)
                        drained(T1, "pc", u)
                        for n, (lo, hi) in enumerate(cuts):
                            last = pe.matmul(O.tile[:, 0:D], pT[0:hi - lo, u % 2, n, :], B0[0:hi - lo, n, :],
                                             start=False, stop=(n == NCH - 1))
                        last.then_inc(O.full, 1)
                    elif k in ("A2", "A3"):
                        drained(X, "vT", u)
                        free(T1, "out", u)
                        last = pe.matmul(T1.tile[:, 0:D], cvT[:, u % 2, :], W["wo2" if k == "A2" else "wo3"],
                                         start=True, stop=(k == "A3"))
                        if k == "A2":
                            last = pe.matmul(T1.tile[:, 0:D], ones[0:1, :], W["bo2"], start=False, stop=True)
                        last.then_inc(T1.full, 1)
                    elif k == "F2":
                        free(O, "out", u)
                        drained(T1, "hb", u)
                        drained(T0, "hc", u)
                        for n in range(9):
                            last = pe.matmul(O.tile[:, 0:D], hT[:, u % 2, n, :], W["w2s"][:, n * D:(n + 1) * D],
                                             start=(n == 0), stop=(n == 8))
                        last.then_inc(O.full, 1)
                    elif k == "F3":
                        drained(X, "downT", u)
                        free(O, "out", u)
                        pe.matmul(O.tile[:, 0:D], dmT[:, u % 2, :], W["wu"], start=True, stop=True).then_inc(O.full, 1)

                def values(k, u, t):
                    if k == "A1":
                        drained(T0, "pT", u)
                        free(O, "out", u)
                        pe.matmul(O.tile[:, 0:D], pT[0:CTX, u % 2, 0, :], ctx[:, :], start=True, stop=True)\
                          .then_inc(O.full, 1)
                    elif k == "F1":
                        drained(T0, "hT", u)
                        free(O, "out", u)
                        for n in range(4):
                            last = pe.matmul(O.tile[:, 0:D], hqT[:, u % 2, n, :],
                                             wt_q[:, 2 * FB + n * D:2 * FB + (n + 1) * D],
                                             start=(n == 0), stop=(n == 3))
                        last.then_inc(O.full, 1)
                    elif k in ("A2", "A3"):
                        V = V2 if k == "A2" else V3
                        drained(T0, "vc" if k == "A2" else "kc")
                        drained(T1, "pb", u)
                        drained(T0, "pc", u)
                        free(O, "values", u)
                        for n, (lo, hi) in enumerate(cuts):
                            last = pe.matmul(O.tile[:, 0:H * VW], pT[0:hi - lo, u % 2, n, :],
                                             V[0:hi - lo, n, :, :].rearrange("p h v -> p (h v)"),
                                             start=(n == 0), stop=(n == NCH - 1))
                        last.then_inc(O.full, 1)

                def spread(k, u, t):
                    if k == "F0":
                        drained(X, "pickT", u)
                        free(S, "masks", u)
                        for e in range(E0):
                            last = pe.matmul(S.tile[:, e // 4, e % 4 * P:(e % 4 + 1) * P], pick_row[:, e, :],
                                             ohTb[:, u % 2, :], start=True, stop=True)
                        last.then_inc(S.full, 1)

                parts = dict(first=first, late_transpose=late_transpose, late_rest=late_rest, transpose=transpose,
                             rest=rest, xT_early=xT_early, xT=xT_late, query=query, middle=middle, extra=extra,
                             project=project, output=output, values=values, spread=spread)
                prepare = keys_values(full, free, drained, wait)[0]

                def work(part, v):
                    if part == "prepare":
                        for do in prepare[v]:
                            do()
                    else:
                        parts[part](UNITS[v % U][0], v, UNITS[v % U][1])
                return free, work

            free, work = one_pass(-1)
            for part, v in steps(PE_PARTS, U, U + 3):
                if v >= U:
                    work(part, v)
                    continue
                for f in fillings(part, v):
                    bank = next(b for b in banks if b.name == f.split()[0])
                    free(bank, f.split()[1], v)
                    pe.sem_inc(bank.full, 1)
                    pe.sem_inc(bank.drained, 1)

            with pe.Fori(0, B) as it:
                free, work = one_pass(it)
                for part, v in steps(PE_PARTS, 3, U + 3):
                    work(part, v)

        @block.scalar
        def _(act):
            Copy, Exp, Tanh, Relu, Ident = ACT.Copy, ACT.Exp, ACT.Tanh, ACT.Relu, ACT.Identity
            act.sem_inc(X.drained, 1)
            act.sem_inc(T0.drained, 1)
            act.sem_inc(T1.drained, 1)
            act.wait_ge(loaded["base"], 16)
            act.activation(tg[:, :], W["gates"], Tanh).then_inc(s_tg, 1)

            groups = ((0, 4), (4, 8), (8, NCH))

            def keys_values(full, free, drained, wait):
                def cT():
                    full(X, "cT")
                    act.activation(ctxnT[:, :], X.tile[:, 0:CTX], Copy, scale=W["ln_gamma"][:, 1:2])\
                       .then_inc(X.drained, 1)

                def kv():
                    full(X, "kv")
                    act.activation(k2[:, :], X.tile[:, 0:CTX], Ident, bias=W["b2qkv"][:, 1:2])
                    act.activation(v2[:, :], X.tile[:, P:P + CTX], Ident, bias=W["b2qkv"][:, 2:3])
                    act.activation(k3[:, :], X.tile[:, 2 * P:2 * P + CTX], Copy).then_inc(X.drained, 1)

                def kv0():
                    full(X, "kv0")
                    wait("ctx_used", 0)
                    for g in range(2):
                        rows = slice(g * DH0, (g + 1) * DH0)
                        act.activation(k0[rows, g, :], X.tile[rows, 0:CTX], Copy, scale=float(DH0) ** -0.5)
                        last = act.activation(v0[rows, g, :], X.tile[rows, P:P + CTX], Copy, scale=anyseen[rows, 2:3])
                    last.then_inc(X.drained, 1)

                def product(what, dst):
                    full(S, what)
                    act.activation(dst.rearrange("p (b n) -> p b n", b=4), S.tile[:, :, 0:SB], Copy)\
                       .then_inc(S.drained, 1)

                def a():
                    product("a", A0[:, :])

                def b():
                    product("b", B0T)

                def bT():
                    for bank, what, (lo, hi) in zip((T0, T1, T0), ("ba", "bb", "bc"), groups):
                        full(bank, what)
                        act.activation(B0[:, lo:hi, :], bank.tile[:, 0:(hi - lo) * P].rearrange("p (n d) -> p n d", d=P),
                                       Copy).then_inc(bank.drained, 1)

                def turned(V, names):
                    for bank, what, (lo, hi) in zip((T0, T1, T0), names, groups):
                        full(bank, what)
                        src = bank.tile[:, 0:(hi - lo) * P].rearrange("p (n h v) -> p n h v", h=H, v=DH)
                        for n in range(lo, hi):
                            last = act.activation(V[:, n, :, 0:DH], src[:, n - lo, :, :], Copy)
                        last.then_inc(bank.drained, 1)

                def vb():
                    turned(V2, ("va", "vb", "vc"))

                def kT():
                    turned(V3, ("ka", "kb", "kc"))
                return {12: (cT,), 13: (kv, kv0), 14: (a,), 15: (b,), 16: (vb,), 17: (bT,), 19: (kT,)}, \
                    (cT, kv0, a, b, bT)

            act.wait_ge(s_const, 12)
            first_parts = keys_values(*helpers(act, -1))[1]
            for part in first_parts[0:3]:
                part()
            act.wait_ge(s_prel, 3)
            act.activation(sim_s[:, :], sim_s[:, :], Exp).then_inc(s_temp, 1)
            for part in first_parts[3:]:
                part()

            def one_pass(it, first):
                full, free, drained, wait = helpers(act, it)
                prepare = keys_values(full, free, drained, wait)[0]

                def evac_probs(bank, what, u, t, lo, hi):
                    full(bank, what, u)
                    act.activation(pT[:, u % 2, lo:hi, :], bank.tile[:, 0:(hi - lo) * P].rearrange("p (n d) -> p n d", d=P),
                                   Copy).then_inc(bank.drained, 1)

                def phase3(k, u, t):
                    if k == "A0":
                        full(T0, "hT", u)
                        act.activation(hT[:, u % 2, 0:4, :], T0.tile[:, :].rearrange("p (n d) -> p n d", d=P), Copy)\
                           .then_inc(T0.drained, 1)
                        evac_probs(T1, "pa", u, t, *groups[0])
                    elif k in ("A2", "A3"):
                        full(X, "vT", u)
                        act.activation(cvT[:, u % 2, :], X.tile[:, 0:P], Copy).then_inc(X.drained, 1)
                    elif k == "F2":
                        evac_hidden(T0, "ha", u, 0, 4)
                        evac_hidden(T1, "hb", u, 4, 8)
                    elif k == "F3":
                        full(X, "downT", u)
                        act.activation(dmT[:, u % 2, :], X.tile[0:R, 0:P], Copy).then_inc(X.drained, 1)

                def evac_hidden(bank, what, u, lo, hi):
                    full(bank, what, u)
                    act.activation(hT[:, u % 2, lo:hi, :],
                                   bank.tile[:, 0:(hi - lo) * P].rearrange("p (n d) -> p n d", d=P), Copy)\
                       .then_inc(bank.drained, 1)

                def phase3_rest(k, u, t):
                    if k == "A0":
                        evac_probs(T0, "pb", u, t, *groups[1])
                        evac_probs(T1, "pc", u, t, *groups[2])
                    elif k == "F2":
                        evac_hidden(T0, "hc", u, 8, 9)

                def phase2_first(k, u, t):
                    if k in ("A2", "A3"):
                        evac_probs(T0, "pa", u, t, *groups[0])
                        evac_probs(T1, "pb", u, t, *groups[1])

                def phase0_early(k, u, t):
                    if k in XT_EARLY:
                        phase0(k, u, t)

                def phase0_late(k, u, t):
                    if k not in XT_EARLY:
                        phase0(k, u, t)

                def phase0(k, u, t):
                    full(X, "xT", u)
                    if k == "A0":
                        act.activation(xT[:, t, :], X.tile[:, 0:P], Copy, scale=W["ln_gamma"][:, 0:1])\
                           .then_inc(X.drained, 1)
                    elif k == "F1":
                        act.activation(xTq[:, t, :], X.tile[:, 0:P // 2].bitcast(BF16), Copy).then_inc(X.drained, 1)
                    else:
                        act.activation(xT[:, t, :], X.tile[:, 0:P], Copy).then_inc(X.drained, 1)

                def phase2(k, u, t):
                    if k == "A0":
                        full(T0, "gate", u)
                        inc(act.activation(th[:, u % 2, 0:FF0], T0.tile[:, :], Tanh, scale=0.5), "tanh_A0")
                    elif k == "F0":
                        full(O, "hidden", u)
                        act.activation(hid[:, u % 2, :, :], O.tile[:, 0:2 * P].rearrange("p (j n) -> p j n", j=2), Relu)\
                           .then_inc(O.drained, 1)
                    elif k == "A1":
                        full(T0, "pT", u)
                        act.activation(pT[0:CTX, u % 2, 0, :], T0.tile[0:CTX, 0:P], Copy).then_inc(T0.drained, 1)
                    elif k == "F1":
                        full(T0, "hT", u)
                        act.activation(hqT[:, u % 2, :, :], T0.tile[:, 0:256].bitcast(BF16).rearrange("p (n d) -> p n d", d=P),
                                       Copy).then_inc(T0.drained, 1)
                    elif k in ("A2", "A3"):
                        evac_probs(T0, "pc", u, t, *groups[2])
                    elif k == "F2":
                        full(T0, "gate", u)
                        inc(act.activation(th[:, u % 2, 2 * GW:3 * GW], T0.tile[:, 0:GW], Tanh, scale=0.5), "tanh_F2b")

                def phase1_extra(k, u, t):
                    if k == "F0":
                        full(X, "pickT", u)
                        act.activation(ohT[:, t, :], X.tile[0:E0, 0:P], Copy)
                        act.activation(ohTb[:, u % 2, :], X.tile[0:E0, 0:P], Copy).then_inc(X.drained, 1)
                    elif k == "F3":
                        full(X, "projT", u)
                        act.activation(pjT[:, u % 2, :], X.tile[0:PROJ, 0:P], Copy).then_inc(X.drained, 1)

                def phase0_project(k, u, t):
                    if k == "A2":
                        full(X, "q", u)
                        act.wait_ge(s_tg, 2)
                        act.activation(qT[:, u % 2, :], X.tile[:, 0:P], Ident, bias=sq2[:, :], scale=float(DH) ** -0.5)\
                           .then_inc(X.drained, 1)
                    elif k == "A3":
                        full(X, "q", u)
                        act.activation(qT[:, u % 2, :], X.tile[:, 0:P], Copy, scale=float(DH) ** -0.5)\
                           .then_inc(X.drained, 1)
                    elif k == "F2":
                        full(X, "gate", u)
                        act.activation(sg[:, t, :], X.tile[:, 0:E2], Tanh, scale=0.5).then_inc(X.drained, 1)

                def phase1(k, u, t):
                    if k in ("A0", "A2", "A3"):
                        drained(S, "scores", u)
                        inc(act.activation(pr[:, u % U % 3, :], pr[:, u % U % 3, :], Exp), "probs_" + k)
                    elif k == "A1":
                        wait("nmax_A1", t, u)
                        act.activation(pr[:, u % U % 3, 0:CTX], S.tile[:, 0, 0:CTX], Exp, bias=sc[:, t, 0:1],
                                       accum_out=sc[:, t, 1:2]).then_inc(S.drained, 1)
                    elif k == "F0":
                        wait("centred_F0", t, u)
                        inc(act.activation(ex[:, t, :], lg[:, t, 0:E0], Exp, accum_out=sc[:, t, 1:2]), "expsum_F0")

                def phase1_first(k, u, t):
                    if k == "F1":
                        full(S, "gu", u)
                        inc(act.activation(th[:, u % 2, 0:FB], S.tile[:, 0, :], Tanh, scale=sc[:, t, 3:4]), "tanh_F1")
                    if k == "F2":
                        full(S, "gu", u)
                        inc(act.activation(th[:, u % 2, 0:2 * GW].rearrange("p (b n) -> p b n", b=2),
                                           S.tile[:, 0:2, 0:GW], Tanh, scale=0.5), "tanh_F2a")

                def phase2_end(k, u, t):
                    if k == "F3":
                        wait("centred_F3", t, u)
                        inc(act.activation(ex[:, t, 0:4], lg[:, t, 0:4], Exp, accum_out=sc[:, t, 1:2]), "expsum_F3")

                order = ((phase1_first, 1), (phase3, 3), (phase2_first, 2), (phase0_early, 0), (phase3_rest, 3), (phase1_extra, 1), (phase2, 2), (phase0_late, 0),
                         
                         (phase0_project, 0), (phase1, 1), (phase2_end, 2), ("prepare", 0))
                for work, v in steps(order, first, U + 3, next_only=first == U):
                    if work == "prepare":
                        for do in prepare[v]:
                            do()
                    else:
                        work(UNITS[v % U][0], v, UNITS[v % U][1])

            one_pass(-1, U)
            with act.Fori(0, B) as it:
                one_pass(it, 3)

        @block.gpsimd
        def _(pool):
            def carry():
                pool.sem_inc(s_carry, 1)

            pool.memset(half[:, :], -0.5).then_inc(s_const, 1)
            pool.wait_ge(loaded["base"], 16)
            for V in (V2, V3):
                pool.tensor_copy(V[:, :, :, DH:VW].rearrange("p n h o -> p n (h o)"),
                                 W["ones_col"].rearrange("p (n h) -> p n h", h=H)).then_inc(s_const, 1)
            pool.wait_ge(s_const, 12)

            def context(it):
                full, free, drained, wait = helpers(pool, it)
                def ctx_rstd():
                    wait("ctx_var", 0)
                    inc(pool.tensor_tensor(crs[:, :], cve[:, :], half[0:CTX, 0:1], ALU.pow), "ctx_rstd")

                def ctx_copy():
                    pool.wait_ge(s_c_loaded, it * 48 + 96)
                    carry()
                    pool.tensor_copy(ctx[:, :], ctx_st[:, :])
                    inc(pool.tensor_copy(ctxT[:, :], ctxT_st[:, :]), "ctx_copied")

                def expand(dst, src):
                    inc(pool.tensor_tensor(dst, src[:, :].unsqueeze(1).broadcast_to([P, H, CTX]),
                                           W["delta"].unsqueeze(2).broadcast_to([P, H, CTX]), ALU.mult), "expanded")

                def k2_():
                    drained(X, "kv")
                    expand(K2[:, :, :], k2)
                    ctx_copy()
                return {12: (ctx_rstd,), 13: (k2_,), 14: (lambda: expand(V2x, v2),),
                        15: (lambda: expand(K3[:, :, :], k3),)}, (ctx_rstd, ctx_copy)

            for part in context(-1)[1]:
                part()
            pool.wait_ge(X.drained, X.prelude.index("simnorm") + 2)
            pool.tensor_tensor(sim_sq[:, :], sim_sq[:, :], half[0:PROJ, 0:1].broadcast_to([PROJ, 4 + R]), ALU.pow)\
                .then_inc(s_simpow, 1)

            def one_pass(it, first):
                full, free, drained, wait = helpers(pool, it)
                prepare = context(it)[0]

                def phase0(k, u, t):
                    wait("var_ready", u)
                    inc(pool.tensor_tensor(rstd[:, t:t + 1], ve[:, t:t + 1], half[:, 0:1], ALU.pow), "rstd_ready")

                def weigh(u, t, e0, e1):
                    h = hh[:, u % U % 3, e0 * F2W:e1 * F2W].rearrange("p (e f) -> p e f", f=F2W)
                    return pool.tensor_tensor(h, h, comb[:, t, e0:e1].unsqueeze(2).broadcast_to([P, e1 - e0, F2W]),
                                              ALU.mult)

                def phase1(k, u, t):
                    if k == "F3":
                        wait("ss_ready", t, u)
                        inc(pool.tensor_tensor(sc[:, t, 5:6], sc[:, t, 4:5], half[:, 0:1], ALU.pow), "rn_ready")
                    elif k == "F2":
                        drained(S, "gu", u)
                        wait("comb_ready", t, u)
                        inc(weigh(u, t, 0, 12), "weighted_F2a")

                def phase2(k, u, t):
                    if k == "A0":
                        wait("inv0", t, u)
                        p = pr[:, u % U % 3, :].rearrange("p (h c) -> p h c", c=CTX)
                        inc(pool.tensor_tensor(p, p, ri[:, t, :].unsqueeze(2).broadcast_to([P, H, CTX]), ALU.mult),
                            "probs0")
                    elif k == "F2":
                        drained(T1, "up", u)
                        inc(weigh(u, t, 12, E2), "weighted_F2b")

                order = ((phase0, 0), (phase2, 2), (phase1, 1), ("prepare", 0))
                for work, v in steps(order, first, U + 3, next_only=first == U):
                    if work == "prepare":
                        for do in prepare.get(v, ()):
                            do()
                    else:
                        work(UNITS[v % U][0], v, UNITS[v % U][1])

            one_pass(-1, U)
            with pool.Fori(0, B) as it:
                one_pass(it, 3)

        @block.vector
        def _(dve):
            steps_done = [0]

            def link(ins):
                steps_done[0] += 1
                ins.then_inc(s_dve, 1)
                dve.wait_ge(s_dve, at[0] * DVE_STEPS + (BEFORE_LOOP[0] + steps_done[0]) if at else steps_done[0])

            def carry():
                dve.sem_inc(s_carry, 1)

            at, BEFORE_LOOP = [], [0]
            tanh_gate = {k: tg[:, GATE[k]:GATE[k] + 1] for k in BLOCKS}
            for bank in (S, O):
                dve.sem_inc(bank.drained, 1)
            dve.memset(ones[:, :], 1.0).then_inc(s_const, 1)
            dve.memset(ones_b[:, :], 1.0).then_inc(s_const, 1)
            dve.memset(k0[:, :, :], 0.0).then_inc(s_const, 1)
            dve.memset(v0[:, :, :], 0.0).then_inc(s_const, 1)
            dve.memset(gs[:, :], TAKEN / 4).then_inc(s_const, 1)
            for n in taken:
                dve.memset(taken[n][:, :], 2 * TAKEN).then_inc(s_const, 1)
            dve.wait_ge(loaded["base"], 16)
            dve.tensor_copy(ident_b[:, :], ident).then_inc(s_const, 1)
            dve.tensor_copy(pick_row[:, :, :], W["ident"][0:E0, 0:E0].unsqueeze(2).broadcast_to([E0, E0, P]))\
               .then_inc(s_const, 1)

            def context(it):
                full, free, drained, wait = helpers(dve, it)
                dve.wait_ge(s_c_loaded, it * 48 + 96)
                link(dve.bn_stats(cstat[:, :], ctx_st[:, :]))
                carry()
                link(dve.bn_aggr(cmv[:, :], cstat[:, :]))
                inc(dve.tensor_scalar(cve[:, :], cmv[:, 1:2], LN_EPS, None, ALU.add), "ctx_var")
                link(dve.tensor_scalar(seen[:, :], mask_st[:, :], 0.0, None, ALU.not_equal))
                link(dve.tensor_reduce(anyseen[:, 0:1], seen[:, :], AX.X, ALU.max))
                link(dve.reciprocal(anyseen[:, 1:2], anyseen[:, 0:1]))
                inc(dve.tensor_scalar(mask_row[:, :, :], mask_st[0:1, :].unsqueeze(1).broadcast_to([1, HB, CTX]),
                                      0.0, MASKED, ALU.is_equal, ALU.mult), "mask_ready")
                wait("ctx_rstd", 0)
                inc(dve.tensor_scalar(ctxn[:, :], ctx_st[:, :], cmv[:, 0:1], crs[:, 0:1], ALU.subtract, ALU.mult),
                    "ctx_norm")
                inc(dve.tensor_tensor(anyseen[:, 2:3], anyseen[:, 0:1], anyseen[:, 1:2], ALU.mult), "ctx_used")

            context(-1)
            dve.wait_ge(loaded["tern"], 16)
            dve.tensor_reduce(wt_sum[:, :], W["wt"].rearrange("p (w n) -> p w n", w=3), AX.X, ALU.add,
                              apply_absolute_value=True).then_inc(s_prel, 1)
            dve.wait_ge(loaded["low"], 16)
            dve.tensor_tensor(sim_sq[:, :], W["sim"], W["sim"], ALU.mult).then_inc(s_prel, 1)
            dve.tensor_scalar(sim_s[:, :], W["temp"], CLAMP, None, ALU.min).then_inc(s_prel, 1)
            full, free, drained, wait = helpers(dve, -1)
            full(X, "wmean")
            dve.tensor_scalar(wt_mean[:, :], X.tile[:, 0:3], 1.0 / (FB * D), 1e-5, ALU.mult, ALU.max)\
               .then_inc(X.drained, 1)
            drained(X, "wmean")
            link(dve.reciprocal(wt_inv[:, :], wt_mean[:, :]))
            for n in range(3):
                cols = slice(n * FB, (n + 1) * FB)
                last = dve.tensor_scalar(wt_r[:, cols], W["wt"][:, cols], wt_inv[:, n:n + 1], MAGIC, ALU.mult, ALU.add)
            link(last)
            link(dve.tensor_scalar(wt_r, wt_r, -MAGIC, 1.0, ALU.add, ALU.min))
            dve.tensor_scalar(wt_q[:, :], wt_r, -1.0, None, ALU.max).then_inc(s_quant, 1)
            dve.wait_ge(s_tg, 1)
            dve.tensor_scalar(tgh[:, :], tanh_gate.get("F2", tg[:, 6:7]), 0.5, None, ALU.mult)
            dve.tensor_scalar(wt_c[:, 0:1], wt_mean[:, 0:1], 0.5 / 127.0, None, ALU.mult)
            dve.tensor_scalar(wt_c[:, 1:2], wt_mean[:, 0:1], wt_mean[:, 1:2], 0.5 / 127.0 ** 2, ALU.mult, ALU.mult)
            dve.tensor_scalar(wt_c[:, 2:3], wt_mean[:, 2:3], tg[:, 5:6], 1.0 / 127.0, ALU.mult, ALU.mult)
            dve.wait_ge(loaded["att23"], 16)
            dve.tensor_scalar(sq2[:, :], W["b2qkv"][:, 0:1], float(DH) ** -0.5, None, ALU.mult).then_inc(s_tg, 1)
            full(X, "simnorm")
            dve.tensor_scalar(sim_sq[:, :], X.tile[0:PROJ, 0:4 + R], 1e-24, None, ALU.max).then_inc(X.drained, 1)
            dve.wait_ge(s_simpow, 1)
            link(dve.tensor_tensor(sim_n[:, :], W["sim"], sim_sq[:, :], ALU.mult))
            dve.wait_ge(s_temp, 1)
            dve.tensor_scalar(sim_n[:, :], sim_n[:, :], sim_s[:, 0:1], None, ALU.mult).then_inc(s_prel, 1)
            dve.wait_ge(s_prel, 4)
            dve.wait_ge(s_const, 12)
            dve.wait_ge(s_quant, 1)

            def one_pass(it, first):
                full, free, drained, wait = helpers(dve, it)

                def now(k, t):
                    return x_st[:, t, :] if k == "A0" else x[:, t, :]

                def phase0_stats(k, u, t):
                    if k == "A0" and t == 0:
                        dve.wait_ge(s_x_loaded, it * 16 + (u // U + 1) * 16)
                    link(dve.bn_stats(stat[:, :], now(k, t)))
                    carry()
                    link(dve.bn_aggr(mv[:, t, :], stat[:, :]))
                    a, b_ = (1.0 + LN_EPS, LN_EPS * LN_EPS) if k == "A0" else (1.0, LN_EPS)
                    inc(dve.tensor_scalar(ve[:, t:t + 1], mv[:, t, 1:2], a, b_, ALU.mult, ALU.add), "var_ready")

                def phase0_norm(k, u, t):
                    wait("rstd_ready", u)
                    norm = dve.tensor_scalar(xh[:, t, :], now(k, t), mv[:, t, 0:1], rstd[:, t:t + 1],
                                             ALU.subtract, ALU.mult)
                    if k != "F1":
                        inc(norm, "xh_ready")
                        return
                    link(norm)
                    link(dve.tensor_reduce(sc[:, t, 4:5], xh[:, t, :], AX.X, ALU.max, apply_absolute_value=True))
                    link(dve.tensor_scalar(sc[:, t, 4:5], sc[:, t, 4:5], 1e-5, None, ALU.max))
                    link(dve.reciprocal(sc[:, t, 5:6], sc[:, t, 4:5]))
                    link(dve.tensor_scalar(sc[:, t, 5:6], sc[:, t, 5:6], 127.0, None, ALU.mult))
                    dve.tensor_scalar(sc[:, t, 3:4], sc[:, t, 4:5], wt_c[:, 0:1], None, ALU.mult)
                    dve.tensor_scalar(sc[:, t, 6:7], sc[:, t, 4:5], sc[:, t, 4:5], wt_c[:, 1:2], ALU.mult, ALU.mult)
                    link(dve.tensor_scalar(xhq[:, u % 2, :], xh[:, t, :], sc[:, t, 5:6], MAGIC, ALU.mult, ALU.add))
                    inc(dve.tensor_scalar(xq[:, t, :], xhq[:, u % 2, :], -MAGIC, 127.0, ALU.add, ALU.min), "xh_ready")

                def residual(k, t, src, scale, out=None):
                    return dve.scalar_tensor_tensor(out=x[:, t, :] if out is None else out, in0=src, scalar=scale,
                                                    in1=now(k, t), op0=ALU.mult, op1=ALU.add)

                def inverse_sum(k, t):
                    link(dve.reciprocal(sc[:, t, 2:3], sc[:, t, 1:2]))
                    link(dve.tensor_scalar(sc[:, t, 3:4], sc[:, t, 2:3], tanh_gate[k], None, ALU.mult))

                def phase3_early(k, u, t):
                    if k == "F0":
                        wait("expsum_F0", t, u)
                        inverse_sum(k, t)
                        link(dve.tensor_scalar(ri[:, t, 0:E0], oh[:, t, 0:E0], sc[:, t, 3:4], None, ALU.mult))
                        full(O, "bias", u)
                        residual(k, t, O.tile[:, 0:D], sc[:, t, 3:4]).then_inc(O.drained, 1)
                    elif k == "A1":
                        drained(S, "scores", u)
                        inverse_sum(k, t)
                        full(O, "out", u)
                        residual(k, t, O.tile[:, 0:D], sc[:, t, 3:4]).then_inc(O.drained, 1)
                        drained(O, "out", u)
                    elif k == "F1":
                        full(O, "out", u)
                        residual(k, t, O.tile[:, 0:D], sc[:, t, 7:8]).then_inc(O.drained, 1)
                        drained(O, "out", u)
                    elif k in ("A2", "A3"):
                        full(O, "values", u)
                        o = O.tile[:, 0:H * VW].rearrange("p (h v) -> p h v", v=VW)
                        link(dve.reciprocal(ri[:, t, :], o[:, :, DH:VW].rearrange("p h o -> p (h o)")))
                        dve.tensor_tensor(cv[:, u % 2, :].rearrange("p (h v) -> p h v", v=DH), o[:, :, 0:DH],
                                          ri[:, t, :].unsqueeze(2).broadcast_to([P, H, DH]), ALU.mult)\
                           .then_inc(O.drained, 1)

                def phase1(k, u, t):
                    if k in ("A0", "A2", "A3"):
                        full(S, "scores", u)
                        s4 = S.tile[:, :, 0:SB].rearrange("p b (h c) -> p b h c", c=CTX)
                        link(dve.tensor_reduce(mx[:, t, :].rearrange("p (b h) -> p b h", b=4), s4, AX.X, ALU.max))
                        m4 = mx[:, t, :].rearrange("p (b h) -> p b h", b=4).unsqueeze(3)
                        dve.tensor_tensor(pr[:, u % U % 3, :].rearrange("p (b h c) -> p b h c", b=4, c=CTX), s4,
                                          m4.broadcast_to([P, 4, HB, CTX]), ALU.subtract).then_inc(S.drained, 1)
                    elif k == "A1":
                        full(S, "scores", u)
                        inc(dve.tensor_reduce(sc[:, t, 0:1], S.tile[:, 0, 0:CTX], AX.X, ALU.max, negate=True),
                            "nmax_A1")
                    elif k == "F0":
                        full(X, "logits", u)
                        dve.tensor_tensor(lg[:, t, 0:E0], X.tile[:, 0:E0], W["br"], ALU.add).then_inc(X.drained, 1)
                        drained(X, "logits", u)
                        link(dve.tensor_reduce(sc[:, t, 0:1], lg[:, t, 0:E0], AX.X, ALU.max, negate=True))
                        inc(dve.tensor_scalar(lg[:, t, 0:E0], lg[:, t, 0:E0], sc[:, t, 0:1], None, ALU.add),
                            "centred_F0")
                        wait("centred_F0", t, u)
                        link(dve.scalar_tensor_tensor(out=tt[:, t, 0:E0], in0=lg[:, t, 0:E0], scalar=0.0,
                                                      in1=W["desc0"], op0=ALU.is_ge, op1=ALU.mult))
                        link(dve.tensor_reduce(sc[:, t, 5:6], tt[:, t, 0:E0], AX.X, ALU.max))
                        inc(dve.tensor_scalar(oh[:, t, 0:E0], tt[:, t, 0:E0], sc[:, t, 5:6], None, ALU.is_equal),
                            "pick_ready")
                    elif k == "F2":
                        wait("tanh_F2a", t, u)
                        def two(a, n):
                            return a[:, u % n, 0:2 * GW].rearrange("p (b n) -> p b n", b=2)

                        link(dve.scalar_tensor_tensor(out=two(g1, 2), in0=two(th, 2), scalar=1.0, in1=S.tile[:, 0:2, 0:GW],
                                                      op0=ALU.add, op1=ALU.mult))
                        dve.tensor_tensor(two(hh, 3), two(g1, 2), S.tile[:, 2:4, 0:GW], ALU.mult).then_inc(S.drained, 1)
                    elif k == "F3":
                        full(S, "all", u)
                        inc(dve.tensor_tensor(pj[:, t, :], S.tile[:, 0, 0:PROJ], W["bp"], ALU.add), "pj_ready")
                        dve.tensor_copy(dn[:, t, :], S.tile[:, 0, PROJ:PROJ + R])
                        residual(k, t, S.tile[:, 0, PROJ + R:PROJ + R + D], tanh_gate[k]).then_inc(S.drained, 1)
                        wait("pj_ready", t, u)
                        link(dve.tensor_tensor(pj2[:, :], pj[:, t, :], pj[:, t, :], ALU.mult))
                        link(dve.tensor_reduce(sc[:, t, 4:5], pj2[:, :], AX.X, ALU.add))
                        inc(dve.tensor_scalar(sc[:, t, 4:5], sc[:, t, 4:5], 1e-24, None, ALU.max), "ss_ready")

                def take_best(values, n):
                    carry()
                    link(dve.max(out=best[:, :], in_=values))
                    link(dve.tensor_copy(taken[n][:, 0:n], best[:, 0:n]))
                    carry()
                    out = left[:, 0:values.free_size()]
                    link(dve.match_replace(out=out, in_to_replace=taken[n][:, :], in_values=values, imm_value=TAKEN))
                    return out

                def route_groups(k, u, t):
                    if k != "F2":
                        return
                    drained(X, "gate", u)
                    link(dve.tensor_scalar(sig[:, t, :], sg[:, t, :], 0.5, 0.5, ALU.mult, ALU.add))
                    s4 = sig[:, t, :].rearrange("p (g e) -> p g e", g=4)
                    dve.tensor_tensor(pairs[:, :, 0:3], s4[:, :, 0:3], s4[:, :, 1:4], ALU.add)
                    dve.tensor_tensor(pairs[:, :, 3:5], s4[:, :, 0:2], s4[:, :, 2:4], ALU.add)
                    link(dve.tensor_tensor(pairs[:, :, 5:6], s4[:, :, 0:1], s4[:, :, 3:4], ALU.add))
                    link(dve.tensor_reduce(gs[:, 0:4], pairs[:, :, :], AX.X, ALU.max))
                    left4 = take_best(gs[:, :], 2)
                    link(dve.tensor_scalar(cap[:, :], left4[:, 0:4], TAKEN / 2, 4.0, ALU.is_lt, ALU.mult))

                def route_experts(u, t):
                    s4 = sig[:, t, :].rearrange("p (g e) -> p g e", g=4)
                    m4 = msk[:, :].rearrange("p (g e) -> p g e", g=4)
                    link(dve.tensor_tensor(m4, s4, cap[:, :].unsqueeze(2).broadcast_to([P, 4, 4]), ALU.min))
                    left16 = take_best(msk[:, :], 4)
                    link(dve.scalar_tensor_tensor(out=picked[:, :], in0=left16, scalar=TAKEN / 2, in1=msk[:, :],
                                                  op0=ALU.is_lt, op1=ALU.mult))
                    link(dve.tensor_reduce(psc[:, 0:1], picked[:, :], AX.X, ALU.add))
                    link(dve.tensor_scalar(psc[:, 1:2], psc[:, 0:1], 1e-6, None, ALU.add))
                    link(dve.reciprocal(psc[:, 2:3], psc[:, 1:2]))
                    inc(dve.tensor_scalar(comb[:, t, :], picked[:, :], psc[:, 2:3], None, ALU.mult), "comb_ready")

                def silu_times_up(k, u, t, cols, gate, up, factor):
                    n = gate.free_size()
                    dve.scalar_tensor_tensor(out=g1[:, u % 2, cols], in0=th[:, u % 2, cols], scalar=1.0, in1=gate,
                                             op0=ALU.add, op1=ALU.mult).then_inc(T0.drained, 1)
                    drained(T0, "gate", u)
                    full(T1, "up", u)
                    dve.scalar_tensor_tensor(out=hh[:, u % U % 3, cols], in0=g1[:, u % 2, cols], scalar=factor, in1=up,
                                             op0=ALU.mult, op1=ALU.mult).then_inc(T1.drained, 1)

                def phase2(k, u, t):
                    if k == "A0":
                        wait("probs_A0", t, u)
                        link(dve.tensor_reduce(rs[:, t, :], pr[:, u % U % 3, :].rearrange("p (h c) -> p h c", c=CTX),
                                               AX.X, ALU.add))
                        inc(dve.reciprocal(ri[:, t, :], rs[:, t, :]), "inv0")
                        wait("tanh_A0", t, u)
                        silu_times_up(k, u, t, slice(0, FF0), T0.tile[:, :], T1.tile[:, :], 0.5)
                    elif k == "F2":
                        wait("tanh_F2b", t, u)
                        silu_times_up(k, u, t, slice(2 * GW, 3 * GW), T0.tile[:, 0:GW], T1.tile[:, 0:GW], 1.0)
                    elif k == "F3":
                        full(X, "logits", u)
                        wait("rn_ready", t, u)
                        dve.tensor_scalar(lg[:, t, :], X.tile[:, 0:4 + R], sc[:, t, 5:6], None, ALU.mult)\
                           .then_inc(X.drained, 1)
                        drained(X, "logits", u)
                        link(dve.tensor_reduce(sc[:, t, 0:1], lg[:, t, 0:4], AX.X, ALU.max, negate=True))
                        inc(dve.tensor_scalar(lg[:, t, :], lg[:, t, :], sc[:, t, 0:1], None, ALU.add), "centred_F3")
                        wait("centred_F3", t, u)
                        link(dve.scalar_tensor_tensor(out=tt[:, t, :], in0=lg[:, t, :], scalar=0.0, in1=W["desc3"],
                                                      op0=ALU.is_ge, op1=ALU.mult))
                        link(dve.tensor_reduce(sc[:, t, 6:7], tt[:, t, 0:4], AX.X, ALU.max))
                        inc(dve.scalar_tensor_tensor(out=dm[:, t, :], in0=tt[:, t, 4:4 + R], scalar=sc[:, t, 6:7],
                                                     in1=dn[:, t, :], op0=ALU.is_equal, op1=ALU.mult), "dm_ready")

                def phase3(k, u, t):
                    if k == "F0":
                        drained(O, "bias", u)
                        for e in range(E0):
                            bank, what = (T0, "ya") if e < 4 else (T1, "yb")
                            if e % 4 == 0:
                                full(bank, what, u)
                            r = residual(k, t, bank.tile[:, e % 4 * D:(e % 4 + 1) * D], ri[:, t, e:e + 1])
                            if e % 4 == 3:
                                r.then_inc(bank.drained, 1)
                                drained(bank, what, u)
                            else:
                                link(r)
                        return
                    if k in ("A1", "F1"):
                        return
                    scale = tgh[:, 0:1] if k == "F2" else tanh_gate[k]
                    if k == "F3":
                        wait("expsum_F3", t, u)
                        inverse_sum(k, t)
                        scale = sc[:, t, 3:4]
                    bank = T1 if k in ("A2", "A3") else O
                    if k == "F3" and t == 0:
                        dve.wait_ge(s_stored, (it + 1) * (16 * TILES))
                    full(bank, "out", u)
                    residual(k, t, bank.tile[:, 0:D], scale, y[:, t, :] if k == "F3" else None).then_inc(bank.drained, 1)
                    drained(bank, "out", u)

                def phase1_extra(k, u, t):
                    if k == "F2":
                        route_experts(u, t)
                    elif k == "F1":
                        wait("tanh_F1", t, u)
                        link(dve.scalar_tensor_tensor(out=g1[:, u % 2, 0:FB], in0=th[:, u % 2, 0:FB], scalar=1.0,
                                                      in1=S.tile[:, 0, :], op0=ALU.add, op1=ALU.mult))
                        dve.tensor_tensor(hh[:, u % U % 3, 0:FB], g1[:, u % 2, 0:FB], S.tile[:, 1, :], ALU.mult)\
                           .then_inc(S.drained, 1)
                        drained(S, "gu", u)
                        h = hh[:, u % U % 3, 0:FB]
                        link(dve.tensor_reduce(sc[:, t, 8:9], h, AX.X, ALU.max, apply_absolute_value=True))
                        link(dve.tensor_scalar(sc[:, t, 8:9], sc[:, t, 8:9], sc[:, t, 6:7], 1e-5, ALU.mult, ALU.max))
                        link(dve.reciprocal(sc[:, t, 9:10], sc[:, t, 8:9]))
                        link(dve.tensor_scalar(sc[:, t, 9:10], sc[:, t, 9:10], sc[:, t, 6:7], 127.0, ALU.mult, ALU.mult))
                        dve.tensor_scalar(sc[:, t, 7:8], sc[:, t, 8:9], wt_c[:, 2:3], None, ALU.mult)
                        link(dve.tensor_scalar(h, h, sc[:, t, 9:10], MAGIC, ALU.mult, ALU.add))
                        inc(dve.tensor_scalar(hq[:, u % 2, :], h, -MAGIC, 127.0, ALU.add, ALU.min), "hq_ready")

                def phase1_late(k, u, t):
                    if k == "F0":
                        full(S, "masks", u)
                        dve.tensor_tensor(xm[:, u % 2, :, :].rearrange("p (b e) n -> p b e n", b=2),
                                          S.tile[:, 0:2, :].rearrange("p b (e n) -> p b e n", n=P),
                                          xT[:, t, :].unsqueeze(1).unsqueeze(1).broadcast_to([P, 2, 4, P]), ALU.mult)\
                           .then_inc(S.drained, 1)

                order = ((phase0_stats, 0), (phase3_early, 3), (route_groups, 1), (phase0_norm, 0), (phase1, 1), (phase2, 2),
                         (phase1_extra, 1), (phase3, 3), (phase1_late, 1), ("prepare", 0))
                for work, v in steps(order, first, U + 3, next_only=first == U):
                    if work != "prepare":
                        work(UNITS[v % U][0], v, UNITS[v % U][1])
                    elif v == min(PREPARE):
                        context(it)

            one_pass(-1, U)
            BEFORE_LOOP[0], steps_done[0] = steps_done[0], 0
            with dve.Fori(0, B) as it:
                at.append(it)
                one_pass(it, 3)
            assert steps_done[0] == DVE_STEPS, steps_done[0]


def _columns(a, rows=P):
    return np.broadcast_to(np.asarray(a).reshape(1, -1), (rows, a.size))


def _pack(parts, given):
    out = np.zeros((P, sum(c for _, _, c in parts)), np.float32)
    at = 0
    for name, rows, cols in parts:
        out[0:rows, at:at + cols] = np.asarray(given[name]).reshape(rows, cols)
        at += cols
    return out


def kernel(**inputs):
    import concourse.bacc as _bacc
    from concourse.bass_utils import run_bass_kernel_spmd as _run

    a = {k: np.asarray(v) for k, v in inputs.items()}
    g = {}
    rows = np.arange(NCH * P)
    g["ident"] = np.eye(P)
    g["delta"] = np.arange(P)[:, None] // DH == np.arange(H)[None, :]
    g["ones_col"] = (rows.reshape(NCH, P, 1) // CTX == np.arange(H)).transpose(1, 0, 2)
    g["desc0"] = _columns(np.arange(E0, 0, -1))
    expert = [e for e, r in enumerate(RANKS) for _ in range(r)]
    cols3 = list(range(4)) + expert
    g["desc3"] = _columns(4 - np.array(cols3))
    g["gates"] = np.concatenate([_columns(a["g_xattn"]), _columns(a["g_ffn"])], axis=1)
    g["ln_gamma"] = np.stack([a["L0_xattn_gamma"], a["L0_xattn_ctx_gamma"]], axis=1)
    wkv = a["L0_xattn_Wkv"]
    g["wk0"] = np.concatenate([wkv[:, :DH0]] * 2, axis=1)
    g["wv0"] = np.concatenate([wkv[:, DH0:]] * 2, axis=1)
    g["wq0"] = a["L0_xattn_Wq"].T.reshape(8, P, D).transpose(1, 0, 2)
    g["wo0"] = a["L0_xattn_Wout"].reshape(8, P, D).transpose(1, 0, 2)
    g["wff1"] = a["L0_xattn_Wff1"]
    g["wff2"] = a["L0_xattn_Wff2"].reshape(4, P, D).transpose(1, 0, 2)
    g["wr"] = a["L0_ffn_Wr"]
    g["br"] = _columns(a["L0_ffn_br"])
    g["w1"] = a["L0_ffn_W1"].transpose(1, 0, 2)
    g["b1"] = a["L0_ffn_b1"]
    g["w2"] = a["L0_ffn_W2"].reshape(E0, 2, P, D).transpose(2, 1, 0, 3)
    g["b2"] = a["L0_ffn_b2"]
    g["wt"] = np.concatenate([a["L1_ffn_w_gate"].T, a["L1_ffn_w_up"].T,
                              a["L1_ffn_w_down"].T.reshape(4, P, D).transpose(1, 0, 2).reshape(P, FB)], axis=1)
    for n, name in (("wq2", "Wq"), ("wk2", "Wk"), ("wv2", "Wv")):
        g[n] = a["L2_xattn_" + name].transpose(1, 0, 2)
    g["b2qkv"] = np.stack([a["L2_xattn_b" + n].reshape(P) for n in "qkv"], axis=1)
    g["wo2"], g["bo2"] = a["L2_xattn_Wo"], a["L2_xattn_bo"]
    g["wg"] = a["L2_ffn_w_gate"].T
    g["w13"] = np.concatenate([m for e, s in (("w1_e", "w1_s"), ("w3_e", "w3_s"))
                               for m in (a["L2_ffn_" + e].reshape(E2 * F2W, D).T, a["L2_ffn_" + s].T)], axis=1)
    g["w2s"] = np.concatenate([a["L2_ffn_w2_e"].transpose(0, 2, 1).reshape(8, P, D),
                               a["L2_ffn_w2_s"].T[None]]).transpose(1, 0, 2)
    by_head = np.arange(D).reshape(DH, H).T.reshape(-1)
    g["wq3"], g["wk3"] = a["L3_xattn_Wq"][by_head].T, a["L3_xattn_Wk"][by_head].T
    g["wo3"] = a["L3_xattn_Wo"][:, by_head].T
    g["w3"] = np.concatenate([a["L3_ffn_Wp"].T] + [a[f"L3_ffn_Wd{i}"].T for i in range(4)] + [a["L3_ffn_W"].T], axis=1)
    g["bp"] = _columns(a["L3_ffn_bp"])
    g["sim"] = a["L3_ffn_sim"][:, cols3]
    g["temp"] = _columns(a["L3_ffn_temp"], PROJ)
    g["wu"] = np.concatenate([a[f"L3_ffn_Wu{i}"].T for i in range(4)], axis=0)

    nc = _bacc.Bacc("TRN2", target_bir_lowering=False, num_devices=1)
    arrays = {"x": a["x"], "ctx": a["ctx_1024"], "ctxT": np.ascontiguousarray(a["ctx_1024"].transpose(0, 2, 1)),
              "mask": np.ascontiguousarray(np.broadcast_to(a["mask_BxS2_ik0"][:, None, :], (B, P, CTX)))}
    for pack, parts in PACKS.items():
        arrays["w_" + pack] = _pack(parts, g)
    aps = {n: nc.dram_tensor("in_" + n, v.shape, mybir.dt.from_np(v.dtype), kind="ExternalInput").ap()
           for n, v in arrays.items()}
    out = nc.dram_tensor("out_0", (B, SEQ, D), F32, kind="ExternalOutput").ap()
    gated_flamingo(nc, aps["x"], aps["ctx"], aps["ctxT"], aps["mask"], {p: aps["w_" + p] for p in PACKS}, out)
    r = _run(nc, [{"in_" + n: v for n, v in arrays.items()}], core_ids=[0])
    return r.results[0]["out_0"]
```
